# Optimizing a Trainium2 kernel written in Bass

```python
import numpy as np
import jax
import jax.numpy as jnp

def _softmax(x, axis=-1):
    return jax.nn.softmax(x, axis=axis)

def _gelu(x):
    return jax.nn.gelu(x, approximate=True)

def _silu(x):
    return jax.nn.silu(x)

def _sigmoid(x):
    return jax.nn.sigmoid(x)

def _layernorm(x, axis=-1, eps=1e-05):
    m = jnp.mean(x, axis=axis, keepdims=True)
    v = jnp.var(x, axis=axis, keepdims=True)
    return (x - m) / jnp.sqrt(v + eps)

def _scatter_add(tgt, idx, src, axis=0):
    return tgt.at[idx].add(src)

def _segment_sum(src, seg, n):
    return jax.ops.segment_sum(src, seg, n)
kernel_name = 'mk_conv_attn_hybrid_d4_conv_nchw512_r4_17d616'

def setup_inputs(seed: int=0):
    np.random.seed(seed)
    _w = jnp.asarray

    def _rec_inputs():
        import jax
        import jax.numpy as jnp
        _gk = jax.random.key(seed)
        x = -0.0003929 + 0.9999 * jax.random.normal(jax.random.fold_in(_gk, 1), (8, 128, 16, 16), jnp.float32)
        return x
    x = _rec_inputs()

    def _L0_conv_setup():
        import jax, jax.numpy as jnp
        import numpy as np
        key = jax.random.key(seed)
        k1, k2, k3, k4, k5 = jax.random.split(key, 5)
        B, C, H, W = (8, 128, 16, 16)
        mid = C // 8
        x = jax.random.normal(k1, (B, C, H, W), dtype=jnp.float32)
        Wb = jax.random.normal(k2, (mid, C), dtype=jnp.float32) * (1.0 / np.sqrt(C))
        Wc = jax.random.normal(k3, (mid, C), dtype=jnp.float32) * (1.0 / np.sqrt(C))
        Wd = jax.random.normal(k4, (C, C), dtype=jnp.float32) * (1.0 / np.sqrt(C))
        gamma = jax.random.normal(k5, (1,), dtype=jnp.float32)
        return {'x': x, 'Wb': Wb, 'Wc': Wc, 'Wd': Wd, 'gamma': gamma}
    _L0_conv_all = _L0_conv_setup()
    _L0_conv_in = {k: v for k, v in _L0_conv_all.items() if k in ('Wb', 'Wc', 'Wd', 'gamma')}
    del _L0_conv_all

    def _L1_conv_setup():
        import jax, jax.numpy as jnp
        import numpy as np
        NUM_HEADS = 8
        key = jax.random.key(seed)
        k1, k2, k3 = jax.random.split(key, 3)
        B, C, H, W = (16, 128, 32, 32)
        x = jax.random.normal(k1, (B, C, H, W), dtype=jnp.float32)
        W_qkv = jax.random.normal(k2, (3 * C, C), dtype=jnp.float32) * (2.0 / (3 * C)) ** 0.5
        b_qkv = jnp.zeros((3 * C,), dtype=jnp.float32)
        W_proj = jax.random.normal(k3, (C, C), dtype=jnp.float32) * (2.0 / C) ** 0.5
        b_proj = jnp.zeros((C,), dtype=jnp.float32)
        return {'x': x, 'W_qkv': W_qkv, 'b_qkv': b_qkv, 'W_proj': W_proj, 'b_proj': b_proj}
    _L1_conv_all = _L1_conv_setup()
    _L1_conv_in = {k: v for k, v in _L1_conv_all.items() if k in ('W_qkv', 'b_qkv', 'W_proj', 'b_proj')}
    del _L1_conv_all

    def _L2_attn_setup():
        import jax, jax.numpy as jnp
        import numpy as np
        key = jax.random.key(seed)
        x = jax.random.normal(key, (4, 1024, 128), dtype=jnp.float32)
        return {'x': x}
    _L2_attn_all = _L2_attn_setup()
    _L2_attn_in = {k: v for k, v in _L2_attn_all.items() if k in ()}
    del _L2_attn_all

    def _L2_ffn_setup():
        import jax, jax.numpy as jnp
        import numpy as np
        K = 2
        key = jax.random.key(seed)
        ks = jax.random.split(key, 6)
        B, T, d, E, dff = (2, 512, 128, 8, 512)
        x = jax.random.normal(ks[0], (B, T, d), dtype=jnp.float32)
        Wg = jax.random.normal(ks[1], (d, E), dtype=jnp.float32) * 0.02
        W1 = jax.random.normal(ks[2], (E, d, dff), dtype=jnp.float32) * 0.02
        b1 = jnp.zeros((E, dff), dtype=jnp.float32)
        W2 = jax.random.normal(ks[3], (E, dff, d), dtype=jnp.float32) * 0.02
        b2 = jnp.zeros((E, d), dtype=jnp.float32)
        return {'x': x, 'Wg': Wg, 'W1': W1, 'b1': b1, 'W2': W2, 'b2': b2}
    _L2_ffn_all = _L2_ffn_setup()
    _L2_ffn_in = {k: v for k, v in _L2_ffn_all.items() if k in ('Wg', 'W1', 'b1', 'W2', 'b2')}
    del _L2_ffn_all

    def _L3_attn_setup():
        import jax, jax.numpy as jnp
        import numpy as np
        B, T, D, H, C, WIN = (2, 512, 128, 8, 16, 32)
        EPS = 1e-06

        def _rms_norm(x, w):
            norm = jax.lax.rsqrt(jnp.mean(x * x, axis=-1, keepdims=True) + EPS)
            return x * norm * w

        def _apply_rope(x, cos_p, sin_p):
            half = x.shape[-1] // 2
            x1, x2 = (x[..., :half], x[..., half:])
            rotated = jnp.concatenate([-x2, x1], axis=-1)
            return x * cos_p + rotated * sin_p
        key = jax.random.key(seed)
        ks = jax.random.split(key, 5)
        h = jax.random.normal(ks[0], (B, T, D), dtype=jnp.float32)
        inv_freq = 1.0 / 10000.0 ** (jnp.arange(0, C, 2, dtype=jnp.float32) / C)
        pos = jnp.arange(T, dtype=jnp.float32)
        freqs = pos[:, None] * inv_freq[None, :]
        emb = jnp.concatenate([freqs, freqs], axis=-1)
        rope_cos = jnp.cos(emb)
        rope_sin = jnp.sin(emb)
        scale = 0.02
        W_q = jax.random.normal(ks[1], (D, H * C), dtype=jnp.float32) * scale
        W_k = jax.random.normal(ks[2], (D, H * C), dtype=jnp.float32) * scale
        W_v = jax.random.normal(ks[3], (D, H * C), dtype=jnp.float32) * scale
        W_o = jax.random.normal(ks[4], (H * C, D), dtype=jnp.float32) * scale
        q_norm_w = jnp.ones((C,), dtype=jnp.float32)
        k_norm_w = jnp.ones((C,), dtype=jnp.float32)
        return {'h': h, 'rope_cos': rope_cos, 'rope_sin': rope_sin, 'W_q': W_q, 'W_k': W_k, 'W_v': W_v, 'W_o': W_o, 'q_norm_w': q_norm_w, 'k_norm_w': k_norm_w}
    _L3_attn_all = _L3_attn_setup()
    _L3_attn_in = {k: v for k, v in _L3_attn_all.items() if k in ('rope_cos', 'rope_sin', 'W_q', 'W_k', 'W_v', 'W_o', 'q_norm_w', 'k_norm_w')}
    del _L3_attn_all

    def _L3_ffn_setup():
        import jax, jax.numpy as jnp
        import numpy as np
        B, T, D = (4, 256, 128)
        E, TOP_K, H = (8, 2, 64)
        key = jax.random.key(seed)
        ks = jax.random.split(key, 8)
        s = 0.02
        return {'x': jax.random.normal(ks[0], (B, T, D), dtype=jnp.float32), 'router': jax.random.normal(ks[1], (D, E), dtype=jnp.float32) * s, 'shared_gate': jax.random.normal(ks[2], (D, H), dtype=jnp.float32) * s, 'shared_up': jax.random.normal(ks[3], (D, H), dtype=jnp.float32) * s, 'shared_down': jax.random.normal(ks[4], (H, D), dtype=jnp.float32) * s, 'W_gate': jax.random.normal(ks[5], (E, D, H), dtype=jnp.float32) * s, 'W_up': jax.random.normal(ks[6], (E, D, H), dtype=jnp.float32) * s, 'W_down': jax.random.normal(ks[7], (E, H, D), dtype=jnp.float32) * s}
    _L3_ffn_all = _L3_ffn_setup()
    _L3_ffn_in = {k: v for k, v in _L3_ffn_all.items() if k in ('router', 'shared_gate', 'shared_up', 'shared_down', 'W_gate', 'W_up', 'W_down')}
    del _L3_ffn_all
    return {'x': x, 'L0_conv_Wb': _L0_conv_in['Wb'], 'L0_conv_Wc': _L0_conv_in['Wc'], 'L0_conv_Wd': _L0_conv_in['Wd'], 'L0_conv_gamma': _L0_conv_in['gamma'], 'L1_conv_W_qkv': _L1_conv_in['W_qkv'], 'L1_conv_b_qkv': _L1_conv_in['b_qkv'], 'L1_conv_W_proj': _L1_conv_in['W_proj'], 'L1_conv_b_proj': _L1_conv_in['b_proj'], 'L2_ffn_Wg': _L2_ffn_in['Wg'], 'L2_ffn_W1': _L2_ffn_in['W1'], 'L2_ffn_b1': _L2_ffn_in['b1'], 'L2_ffn_W2': _L2_ffn_in['W2'], 'L2_ffn_b2': _L2_ffn_in['b2'], 'L3_attn_rope_cos': _L3_attn_in['rope_cos'], 'L3_attn_rope_sin': _L3_attn_in['rope_sin'], 'L3_attn_W_q': _L3_attn_in['W_q'], 'L3_attn_W_k': _L3_attn_in['W_k'], 'L3_attn_W_v': _L3_attn_in['W_v'], 'L3_attn_W_o': _L3_attn_in['W_o'], 'L3_attn_q_norm_w': _L3_attn_in['q_norm_w'], 'L3_attn_k_norm_w': _L3_attn_in['k_norm_w'], 'L3_ffn_router': _L3_ffn_in['router'], 'L3_ffn_shared_gate': _L3_ffn_in['shared_gate'], 'L3_ffn_shared_up': _L3_ffn_in['shared_up'], 'L3_ffn_shared_down': _L3_ffn_in['shared_down'], 'L3_ffn_W_gate': _L3_ffn_in['W_gate'], 'L3_ffn_W_up': _L3_ffn_in['W_up'], 'L3_ffn_W_down': _L3_ffn_in['W_down']}

def reference(x, L0_conv_Wb, L0_conv_Wc, L0_conv_Wd, L0_conv_gamma, L1_conv_W_qkv, L1_conv_b_qkv, L1_conv_W_proj, L1_conv_b_proj, L2_ffn_Wg, L2_ffn_W1, L2_ffn_b1, L2_ffn_W2, L2_ffn_b2, L3_attn_rope_cos, L3_attn_rope_sin, L3_attn_W_q, L3_attn_W_k, L3_attn_W_v, L3_attn_W_o, L3_attn_q_norm_w, L3_attn_k_norm_w, L3_ffn_router, L3_ffn_shared_gate, L3_ffn_shared_up, L3_ffn_shared_down, L3_ffn_W_gate, L3_ffn_W_up, L3_ffn_W_down):
    import jax
    import jax.numpy as jnp

    def _L0_conv_ref(x, Wb, Wc, Wd, gamma):
        import jax, jax.numpy as jnp
        import numpy as np
        B, C, H, W = x.shape
        N = H * W
        xf = x.reshape(B, C, N)
        b = jnp.einsum('mc,bcn->bnm', Wb, xf)
        c = jnp.einsum('mc,bcn->bmn', Wc, xf)
        d = jnp.einsum('oc,bcn->bno', Wd, xf)
        attn = jax.nn.softmax(jnp.einsum('bnm,bmk->bnk', b, c), axis=-1)
        out = jnp.einsum('bnk,bko->bno', attn, d)
        out = out.transpose(0, 2, 1).reshape(B, C, H, W)
        return gamma * out + x

    def _L1_conv_ref(x, W_qkv, b_qkv, W_proj, b_proj):
        import jax, jax.numpy as jnp
        import numpy as np
        NUM_HEADS = 8
        B, C, H, W = x.shape
        N = H * W
        heads = NUM_HEADS
        head_dim = C // heads
        scale = head_dim ** (-0.5)
        qkv = jnp.einsum('bchw,oc->bohw', x, W_qkv) + b_qkv[None, :, None, None]
        qkv = qkv.reshape(B, 3, heads, head_dim, N)
        q, k, v = (qkv[:, 0], qkv[:, 1], qkv[:, 2])
        q = jnp.swapaxes(q, -1, -2)
        v = jnp.swapaxes(v, -1, -2)
        attn = jnp.einsum('bhnd,bhdm->bhnm', q, k) * scale
        attn = jax.nn.softmax(attn, axis=-1)
        out = jnp.einsum('bhnm,bhmd->bhnd', attn, v)
        out = jnp.swapaxes(out, -1, -2)
        out = out.reshape(B, C, H, W)
        out = jnp.einsum('bchw,oc->bohw', out, W_proj) + b_proj[None, :, None, None]
        return out

    def _L2_attn_ref(x):
        import jax, jax.numpy as jnp
        import numpy as np
        raw_weights = jnp.einsum('btk,bsk->bts', x, x)
        weights = jax.nn.softmax(raw_weights, axis=2)
        y = jnp.einsum('bts,bsk->btk', weights, x)
        return y

    def _L2_ffn_ref(x, Wg, W1, b1, W2, b2):
        import jax, jax.numpy as jnp
        import numpy as np
        K = 2
        logits = jnp.einsum('btd,de->bte', x, Wg)
        probs = jax.nn.softmax(logits, axis=-1)
        top_p, _top_i = jax.lax.top_k(probs, K)
        top_p = top_p / jnp.sum(top_p, axis=-1, keepdims=True)
        b2_sum = jnp.sum(b2, axis=0)
        out = jnp.zeros_like(x)
        for i in range(K):
            w_in = x * top_p[..., i:i + 1]
            h = jax.nn.gelu(jnp.einsum('btd,edf->ebtf', w_in, W1) + b1[:, None, None, :], approximate=False)
            out = out + jnp.einsum('ebtf,efd->btd', h, W2) + b2_sum
        return out

    def _L3_attn_ref(h, rope_cos, rope_sin, W_q, W_k, W_v, W_o, q_norm_w, k_norm_w):
        import jax, jax.numpy as jnp
        import numpy as np
        B, T, D, H, C, WIN = (2, 512, 128, 8, 16, 32)
        EPS = 1e-06

        def _rms_norm(x, w):
            norm = jax.lax.rsqrt(jnp.mean(x * x, axis=-1, keepdims=True) + EPS)
            return x * norm * w

        def _apply_rope(x, cos_p, sin_p):
            half = x.shape[-1] // 2
            x1, x2 = (x[..., :half], x[..., half:])
            rotated = jnp.concatenate([-x2, x1], axis=-1)
            return x * cos_p + rotated * sin_p
        Bx, Tx, _ = h.shape
        q = (h @ W_q).reshape(Bx, Tx, H, C)
        k = (h @ W_k).reshape(Bx, Tx, H, C)
        v = (h @ W_v).reshape(Bx, Tx, H, C)
        q = _rms_norm(q, q_norm_w)
        k = _rms_norm(k, k_norm_w)
        positions = jnp.arange(Tx)
        cos_p = rope_cos[positions]
        sin_p = rope_sin[positions]
        q = _apply_rope(q.transpose(0, 2, 1, 3), cos_p, sin_p).transpose(0, 2, 1, 3)
        k = _apply_rope(k.transpose(0, 2, 1, 3), cos_p, sin_p).transpose(0, 2, 1, 3)
        i = positions[:, None]
        j = positions[None, :]
        sw_mask = (j <= i) & (j > i - WIN)
        logits = jnp.einsum('bthc,bshc->bhts', q, k) / np.sqrt(C).astype(np.float32)
        logits = jnp.where(sw_mask[None, None], logits, jnp.float32(-jnp.inf))
        attn = jax.nn.softmax(logits, axis=-1)
        out = jnp.einsum('bhts,bshc->bthc', attn, v).reshape(Bx, Tx, H * C)
        return out @ W_o

    def _L3_ffn_ref(x, router, shared_gate, shared_up, shared_down, W_gate, W_up, W_down):
        import jax, jax.numpy as jnp
        import numpy as np
        B, T, D = (4, 256, 128)
        E, TOP_K, H = (8, 2, 64)
        b, t, d = x.shape
        n = b * t
        x_flat = x.reshape(n, d)
        shared_out = jax.nn.silu(x_flat @ shared_gate) * (x_flat @ shared_up) @ shared_down
        probs = jax.nn.softmax(x_flat @ router, axis=-1)
        topk_scores, topk_idx = jax.lax.top_k(probs, TOP_K)
        combine = jnp.zeros((n, E), dtype=x.dtype)
        combine = combine.at[jnp.arange(n)[:, None], topk_idx].set(topk_scores)
        gate = jax.nn.silu(jnp.einsum('nd,edh->enh', x_flat, W_gate))
        up = jnp.einsum('nd,edh->enh', x_flat, W_up)
        y = jnp.einsum('enh,ehd->end', gate * up, W_down)
        routed_out = jnp.einsum('ne,end->nd', combine, y)
        return (shared_out + routed_out).reshape(b, t, d)

    def _gn(v, G=32, eps=1e-05):
        B_, C_, H_, W_ = v.shape
        g = v.reshape(B_, G, C_ // G, H_, W_)
        m = jnp.mean(g, axis=(2, 3, 4), keepdims=True)
        s = jnp.var(g, axis=(2, 3, 4), keepdims=True)
        return ((g - m) / jnp.sqrt(s + eps)).reshape(v.shape)

    def _ln_c(v, eps=1e-06):
        m = jnp.mean(v, axis=1, keepdims=True)
        s = jnp.var(v, axis=1, keepdims=True)
        return (v - m) / jnp.sqrt(s + eps)

    def _ln_t(v, eps=1e-05):
        m = jnp.mean(v, axis=-1, keepdims=True)
        s = jnp.var(v, axis=-1, keepdims=True)
        return (v - m) / jnp.sqrt(s + eps)

    def _to_tokens(v):
        B_, C_, H_, W_ = v.shape
        return v.reshape(B_, C_, H_ * W_).transpose(0, 2, 1)

    def _from_tokens(t, like):
        B_, C_, H_, W_ = like.shape
        return t.transpose(0, 2, 1).reshape(B_, C_, H_, W_)
    x = _L0_conv_ref(x, L0_conv_Wb, L0_conv_Wc, L0_conv_Wd, L0_conv_gamma)
    x = x + _L1_conv_ref(_gn(x), L1_conv_W_qkv, L1_conv_b_qkv, L1_conv_W_proj, L1_conv_b_proj)
    t = _to_tokens(x)
    t = t + _L2_attn_ref(_ln_t(t))
    t = t + _L2_ffn_ref(_ln_t(t), L2_ffn_Wg, L2_ffn_W1, L2_ffn_b1, L2_ffn_W2, L2_ffn_b2)
    t = t + _L3_attn_ref(_ln_t(t), L3_attn_rope_cos, L3_attn_rope_sin, L3_attn_W_q, L3_attn_W_k, L3_attn_W_v, L3_attn_W_o, L3_attn_q_norm_w, L3_attn_k_norm_w)
    t = t + _L3_ffn_ref(_ln_t(t), L3_ffn_router, L3_ffn_shared_gate, L3_ffn_shared_up, L3_ffn_shared_down, L3_ffn_W_gate, L3_ffn_W_up, L3_ffn_W_down)
    x = _from_tokens(t, x)
    return x

_drawn_inputs = setup_inputs


def setup_inputs(seed=0):
    import zlib

    import numpy as np

    out = dict(_drawn_inputs(seed))
    spreads = {'L1_conv_b_qkv': (0.0, 0.1),
     'L1_conv_b_proj': (0.0, 0.1),
     'L2_ffn_b1': (0.0, 0.1),
     'L2_ffn_b2': (0.0, 0.1),
     'L3_attn_q_norm_w': (1.0, 0.6),
     'L3_attn_k_norm_w': (1.0, 0.6)}
    factors = {'L2_ffn_Wg': 8.0,
     'L3_attn_rope_cos': 8.0,
     'L3_attn_rope_sin': 8.0,
     'L3_attn_W_q': 8.0,
     'L3_attn_W_k': 8.0,
     'L3_attn_W_v': 5.496,
     'L3_attn_W_o': 5.565,
     'L3_ffn_router': 8.0,
     'L3_ffn_shared_gate': 8.0,
     'L3_ffn_shared_up': 8.0,
     'L3_ffn_shared_down': 8.0,
     'L3_ffn_W_gate': 8.0,
     'L3_ffn_W_up': 8.0,
     'L3_ffn_W_down': 8.0}
    for name, (base, spread) in spreads.items():
        noise = np.random.default_rng([zlib.crc32(name.encode()), seed]).standard_normal(out[name].shape)
        drawn = base * np.exp(spread * noise) if base else spread * noise
        out[name] = jnp.asarray(drawn.astype(out[name].dtype))
    for name, factor in factors.items():
        out[name] = (out[name] * factor).astype(out[name].dtype)
    return out
```

```python
from contextlib import ExitStack

import concourse.bass as bass
from concourse import mybir
from concourse.alu_op_type import AluOpType as ALU

F32 = mybir.dt.float32
BF16 = mybir.dt.bfloat16
I32 = mybir.dt.int32
U32 = mybir.dt.uint32
ACT = mybir.ActivationFunctionType
AX = mybir.AxisListType

P = 128
IMAGES = 8
N = 256
TOKENS = IMAGES * N
GROUPS = 4
W = TOKENS // GROUPS
TILES = W // P
PAIR = W // N
NT = N // P
HEADS, HD = 8, 16
SLOTS = 4
EXPERTS = 8
FF = 512
FT = EXPERTS * FF // P
EH = 64
WIN = 32
KEYS = WIN + P
NO_KEY = -1.0e30


class Signal:

    def __init__(self, sem, per, ahead):
        self.sem, self.per, self.ahead = sem, per, per if ahead else 0

    def after(self, turn, count=None):
        return turn * self.per + self.ahead + (self.per if count is None else count)

    def before(self, turn):
        assert self.ahead
        return turn * self.per + self.ahead


class Chain:

    def __init__(self, eng, sem):
        self.eng, self.sem, self.count, self.base = eng, sem, 0, 0

    def turn(self, i, steps):
        self.base, self.count = i * steps, 0

    def __call__(self, ins):
        ins.then_inc(self.sem, 1)
        self.count += 1
        self.eng.wait_ge(self.sem, self.base + self.count)

    def ended(self, steps):
        assert self.count == steps, f"a turn has {self.count} linked steps, not {steps}"


def bass_conv_attn_hybrid_kernel(nc, A, out):
    with ExitStack() as ctx:
        def sb(name, shape, dt=F32):
            return ctx.enter_context(nc.sbuf_tensor(name, shape, dt))

        def sem(name):
            return ctx.enter_context(nc.semaphore(name))

        def signal(name, per, ahead=False):
            return Signal(sem(name), per, ahead)

        bank = [ctx.enter_context(nc.psum_tensor(f"bank{k}", [P, 512], F32)) for k in range(8)]

        R = sb("R", [P, TOKENS])
        XN_C = sb("XN_C", [P, TOKENS])
        XN_T = sb("XN_T", [P, TOKENS])
        R_C = sb("R_C", [P, TOKENS])

        ident = sb("ident", [P, P])
        ones = sb("ones", [P, P])
        identb = sb("identb", [P, P], BF16)
        bandb = sb("bandb", [P, 2, KEYS], BF16)
        band = sb("band", [P, 2, KEYS])
        groups4 = sb("groups4", [P, P])
        wraw = sb("wraw", [P, 7, P])
        WbT = sb("WbT", [P, 16])
        WcT = sb("WcT", [P, 16])
        WdT = sb("WdT", [P, P])
        Wqk1 = sb("Wqk1", [P, 4, P])
        WvT = sb("WvT", [P, P])
        WpT = sb("WpT", [P, P])
        bqk_raw = sb("bqk_raw", [P, 4])
        bqk = sb("bqk", [P, 4])
        bv_all = sb("bv_all", [P, P])
        bp_all = sb("bp_all", [P, P])
        gamma_all = sb("gamma_all", [P, 1])
        Wg = sb("Wg", [P, EXPERTS])
        W1 = sb("W1", [P, EXPERTS, FF])
        W2 = sb("W2", [P, FT, P])
        b1 = sb("b1", [P, FT])
        b2two = sb("b2two", [P, 1])
        Wqkv3 = sb("Wqkv3", [P, 3 * P])
        Wo3 = sb("Wo3", [P, P])
        norm_w = sb("norm_w", [P, 2, HD])
        rope = sb("rope", [P, 2, NT, HD])
        cosw = sb("cosw", [P, NT, 2, HD])
        sinw = sb("sinw", [P, NT, 2, HD])
        tail_mask = sb("tail_mask", [P, HEADS])
        router = sb("router", [P, EXPERTS])
        Wgate = sb("Wgate", [P, EXPERTS, EH])
        Wup = sb("Wup", [P, EXPERTS, EH])
        Wdown = sb("Wdown", [P, 4, P])
        Sgate = sb("Sgate", [P, EH])
        Sup = sb("Sup", [P, EH])
        Sdown = sb("Sdown", [EH, P])
        iota_i = sb("iota_i", [P, EXPERTS], I32)
        iota8 = sb("iota8", [P, EXPERTS])
        expert_rows = sb("expert_rows", [EXPERTS, EXPERTS * EH])

        xs = sb("xs", [P, W])
        q_s = sb("q_s", [P, 2, W])
        k_s = sb("k_s", [P, 2, W])
        v_s = sb("v_s", [P, TILES, P])
        xT_s = sb("xT_s", [P, W])
        E_s = sb("E_s", [P, 2, SLOTS, 2, N])
        ET_s = sb("ET_s", [P, SLOTS, 2, N])
        tail_s = sb("tail_s", [P, 2, P])
        vt_s = sb("vt_s", [P, PAIR, P])
        negmax = sb("negmax", [P, PAIR, HEADS, NT])
        rowsum = sb("rowsum", [P, PAIR, HEADS, NT])
        rinv = sb("rinv", [P, PAIR, HEADS, NT])
        o_s = sb("o_s", [P, TILES, P])
        oT_s = sb("oT_s", [P, W])
        r_s = sb("r_s", [P, W])
        xn_s = sb("xn_s", [P, W])
        xc_s = sb("xc_s", [P, W])
        stats = sb("stats", [P, TILES, 6])
        mv = sb("mv", [P, TILES, 2])
        mm_s = sb("mm_s", [P, PAIR, 2])
        gm = sb("gm", [P, PAIR, 2])
        var = sb("var", [P, 64])
        rstd = sb("rstd", [P, 64])
        ntmp = sb("ntmp", [P, 64])
        ntmp_i = sb("ntmp_i", [P, 64], I32)
        top = sb("top", [P, TILES, 8])
        topi = sb("topi", [P, TILES, 8], U32)
        topf = sb("topf", [P, TILES, 8])
        gate = sb("gate", [P, 6, TILES])
        pr = sb("pr", [P, 4, TILES, EXPERTS])
        y_s = sb("y_s", [P, W])
        idle = sem("idle")

        X = A["x"].rearrange("b c h w -> c b (h w)")
        OUT = out.rearrange("b c h w -> c b (h w)")

        def hold(eng):
            eng.sem_inc(idle, 1)

        def rsqrt(link, n):
            y, v, t, ti = rstd[:, 0:n], var[:, 0:n], ntmp[:, 0:n], ntmp_i[:, 0:n]
            link(nc.vector.tensor_single_scalar(ti, v.bitcast(I32), 1, ALU.logical_shift_right))
            link(nc.vector.tensor_scalar(y.bitcast(I32), ti, -1.0, float(0x5F3759DF), ALU.mult, ALU.add))
            for _ in range(3):
                link(nc.vector.tensor_tensor(t, y, y, ALU.mult))
                link(nc.vector.scalar_tensor_tensor(t, t, -0.5, v, ALU.mult, ALU.mult))
                link(nc.vector.scalar_tensor_tensor(y, t, 1.5, y, ALU.add, ALU.mult))

        RSQRT = 11

        def token_norm(dve, link, eps, tiles, done):
            a, n = tiles[0], len(tiles)
            for t in tiles:
                ins = nc.vector.bn_stats(stats[:, t, :], r_s[:, t * P:(t + 1) * P])
            link(ins)
            hold(dve)
            for t in tiles:
                ins = nc.vector.bn_aggr(mv[:, t, :], stats[:, t, :])
            link(ins)
            link(nc.vector.tensor_scalar(var[:, 0:n], mv[:, a:a + n, 1], eps, None, ALU.add))
            rsqrt(link, n)
            for t in tiles:
                ins = nc.vector.tensor_scalar(xn_s[:, t * P:(t + 1) * P], r_s[:, t * P:(t + 1) * P],
                                              mv[:, t, 0:1], rstd[:, t - a:t - a + 1], ALU.subtract, ALU.mult)
            ins.then_inc(done.sem, 1)

        NORM = 3 + RSQRT

        w_raw, w_c, w_l1, w_l2, w_l3, w_pads = (sem(n) for n in (
            "w_raw_loaded", "w_conv_loaded", "w_layer1_loaded", "w_layer2_loaded", "w_layer3_loaded", "pads_zero"))
        s_ident, s_wT, s_wE, s_prep = sem("ident_ready"), sem("weights_turned"), sem("weights_stored"), sem("prep_steps")
        s_prep_p, s_zero = sem("pool_prep_steps"), sem("raw_rows_zero")
        RAW = 7
        with nc.Block() as block:
            @block.sync
            def _(sp):
                sp.wait_ge(s_zero, 2)
                sp.dma_start(wraw[0:16, 0, :], A["L0_conv_Wb"]).then_inc(w_raw, 16)
                sp.dma_start(wraw[32:48, 0, :], A["L0_conv_Wc"]).then_inc(w_raw, 16)
                sp.dma_start(wraw[:, 1, :], A["L0_conv_Wd"]).then_inc(w_raw, 16)
                sp.dma_start(wraw[:, 2:5, :], A["L1_conv_W_qkv"].rearrange("(k o) c -> o k c", k=3)).then_inc(w_raw, 16)
                sp.dma_start(wraw[:, 5, :], A["L1_conv_W_proj"]).then_inc(w_raw, 16)
                sp.dma_start(wraw[0:FT, 6, :], A["L2_ffn_b1"].rearrange("e (q f) -> (e q) f", f=P)).then_inc(w_raw, 16)
                sp.dma_start(wraw[32:32 + EXPERTS, 6, :], A["L2_ffn_b2"]).then_inc(w_raw, 16)
                sp.dma_start(gamma_all[:, :], A["L0_conv_gamma"][None, :].broadcast_to([P, 1])).then_inc(w_c, 16)
                sp.dma_start(bv_all[:, :], A["L1_conv_b_qkv"][None, 2 * P:3 * P].broadcast_to([P, P])).then_inc(w_c, 16)
                sp.dma_start(bp_all[:, :], A["L1_conv_b_proj"][None, :].broadcast_to([P, P])).then_inc(w_c, 16)
                sp.wait_ge(w_pads, 3)
                for half in range(2):
                    for kind in range(2):
                        for j in range(SLOTS):
                            a = kind * P + (half * SLOTS + j) * HD
                            sp.dma_start(bqk_raw[32 * j:32 * j + HD, 2 * kind + half:2 * kind + half + 1],
                                         A["L1_conv_b_qkv"][a:a + HD].rearrange("(c o) -> c o", o=1)).then_inc(w_l1, 16)
                sp.dma_start(rope[:, 0, :, :], A["L3_attn_rope_cos"][0:N, :].rearrange("(t p) d -> p t d", p=P)).then_inc(w_l3, 16)
                sp.dma_start(rope[:, 1, :, :], A["L3_attn_rope_sin"][0:N, :].rearrange("(t p) d -> p t d", p=P)).then_inc(w_l3, 16)
                sp.dma_start(norm_w[:, 0, :], A["L3_attn_q_norm_w"][None, :].broadcast_to([P, HD])).then_inc(w_l3, 16)
                sp.dma_start(norm_w[:, 1, :], A["L3_attn_k_norm_w"][None, :].broadcast_to([P, HD])).then_inc(w_l3, 16)
                sp.dma_start(Wg[:, :], A["L2_ffn_Wg"]).then_inc(w_l2, 16)
                sp.dma_start(W1[:, :, :], A["L2_ffn_W1"].rearrange("e d f -> d e f")).then_inc(w_l2, 16)
                sp.dma_start(W2[:, :, :], A["L2_ffn_W2"].rearrange("e (q f) c -> f (e q) c", f=P)).then_inc(w_l2, 16)
                for n, name in enumerate(("L3_attn_W_q", "L3_attn_W_k", "L3_attn_W_v")):
                    sp.dma_start(Wqkv3[:, n * P:(n + 1) * P], A[name]).then_inc(w_l2, 16)
                sp.dma_start(Wo3[:, :], A["L3_attn_W_o"]).then_inc(w_l2, 16)
                sp.dma_start(router[:, :], A["L3_ffn_router"]).then_inc(w_l2, 16)
                sp.dma_start(Wgate[:, :, :], A["L3_ffn_W_gate"].rearrange("e d f -> d e f")).then_inc(w_l2, 16)
                sp.dma_start(Wup[:, :, :], A["L3_ffn_W_up"].rearrange("e d f -> d e f")).then_inc(w_l2, 16)
                sp.dma_start(Wdown[:, :, :], A["L3_ffn_W_down"].rearrange("(q e) f c -> (e f) q c", e=2)).then_inc(w_l2, 16)
                sp.dma_start(Sgate[:, :], A["L3_ffn_shared_gate"]).then_inc(w_l2, 16)
                sp.dma_start(Sup[:, :], A["L3_ffn_shared_up"]).then_inc(w_l2, 16)
                sp.dma_start(Sdown[:, :], A["L3_ffn_shared_down"]).then_inc(w_l2, 16)

            @block.gpsimd
            def _(pool):
                link = Chain(pool, s_prep_p)
                nc.gpsimd.memset(wraw[:, 0, :], 0.0).then_inc(s_zero, 1)
                nc.gpsimd.memset(wraw[:, 6, :], 0.0).then_inc(s_zero, 1)
                link(nc.gpsimd.memset(ones[:, :], 1.0))
                nc.gpsimd.affine_select(out=ident[:, :], in_=ones[:, :], compare_op=ALU.is_equal, fill=0.0,
                                        base=0, pattern=[[-1, P]], channel_multiplier=1).then_inc(s_ident, 1)
                link(nc.gpsimd.memset(groups4[:, :], 0.25))
                v = groups4[:, :].rearrange("p (g d) -> p g d", d=4)
                link(nc.gpsimd.affine_select(out=v, in_=v, compare_op=ALU.is_ge, fill=0.0, base=0,
                                             pattern=[[-4, P // 4], [0, 4]], channel_multiplier=1))
                link(nc.gpsimd.affine_select(out=v, in_=v, compare_op=ALU.is_ge, fill=0.0, base=3,
                                             pattern=[[4, P // 4], [0, 4]], channel_multiplier=-1))
                link(nc.gpsimd.memset(band[:, :, :], 0.0))
                link(nc.gpsimd.affine_select(out=band[:, :, :], in_=band[:, :, :], compare_op=ALU.is_ge, fill=NO_KEY,
                                             base=WIN, pattern=[[0, 2], [-1, KEYS]], channel_multiplier=1))
                link(nc.gpsimd.affine_select(out=band[:, :, :], in_=band[:, :, :], compare_op=ALU.is_gt, fill=NO_KEY,
                                             base=0, pattern=[[0, 2], [1, KEYS]], channel_multiplier=-1))
                link(nc.gpsimd.memset(band[:, 0, 0:WIN], NO_KEY))
                link(nc.gpsimd.tensor_copy(bandb[:, :, :], band[:, :, :]))
                link(nc.gpsimd.tensor_copy(identb[:, :], ident[:, :]))
                link(nc.gpsimd.memset(tail_mask[:, :], 1.0))
                m = tail_mask[:, :].rearrange("p (a j) -> p a j", j=SLOTS)
                link(nc.gpsimd.affine_select(out=m, in_=m, compare_op=ALU.is_ge, fill=0.0, base=0,
                                             pattern=[[0, 2], [-WIN, SLOTS]], channel_multiplier=1))
                link(nc.gpsimd.affine_select(out=m, in_=m, compare_op=ALU.is_ge, fill=0.0, base=WIN - 1,
                                             pattern=[[0, 2], [WIN, SLOTS]], channel_multiplier=-1))
                link(nc.gpsimd.memset(expert_rows[:, :], 1.0))
                r = expert_rows[:, :].rearrange("p (e f) -> p e f", f=EH)
                link(nc.gpsimd.affine_select(out=r, in_=r, compare_op=ALU.is_equal, fill=0.0, base=0,
                                             pattern=[[-1, EXPERTS], [0, EH]], channel_multiplier=1))
                link(nc.gpsimd.iota(iota_i[:, :], pattern=[[1, EXPERTS]], base=0, channel_multiplier=0))
                link(nc.gpsimd.tensor_copy(iota8[:, :], iota_i[:, :]))

            @block.tensor
            def _(pe):
                pe.wait_ge(s_ident, 1)
                pe.wait_ge(w_raw, 7 * 16)
                pe.wait_ge(w_pads, 3)
                for n in range(RAW):
                    nc.tensor.transpose(bank[n][:, 0:P], wraw[:, n, :], ident[:, :]).then_inc(s_wT, 1)

            @block.vector
            def _(dve):
                link = Chain(dve, s_prep)
                link(nc.vector.memset(bqk_raw[:, :], 0.0))
                nc.vector.memset(Wqk1[:, :, :], 0.0).then_inc(w_pads, 2)
                dve.wait_ge(s_wT, RAW)
                nc.vector.tensor_copy(WbT[:, :], bank[0][:, 0:16])
                nc.vector.tensor_copy(WcT[:, :], bank[0][:, 32:48])
                nc.vector.tensor_copy(WdT[:, :], bank[1][:, 0:P])
                nc.vector.tensor_copy(WvT[:, :], bank[4][:, 0:P])
                nc.vector.tensor_copy(WpT[:, :], bank[5][:, 0:P])
                nc.vector.tensor_copy(b1[:, :], bank[6][:, 0:FT])
                link(nc.vector.tensor_reduce(b2two[:, :], bank[6][:, FT:FT + EXPERTS], AX.X, ALU.add))
                dve.wait_ge(w_pads, 3)
                for kind in range(2):
                    for half in range(2):
                        to = Wqk1[:, 2 * kind + half, :].rearrange("p (j r) -> p j r", r=32)[:, :, 0:HD]
                        of = bank[2 + kind][:, half * 64:half * 64 + 64].rearrange("p (j r) -> p j r", r=HD)
                        nc.vector.tensor_copy(to, of)
                dve.wait_ge(w_l1, 16 * 16)
                nc.vector.tensor_scalar(bqk[:, 0:2], bqk_raw[:, 0:2], HD ** -0.5, None, ALU.mult)
                nc.vector.tensor_copy(bqk[:, 2:4], bqk_raw[:, 2:4])
                dve.wait_ge(w_l3, 4 * 16)
                link(nc.vector.tensor_scalar(b2two[:, :], b2two[:, :], 2.0, None, ALU.mult))
                link(nc.vector.tensor_scalar(norm_w[:, 0, :], norm_w[:, 0, :], HD ** -0.5, None, ALU.mult))
                H = HD // 2
                for t in range(NT):
                    for kind in range(2):
                        nc.vector.tensor_tensor(cosw[:, t, kind, :], rope[:, 0, t, :], norm_w[:, kind, :], ALU.mult)
                        nc.vector.scalar_tensor_tensor(sinw[:, t, kind, 0:H], rope[:, 1, t, 0:H], -1.0,
                                                       norm_w[:, kind, H:HD], ALU.mult, ALU.mult)
                        nc.vector.tensor_tensor(sinw[:, t, kind, H:HD], rope[:, 1, t, H:HD], norm_w[:, kind, 0:H], ALU.mult)

            @block.scalar
            def _(act):
                act.sem_inc(w_pads, 1)

        x_in = signal("l0_x_in", 16)
        ps_x, ps_q, ps_d = signal("l0_xT", 1), signal("l0_qk", 2), signal("l0_d", 1, True)
        a_st = signal("l0_stored", 4)
        s_S, s_nm, s_E = signal("l0_scores", 2), signal("l0_negmax", 2), signal("l0_exp", 4)
        s_ET, s_ETs, s_O = signal("l0_ET", 2), signal("l0_ET_stored", 2), signal("l0_O", 2)
        s_r, s_rc, s_mm, s_gm, s_done = (signal("l0_r", 1), signal("l0_r_c", 1), signal("l0_moments", 1),
                                         signal("l0_group_moments", 1), signal("l0_done", 1, True))
        s_link = sem("l0_steps")
        with nc.Block() as block:
            @block.sync
            def _(sp):
                with sp.Fori(0, GROUPS) as i:
                    sp.wait_ge(ps_d.sem, ps_d.before(i))
                    sp.dma_start(xs[:, :].rearrange("p (b n) -> p b n", n=N), X[:, bass.ds(i * PAIR, PAIR), :]).then_inc(x_in.sem, 16)

            @block.tensor
            def _(pe):
                pe.sem_inc(ps_d.sem, ps_d.ahead)
                with pe.Fori(0, GROUPS) as i:
                    pe.wait_ge(x_in.sem, x_in.after(i))
                    pe.wait_ge(s_done.sem, s_done.before(i))
                    for t in range(TILES):
                        ins = nc.tensor.transpose(bank[0][:, t * P:(t + 1) * P], xs[:, t * P:(t + 1) * P], ident[:, :])
                    ins.then_inc(ps_x.sem, 1)
                    nc.tensor.matmul(bank[1][0:16, :], WbT[:, :], xs[:, :], start=True, stop=True).then_inc(ps_q.sem, 1)
                    nc.tensor.matmul(bank[2][0:16, :], WcT[:, :], xs[:, :], start=True, stop=True).then_inc(ps_q.sem, 1)
                    for t in range(TILES):
                        ins = nc.tensor.matmul(bank[3][:, t * P:(t + 1) * P], xs[:, t * P:(t + 1) * P], WdT[:, :],
                                               start=True, stop=True)
                    ins.then_inc(ps_d.sem, 1)
                    ins = None
                    pe.wait_ge(a_st.sem, a_st.after(i, 3))
                    for b in range(PAIR):
                        for t in range(NT):
                            a = b * N + t * P
                            ins = nc.tensor.matmul(bank[4 + b][:, t * N:(t + 1) * N], q_s[0:16, 0, a:a + P],
                                                   k_s[0:16, 0, b * N:(b + 1) * N], start=True, stop=True)
                        ins.then_inc(s_S.sem, 1)
                    for b in range(PAIR):
                        pe.wait_ge(s_E.sem, s_E.after(i, 2 * b + 2))
                        for t in range(NT):
                            for kt in range(NT):
                                ins = nc.tensor.transpose(bank[6 + b][:, kt * N + t * P:kt * N + (t + 1) * P],
                                                          E_s[:, 0, b, t, kt * P:(kt + 1) * P], ident[:, :])
                        ins.then_inc(s_ET.sem, 1)
                    pe.wait_ge(a_st.sem, a_st.after(i, 4))
                    for b in range(PAIR):
                        pe.wait_ge(s_ETs.sem, s_ETs.after(i, b + 1))
                        for t in range(NT):
                            for kt in range(NT):
                                ins = nc.tensor.matmul(bank[b][:, t * P:(t + 1) * P],
                                                       ET_s[:, b, kt, t * P:(t + 1) * P], v_s[:, b * NT + kt, :],
                                                       start=(kt == 0), stop=(kt == NT - 1))
                        ins.then_inc(s_O.sem, 1)
                    pe.wait_ge(s_r.sem, s_r.after(i))
                    for t in range(TILES):
                        ins = nc.tensor.transpose(bank[2][:, t * P:(t + 1) * P], r_s[:, t * P:(t + 1) * P], ident[:, :])
                    ins.then_inc(s_rc.sem, 1)
                    pe.wait_ge(s_mm.sem, s_mm.after(i))
                    nc.tensor.matmul(bank[3][:, 0:2 * PAIR], groups4[:, :], mm_s[:, :, :].rearrange("p b m -> p (b m)"),
                                     start=True, stop=True).then_inc(s_gm.sem, 1)

            @block.scalar
            def _(act):
                with act.Fori(0, GROUPS) as i:
                    act.wait_ge(ps_x.sem, ps_x.after(i))
                    act.wait_ge(s_done.sem, s_done.before(i))
                    nc.scalar.copy(xT_s[:, :], bank[0][:, :]).then_inc(a_st.sem, 1)
                    act.wait_ge(ps_q.sem, ps_q.after(i, 1))
                    nc.scalar.copy(q_s[0:16, 0, :], bank[1][0:16, :]).then_inc(a_st.sem, 1)
                    act.wait_ge(ps_q.sem, ps_q.after(i, 2))
                    nc.scalar.copy(k_s[0:16, 0, :], bank[2][0:16, :]).then_inc(a_st.sem, 1)
                    act.wait_ge(ps_d.sem, ps_d.after(i))
                    nc.scalar.copy(v_s[:, :, :].rearrange("p t c -> p (t c)"), bank[3][:, :]).then_inc(a_st.sem, 1)
                    for b in range(PAIR):
                        act.wait_ge(s_nm.sem, s_nm.after(i, b + 1))
                        for t in range(NT):
                            nc.scalar.activation(E_s[:, 0, b, t, :], bank[4 + b][:, t * N:(t + 1) * N], ACT.Exp,
                                                 bias=negmax[:, b, 0, t:t + 1],
                                                 accum_out=rowsum[:, b, 0, t:t + 1]).then_inc(s_E.sem, 1)

            @block.vector
            def _(dve):
                link = Chain(dve, s_link)
                STEPS = 9 + RSQRT
                dve.sem_inc(s_done.sem, s_done.ahead)
                with dve.Fori(0, GROUPS) as i:
                    link.turn(i, STEPS)
                    for b in range(PAIR):
                        dve.wait_ge(s_S.sem, s_S.after(i, b + 1))
                        nc.vector.tensor_reduce(negmax[:, b, 0, :], bank[4 + b][:, :].rearrange("p (t k) -> p t k", t=NT),
                                                AX.X, ALU.max, negate=True).then_inc(s_nm.sem, 1)
                    for b in range(PAIR):
                        dve.wait_ge(s_ET.sem, s_ET.after(i, b + 1))
                        nc.vector.tensor_copy(ET_s[:, b, :, :].rearrange("p k n -> p (k n)"), bank[6 + b][:, :]).then_inc(s_ETs.sem, 1)
                    dve.wait_ge(s_E.sem, s_E.after(i))
                    link(nc.vector.reciprocal(rinv[:, :, 0, :], rowsum[:, :, 0, :]))
                    link(nc.vector.tensor_scalar(rinv[:, :, 0, :], rinv[:, :, 0, :], gamma_all[:, :], None, ALU.mult))
                    for b in range(PAIR):
                        dve.wait_ge(s_O.sem, s_O.after(i, b + 1))
                        for t in range(NT):
                            a = (b * NT + t) * P
                            ins = nc.vector.scalar_tensor_tensor(r_s[:, a:a + P], bank[b][:, t * P:(t + 1) * P],
                                                                 rinv[:, b, 0, t:t + 1], xT_s[:, a:a + P], ALU.mult, ALU.add)
                    ins.then_inc(s_r.sem, 1)
                    dve.wait_ge(s_r.sem, s_r.after(i))
                    link(nc.vector.tensor_tensor(R[:, bass.ds(i * W, W)].rearrange("p (t c) -> p t c", c=P),
                                                 r_s[:, :].rearrange("p (t c) -> p t c", c=P),
                                                 bp_all[:, None, :].broadcast_to([P, TILES, P]), ALU.add))
                    dve.wait_ge(s_rc.sem, s_rc.after(i))
                    for b in range(PAIR):
                        ins = nc.vector.bn_stats(stats[:, b, :], bank[2][:, b * N:(b + 1) * N])
                    link(ins)
                    hold(dve)
                    for b in range(PAIR):
                        ins = nc.vector.bn_aggr(mm_s[:, b, :], stats[:, b, :])
                    link(ins)
                    link(nc.vector.tensor_tensor(ntmp[:, 0:PAIR], mm_s[:, :, 0], mm_s[:, :, 0], ALU.mult))
                    nc.vector.tensor_tensor(mm_s[:, :, 1], mm_s[:, :, 1], ntmp[:, 0:PAIR], ALU.add).then_inc(s_mm.sem, 1)
                    dve.wait_ge(s_gm.sem, s_gm.after(i))
                    link(nc.vector.tensor_copy(gm[:, :, :].rearrange("p b m -> p (b m)"), bank[3][:, 0:2 * PAIR]))
                    link(nc.vector.tensor_tensor(ntmp[:, 0:PAIR], gm[:, :, 0], gm[:, :, 0], ALU.mult))
                    link(nc.vector.scalar_tensor_tensor(var[:, 0:PAIR], gm[:, :, 1], 1e-5, ntmp[:, 0:PAIR],
                                                        ALU.add, ALU.subtract))
                    rsqrt(link, PAIR)
                    for b in range(PAIR):
                        ins = nc.vector.tensor_scalar(XN_C[:, bass.ds(i * W + b * N, N)], bank[2][:, b * N:(b + 1) * N],
                                                      gm[:, b, 0:1], rstd[:, b:b + 1], ALU.subtract, ALU.mult)
                    ins.then_inc(s_done.sem, 1)
                    link.ended(STEPS)

        UNITS = PAIR * HEADS
        xs_in = signal("l1_xs_in", 16)
        p_qk, p_v, a_qk, v_st = signal("l1_qk", 4), signal("l1_v", 1, True), signal("l1_qk_stored", 4), signal("l1_v_stored", 1)
        s_S, s_nm, s_E = signal("l1_scores", UNITS), signal("l1_negmax", UNITS), signal("l1_exp", UNITS)
        s_ET, s_ETs, s_PV = signal("l1_ET", UNITS), signal("l1_ET_stored", UNITS), signal("l1_PV", UNITS)
        s_o, s_oT, s_oTs, s_y = (signal("l1_o", PAIR), signal("l1_oT", PAIR), signal("l1_oT_stored", PAIR),
                                 signal("l1_y", PAIR))
        s_xn, s_xT, s_xTs, s_done = (signal("l1_xn", PAIR), signal("l1_xnT", PAIR), signal("l1_xn_kept", PAIR, True),
                                     signal("l1_done", 2, True))
        s_link = sem("l1_steps")
        ET_LAG, PV_LAG = 2, 3
        with nc.Block() as block:
            @block.sync
            def _(sp):
                with sp.Fori(0, GROUPS) as i:
                    sp.wait_ge(p_v.sem, p_v.before(i))
                    sp.dma_start(xs[:, :], XN_C[:, bass.ds(i * W, W)]).then_inc(xs_in.sem, 16)

            @block.tensor
            def _(pe):
                pe.sem_inc(p_v.sem, p_v.ahead)

                def scores(i, u):
                    b, half, j = u // HEADS, u // SLOTS % 2, u % SLOTS
                    if u >= SLOTS:
                        pe.wait_ge(s_E.sem, s_E.after(i, u - SLOTS + 1))
                    rows = slice(32 * j, 32 * j + HD)
                    for t in range(NT):
                        a = b * N + t * P
                        ins = nc.tensor.matmul(bank[j][:, t * N:(t + 1) * N], q_s[rows, half, a:a + P],
                                               k_s[rows, half, b * N:(b + 1) * N], start=True, stop=True)
                    ins.then_inc(s_S.sem, 1)

                def turn_exp(i, u):
                    pe.wait_ge(s_E.sem, s_E.after(i, u + 1))
                    if u >= 2:
                        pe.wait_ge(s_ETs.sem, s_ETs.after(i, u - 1))
                    for t in range(NT):
                        for kt in range(NT):
                            ins = nc.tensor.transpose(bank[4 + u % 2][:, kt * N + t * P:kt * N + (t + 1) * P],
                                                      E_s[:, 0, u % SLOTS, t, kt * P:(kt + 1) * P], ident[:, :])
                    ins.then_inc(s_ET.sem, 1)

                def values(i, u):
                    b, h = u // HEADS, u % HEADS
                    pe.wait_ge(s_ETs.sem, s_ETs.after(i, u + 1))
                    for t in range(NT):
                        for kt in range(NT):
                            ins = nc.tensor.matmul(bank[6 + b][:, t * P + h * HD:t * P + (h + 1) * HD],
                                                   ET_s[:, u % SLOTS, kt, t * P:(t + 1) * P],
                                                   v_s[:, b * NT + kt, h * HD:(h + 1) * HD],
                                                   start=(kt == 0), stop=(kt == NT - 1))
                    ins.then_inc(s_PV.sem, 1)

                def turn_out(i, b):
                    pe.wait_ge(s_o.sem, s_o.after(i, b + 1))
                    for t in range(NT):
                        ins = nc.tensor.transpose(bank[6 + b][:, N + t * P:N + (t + 1) * P], o_s[:, b * NT + t, :], ident[:, :])
                    ins.then_inc(s_oT.sem, 1)

                def project(i, b):
                    pe.wait_ge(s_oTs.sem, s_oTs.after(i, b + 1))
                    for t in range(NT):
                        a = b * N + t * P
                        ins = nc.tensor.matmul(bank[6 + b][:, t * P:(t + 1) * P], oT_s[:, a:a + P], WpT[:, :],
                                               start=True, stop=True)
                    ins.then_inc(s_y.sem, 1)

                def turn_norm(i, b):
                    pe.wait_ge(s_xn.sem, s_xn.after(i, b + 1))
                    for t in range(NT):
                        a = b * N + t * P
                        ins = nc.tensor.transpose(bank[6 + b][:, N + t * P:N + (t + 1) * P], xn_s[:, a:a + P], ident[:, :])
                    ins.then_inc(s_xT.sem, 1)

                with pe.Fori(0, GROUPS) as i:
                    pe.wait_ge(xs_in.sem, xs_in.after(i))
                    pe.wait_ge(s_done.sem, s_done.before(i))
                    for n in range(4):
                        nc.tensor.matmul(bank[n][:, :], Wqk1[:, n, :], xs[:, :], start=True, stop=True).then_inc(p_qk.sem, 1)
                    for t in range(TILES):
                        ins = nc.tensor.matmul(bank[4][:, t * P:(t + 1) * P], xs[:, t * P:(t + 1) * P], WvT[:, :],
                                               start=True, stop=True)
                    ins.then_inc(p_v.sem, 1)
                    pe.wait_ge(a_qk.sem, a_qk.after(i))
                    pe.wait_ge(v_st.sem, v_st.after(i))
                    for s in range(UNITS + PV_LAG):
                        if s < UNITS:
                            scores(i, s)
                        if ET_LAG <= s < UNITS + ET_LAG:
                            turn_exp(i, s - ET_LAG)
                        if s >= PV_LAG:
                            values(i, s - PV_LAG)
                        if s == HEADS + PV_LAG + 1:
                            turn_out(i, 0)
                        if s == HEADS + PV_LAG + 3:
                            project(i, 0)
                    turn_norm(i, 0)
                    turn_out(i, 1)
                    project(i, 1)
                    turn_norm(i, 1)

            @block.scalar
            def _(act):
                act.sem_inc(s_done.sem, s_done.ahead)

                def store_out(i, b):
                    act.wait_ge(s_oT.sem, s_oT.after(i, b + 1))
                    nc.scalar.copy(oT_s[:, b * N:(b + 1) * N], bank[6 + b][:, N:2 * N]).then_inc(s_oTs.sem, 1)

                def store_norm(i, b):
                    act.wait_ge(s_xT.sem, s_xT.after(i, b + 1))
                    hold(act)
                    nc.scalar.copy(XN_C[:, bass.ds(i * W + b * N, N)], bank[6 + b][:, N:2 * N]).then_inc(s_done.sem, 1)

                with act.Fori(0, GROUPS) as i:
                    for n in range(4):
                        act.wait_ge(p_qk.sem, p_qk.after(i, n + 1))
                        to = q_s if n < 2 else k_s
                        nc.scalar.activation(to[:, n % 2, :], bank[n][:, :], ACT.Identity, bias=bqk[:, n:n + 1],
                                             scale=HD ** -0.5 if n < 2 else 1.0).then_inc(a_qk.sem, 1)
                    for u in range(UNITS):
                        b, h = u // HEADS, u % HEADS
                        act.wait_ge(s_nm.sem, s_nm.after(i, u + 1))
                        if u >= SLOTS:
                            act.wait_ge(s_ET.sem, s_ET.after(i, u - SLOTS + 1))
                        for t in range(NT):
                            ins = nc.scalar.activation(E_s[:, 0, u % SLOTS, t, :], bank[u % SLOTS][:, t * N:(t + 1) * N],
                                                       ACT.Exp, bias=negmax[:, b, h, t:t + 1],
                                                       accum_out=rowsum[:, b, h, t:t + 1])
                        ins.then_inc(s_E.sem, 1)
                        if u == HEADS + PV_LAG + 3:
                            store_out(i, 0)
                    store_norm(i, 0)
                    store_out(i, 1)
                    store_norm(i, 1)

            @block.vector
            def _(dve):
                link = Chain(dve, s_link)
                STEPS = PAIR * (3 + NORM)

                def normalise(i, b):
                    dve.wait_ge(s_PV.sem, s_PV.after(i, (b + 1) * HEADS))
                    link(nc.vector.reciprocal(rinv[:, b, :, :], rowsum[:, b, :, :]))
                    nc.vector.tensor_tensor(o_s[:, b * NT:(b + 1) * NT, :].rearrange("p t (h d) -> p t h d", d=HD),
                                            bank[6 + b][:, 0:N].rearrange("p (t h d) -> p t h d", t=NT, d=HD),
                                            rinv[:, b, :, :].rearrange("p h t -> p t h")[:, :, :, None].broadcast_to([P, NT, HEADS, HD]),
                                            ALU.mult).then_inc(s_o.sem, 1)

                def residual(i, b):
                    dve.wait_ge(s_xTs.sem, s_xTs.before(i))
                    dve.wait_ge(s_y.sem, s_y.after(i, b + 1))
                    at = bass.ds(i * W + b * N, N)
                    link(nc.vector.tensor_tensor(r_s[:, b * N:(b + 1) * N], bank[6 + b][:, 0:N], R[:, at], ALU.add))
                    hold(dve)
                    link(nc.vector.tensor_copy(R[:, at], r_s[:, b * N:(b + 1) * N]))
                    token_norm(dve, link, 1e-5, range(b * NT, (b + 1) * NT), s_xn)

                with dve.Fori(0, GROUPS) as i:
                    link.turn(i, STEPS)
                    dve.wait_ge(p_v.sem, p_v.after(i))
                    nc.vector.tensor_tensor(v_s[:, :, :], bank[4][:, :].rearrange("p (t c) -> p t c", c=P),
                                            bv_all[:, None, :].broadcast_to([P, TILES, P]), ALU.add).then_inc(v_st.sem, 1)
                    for s in range(UNITS + PV_LAG):
                        if s < UNITS:
                            dve.wait_ge(s_S.sem, s_S.after(i, s + 1))
                            nc.vector.tensor_reduce(negmax[:, s // HEADS, s % HEADS, :],
                                                    bank[s % SLOTS][:, :].rearrange("p (t k) -> p t k", t=NT),
                                                    AX.X, ALU.max, negate=True).then_inc(s_nm.sem, 1)
                        u = s - ET_LAG
                        if 0 <= u < UNITS:
                            dve.wait_ge(s_ET.sem, s_ET.after(i, u + 1))
                            if u >= SLOTS:
                                dve.wait_ge(s_PV.sem, s_PV.after(i, u - SLOTS + 1))
                            nc.vector.tensor_copy(ET_s[:, u % SLOTS, :, :].rearrange("p k n -> p (k n)"),
                                                  bank[4 + u % 2][:, :]).then_inc(s_ETs.sem, 1)
                        if s == HEADS + PV_LAG:
                            normalise(i, 0)
                    residual(i, 0)
                    normalise(i, 1)
                    residual(i, 1)
                    link.ended(STEPS)

            @block.gpsimd
            def _(pool):
                pool.sem_inc(s_xTs.sem, s_xTs.ahead)
                with pool.Fori(0, GROUPS) as i:
                    for b in range(PAIR):
                        pool.wait_ge(s_xn.sem, s_xn.after(i, b + 1))
                        hold(pool)
                        nc.gpsimd.tensor_copy(XN_T[:, bass.ds(i * W + b * N, N)], xn_s[:, b * N:(b + 1) * N]).then_inc(s_xTs.sem, 1)

        layer2 = ctx.enter_context(ExitStack())

        def sb2(name, shape, dt=F32):
            return layer2.enter_context(nc.sbuf_tensor(name, shape, dt))

        PB = sb2("PB", [P, GROUPS * 2 * W])
        z_s = sb2("z_s", [P, 3, 2 * W])
        g_s = sb2("g_s", [P, 3, 2 * W])
        h_s = sb2("h_s", [P, 3, W])

        xs_in = signal("l2_xs_in", 16)
        s_S, s_nm, s_E = signal("l2_scores", 2, True), signal("l2_negmax", 2), signal("l2_exp", 2)
        s_ET, s_ETs, s_O = signal("l2_ET", 2), signal("l2_ET_stored", 2), signal("l2_O", 2)
        s_xn, s_xT, s_xTs, s_xc = signal("l2_xn", 1), signal("l2_xnT", 1), signal("l2_xnT_stored", 1), signal("l2_xn_c", 1, True)
        s_lg, s_gap, s_e, s_p = signal("l2_logits", 1), signal("l2_gap", 1), signal("l2_gate_exp", 1), signal("l2_gates", 1)
        s_pb, s_done = signal("l2_gate_rows", 2), signal("l2_done", 2, True)
        s_link = sem("l2_steps")
        with nc.Block() as block:
            @block.sync
            def _(sp):
                with sp.Fori(0, GROUPS) as i:
                    sp.wait_ge(s_S.sem, s_S.before(i))
                    sp.dma_start(xs[:, :], XN_C[:, bass.ds(i * W, W)]).then_inc(xs_in.sem, 16)

            @block.tensor
            def _(pe):
                pe.sem_inc(s_S.sem, s_S.ahead)
                with pe.Fori(0, GROUPS) as i:
                    pe.wait_ge(xs_in.sem, xs_in.after(i))
                    pe.wait_ge(s_done.sem, s_done.before(i))
                    for b in range(PAIR):
                        for t in range(NT):
                            a = b * N + t * P
                            ins = nc.tensor.matmul(bank[b][:, t * N:(t + 1) * N], xs[:, a:a + P], xs[:, b * N:(b + 1) * N],
                                                   start=True, stop=True)
                        ins.then_inc(s_S.sem, 1)
                    for b in range(PAIR):
                        pe.wait_ge(s_E.sem, s_E.after(i, b + 1))
                        for t in range(NT):
                            for kt in range(NT):
                                ins = nc.tensor.transpose(bank[2 + b][:, kt * N + t * P:kt * N + (t + 1) * P],
                                                          E_s[:, 0, b, t, kt * P:(kt + 1) * P], ident[:, :])
                        ins.then_inc(s_ET.sem, 1)
                    for b in range(PAIR):
                        pe.wait_ge(s_ETs.sem, s_ETs.after(i, b + 1))
                        for t in range(NT):
                            for kt in range(NT):
                                ins = nc.tensor.matmul(bank[4 + b][:, t * P:(t + 1) * P], ET_s[:, b, kt, t * P:(t + 1) * P],
                                                       XN_T[:, bass.ds(i * W + (b * NT + kt) * P, P)],
                                                       start=(kt == 0), stop=(kt == NT - 1))
                        ins.then_inc(s_O.sem, 1)
                    pe.wait_ge(s_xn.sem, s_xn.after(i))
                    for t in range(TILES):
                        ins = nc.tensor.transpose(bank[6][:, t * P:(t + 1) * P], xn_s[:, t * P:(t + 1) * P], ident[:, :])
                    ins.then_inc(s_xT.sem, 1)
                    pe.wait_ge(s_xTs.sem, s_xTs.after(i))
                    for t in range(TILES):
                        ins = nc.tensor.matmul(bank[7][:, t * EXPERTS:(t + 1) * EXPERTS], xc_s[:, t * P:(t + 1) * P], Wg[:, :],
                                               start=True, stop=True)
                    ins.then_inc(s_lg.sem, 1)
                    pe.wait_ge(s_p.sem, s_p.after(i))
                    for w in range(2):
                        for t in range(TILES):
                            ins = nc.tensor.transpose(bank[w][:, t * P:(t + 1) * P],
                                                      gate[:, 3 + w, t:t + 1].broadcast_to([P, P]), ident[:, :])
                        ins.then_inc(s_pb.sem, 1)

            @block.scalar
            def _(act):
                act.sem_inc(s_done.sem, s_done.ahead)
                with act.Fori(0, GROUPS) as i:
                    for b in range(PAIR):
                        act.wait_ge(s_nm.sem, s_nm.after(i, b + 1))
                        for t in range(NT):
                            ins = nc.scalar.activation(E_s[:, 0, b, t, :], bank[b][:, t * N:(t + 1) * N], ACT.Exp,
                                                       bias=negmax[:, b, 0, t:t + 1], accum_out=rowsum[:, b, 0, t:t + 1])
                        ins.then_inc(s_E.sem, 1)
                    act.wait_ge(s_xc.sem, s_xc.before(i))
                    act.wait_ge(s_xT.sem, s_xT.after(i))
                    nc.scalar.copy(xc_s[:, :], bank[6][:, :]).then_inc(s_xTs.sem, 1)
                    act.wait_ge(s_gap.sem, s_gap.after(i))
                    nc.scalar.activation(gate[:, 1, :], gate[:, 0, :], ACT.Exp).then_inc(s_e.sem, 1)
                    for w in range(2):
                        act.wait_ge(s_pb.sem, s_pb.after(i, w + 1))
                        hold(act)
                        nc.scalar.copy(PB[:, bass.ds(i * 2 * W + w * W, W)], bank[w][:, :]).then_inc(s_done.sem, 1)

            @block.vector
            def _(dve):
                link = Chain(dve, s_link)
                STEPS = 3 + NORM + 3
                with dve.Fori(0, GROUPS) as i:
                    link.turn(i, STEPS)
                    for b in range(PAIR):
                        dve.wait_ge(s_S.sem, s_S.after(i, b + 1))
                        nc.vector.tensor_reduce(negmax[:, b, 0, :], bank[b][:, :].rearrange("p (t k) -> p t k", t=NT),
                                                AX.X, ALU.max, negate=True).then_inc(s_nm.sem, 1)
                    for b in range(PAIR):
                        dve.wait_ge(s_ET.sem, s_ET.after(i, b + 1))
                        nc.vector.tensor_copy(ET_s[:, b, :, :].rearrange("p k n -> p (k n)"), bank[2 + b][:, :]).then_inc(s_ETs.sem, 1)
                    link(nc.vector.reciprocal(rinv[:, :, 0, :], rowsum[:, :, 0, :]))
                    dve.wait_ge(s_O.sem, s_O.after(i))
                    for b in range(PAIR):
                        for t in range(NT):
                            a = b * N + t * P
                            ins = nc.vector.scalar_tensor_tensor(r_s[:, a:a + P], bank[4 + b][:, t * P:(t + 1) * P],
                                                                 rinv[:, b, 0, t:t + 1], R[:, bass.ds(i * W + a, P)],
                                                                 ALU.mult, ALU.add)
                    link(ins)
                    hold(dve)
                    link(nc.vector.tensor_copy(R[:, bass.ds(i * W, W)], r_s[:, :]))
                    token_norm(dve, link, 1e-5, range(TILES), s_xn)
                    dve.wait_ge(s_lg.sem, s_lg.after(i))
                    hold(dve)
                    for t in range(TILES):
                        ins = nc.vector.max(top[:, t, :], bank[7][:, t * EXPERTS:(t + 1) * EXPERTS])
                    link(ins)
                    nc.vector.tensor_tensor(gate[:, 0, :], top[:, :, 1], top[:, :, 0], ALU.subtract).then_inc(s_gap.sem, 1)
                    dve.wait_ge(s_e.sem, s_e.after(i))
                    link(nc.vector.tensor_scalar(gate[:, 2, :], gate[:, 1, :], 1.0, None, ALU.add))
                    link(nc.vector.reciprocal(gate[:, 3, :], gate[:, 2, :]))
                    nc.vector.tensor_tensor(gate[:, 4, :], gate[:, 1, :], gate[:, 3, :], ALU.mult).then_inc(s_p.sem, 1)
                    link.ended(STEPS)

            @block.gpsimd
            def _(pool):
                pool.sem_inc(s_xc.sem, s_xc.ahead)
                with pool.Fori(0, GROUPS) as i:
                    pool.wait_ge(s_xTs.sem, s_xTs.after(i))
                    hold(pool)
                    nc.gpsimd.tensor_copy(XN_C[:, bass.ds(i * W, W)], xc_s[:, :]).then_inc(s_xc.sem, 1)

        s_U, s_z, s_g, s_h, s_D = (signal(n, FT) for n in ("ff_up", "ff_gated", "ff_gelu", "ff_hidden", "ff_down"))
        s_ys, s_yT, s_xn, s_xT, s_done = (signal("ff_y_stored", 1), signal("ff_yT", 1), signal("ff_xn", 1),
                                          signal("ff_xnT", 1), signal("ff_done", 1, True))
        s_link = sem("ff_steps")
        D_LAG, RING = 3, 3
        with nc.Block() as block:
            @block.tensor
            def _(pe):
                pe.wait_ge(w_l2, 13 * 16)
                with pe.Fori(0, GROUPS) as i:
                    pe.wait_ge(s_done.sem, s_done.before(i))
                    for s in range(FT + D_LAG):
                        if s < FT:
                            if s >= 4:
                                pe.wait_ge(s_z.sem, s_z.after(i, s - 3))
                            nc.tensor.matmul(bank[s % 4][:, :], W1[:, s // 4, s % 4 * P:(s % 4 + 1) * P],
                                             XN_C[:, bass.ds(i * W, W)], start=True, stop=True).then_inc(s_U.sem, 1)
                        f = s - D_LAG
                        if f >= 0:
                            pe.wait_ge(s_h.sem, s_h.after(i, f + 1))
                            nc.tensor.matmul(bank[7][:, :], W2[:, f, :], h_s[:, f % RING, :],
                                             start=(f == 0), stop=(f == FT - 1)).then_inc(s_D.sem, 1)
                    pe.wait_ge(s_ys.sem, s_ys.after(i))
                    for t in range(TILES):
                        ins = nc.tensor.transpose(bank[6][:, t * P:(t + 1) * P], y_s[:, t * P:(t + 1) * P], ident[:, :])
                    ins.then_inc(s_yT.sem, 1)
                    pe.wait_ge(s_xn.sem, s_xn.after(i))
                    for t in range(TILES):
                        ins = nc.tensor.transpose(bank[5][:, t * P:(t + 1) * P], xn_s[:, t * P:(t + 1) * P], ident[:, :])
                    ins.then_inc(s_xT.sem, 1)

            @block.vector
            def _(dve):
                link = Chain(dve, s_link)
                STEPS = 2 + NORM
                with dve.Fori(0, GROUPS) as i:
                    link.turn(i, STEPS)
                    for f in range(FT):
                        dve.wait_ge(s_U.sem, s_U.after(i, f + 1))
                        if f >= RING:
                            dve.wait_ge(s_g.sem, s_g.after(i, f - RING + 1))
                        nc.vector.tensor_tensor(z_s[:, f % RING, :].rearrange("p (w n) -> p w n", w=2),
                                                bank[f % 4][:, None, :].broadcast_to([P, 2, W]),
                                                PB[:, bass.ds(i * 2 * W, 2 * W)].rearrange("p (w n) -> p w n", w=2),
                                                ALU.mult).then_inc(s_z.sem, 1)
                    dve.wait_ge(s_yT.sem, s_yT.after(i))
                    link(nc.vector.tensor_tensor(r_s[:, :], bank[6][:, :], R[:, bass.ds(i * W, W)], ALU.add))
                    hold(dve)
                    link(nc.vector.tensor_copy(R[:, bass.ds(i * W, W)], r_s[:, :]))
                    token_norm(dve, link, 1e-5, range(TILES), s_xn)
                    link.ended(STEPS)

            @block.scalar
            def _(act):
                act.sem_inc(s_done.sem, s_done.ahead)
                with act.Fori(0, GROUPS) as i:
                    for f in range(FT):
                        act.wait_ge(s_z.sem, s_z.after(i, f + 1))
                        if f >= RING:
                            act.wait_ge(s_h.sem, s_h.after(i, f - RING + 1))
                        nc.scalar.activation(g_s[:, f % RING, :], z_s[:, f % RING, :], ACT.Gelu,
                                             bias=b1[:, f:f + 1]).then_inc(s_g.sem, 1)
                    act.wait_ge(s_D.sem, s_D.after(i))
                    nc.scalar.activation(y_s[:, :], bank[7][:, :], ACT.Identity, bias=b2two[:, :]).then_inc(s_ys.sem, 1)
                    act.wait_ge(s_xT.sem, s_xT.after(i))
                    hold(act)
                    nc.scalar.copy(XN_C[:, bass.ds(i * W, W)], bank[5][:, :]).then_inc(s_done.sem, 1)

            @block.gpsimd
            def _(pool):
                with pool.Fori(0, GROUPS) as i:
                    for f in range(FT):
                        pool.wait_ge(s_g.sem, s_g.after(i, f + 1))
                        if f >= RING:
                            pool.wait_ge(s_D.sem, s_D.after(i, f - RING + 1))
                        nc.gpsimd.tensor_tensor(h_s[:, f % RING, :], g_s[:, f % RING, 0:W], g_s[:, f % RING, W:2 * W],
                                                ALU.add).then_inc(s_h.sem, 1)
        layer2.close()

        CB = sb("CB", [P, GROUPS * 4 * W])
        attn3 = ctx.enter_context(ExitStack())

        def sb3(name, shape, dt=F32):
            return attn3.enter_context(nc.sbuf_tensor(name, shape, dt))

        xt_s = sb3("xt_s", [P, PAIR, P])
        et_s = sb3("et_s", [P, 2, P])
        cT_s = sb3("cT_s", [EXPERTS, W])
        qk3 = sb3("qk3", [P, TILES, 2 * P])
        qa = sb3("qa", [P, TILES, 2 * P])
        qb = sb3("qb", [P, TILES, 2 * P])
        qp = sb3("qp", [P, TILES, 4, P])

        xs_in = signal("l3_xs_in", 16)
        s_proj, s_tail, s_qks, s_vs = (signal("l3_qkv", TILES), signal("l3_v_tail", 1, True), signal("l3_qk_stored", TILES),
                                       signal("l3_v_stored", TILES))
        s_sq, s_rms, s_rot, s_qp, s_qT, s_qTs = (signal("l3_squares", 1), signal("l3_rms", 1), signal("l3_rotated", 1),
                                                 signal("l3_qk_ready", 1), signal("l3_qkT", 4), signal("l3_qkT_stored", 4))
        s_S, s_nm, s_E = signal("l3_scores", UNITS), signal("l3_negmax", UNITS), signal("l3_exp", UNITS)
        s_ET, s_ETs, s_PV = signal("l3_ET", UNITS), signal("l3_ET_stored", UNITS), signal("l3_PV", UNITS)
        s_o, s_oT, s_oTs, s_y = signal("l3_o", PAIR), signal("l3_oT", PAIR), signal("l3_oT_stored", PAIR), signal("l3_y", PAIR)
        s_r, s_rT, s_rTs = signal("l3_r", PAIR), signal("l3_rT", PAIR), signal("l3_rT_stored", PAIR)
        s_xn, s_xT, s_xTs, s_xc = (signal("l3_xn", PAIR), signal("l3_xnT", PAIR), signal("l3_xnT_stored", PAIR),
                                   signal("l3_xn_c", 1, True))
        s_lg, s_sh, s_pe, s_cb, s_cr, s_done = (signal("l3_logits", 1), signal("l3_shifted", 1), signal("l3_router_exp", 1),
                                                signal("l3_combine", 1), signal("l3_combine_rows", 4), signal("l3_done", 4, True))
        s_xt, s_et, s_cT, s_cTs = (signal("l3_tail_tokens", 1), signal("l3_exp_tail", UNITS // SLOTS),
                                   signal("l3_combineT", 1), signal("l3_combineT_stored", 1))
        s_link, s_pads = sem("l3_steps"), sem("l3_pads_zero")
        with nc.Block() as block:
            @block.sync
            def _(sp):
                with sp.Fori(0, GROUPS) as i:
                    sp.wait_ge(s_tail.sem, s_tail.before(i))
                    sp.dma_start(xs[:, :], XN_C[:, bass.ds(i * W, W)]).then_inc(xs_in.sem, 16)

            @block.tensor
            def _(pe):
                pe.sem_inc(s_tail.sem, s_tail.ahead)

                def scores(i, u):
                    b, half, j = u // HEADS, u // SLOTS % 2, u % SLOTS
                    if u >= SLOTS:
                        pe.wait_ge(s_E.sem, s_E.after(i, u - SLOTS + 1))
                    rows = slice(32 * j, 32 * j + HD)
                    nc.tensor.matmul(bank[j][:, 0:2 * KEYS], identb[:, :], bandb[:, :, :].rearrange("p t s -> p (t s)"),
                                     start=True, stop=False, skip_group_check=True)
                    nc.tensor.matmul(bank[j][:, WIN:KEYS], q_s[rows, half, b * N:b * N + P], k_s[rows, half, b * N:b * N + P],
                                     start=False, stop=False, skip_group_check=True)
                    nc.tensor.matmul(bank[j][:, KEYS:2 * KEYS], q_s[rows, half, b * N + P:(b + 1) * N],
                                     k_s[rows, half, b * N + P - WIN:(b + 1) * N],
                                     start=False, stop=True, skip_group_check=True).then_inc(s_S.sem, 1)

                def turn_exp(i, u):
                    g, j = u // SLOTS % 2, u % SLOTS
                    pe.wait_ge(s_E.sem, s_E.after(i, u + 1))
                    if u >= 2:
                        pe.wait_ge(s_ETs.sem, s_ETs.after(i, u - 1))
                    to = bank[4 + u % 2]
                    for t in range(NT):
                        ins = nc.tensor.transpose(to[:, t * P:(t + 1) * P], E_s[:, g, j, t, WIN:KEYS], ident[:, :])
                    if j == SLOTS - 1:
                        pe.wait_ge(s_et.sem, s_et.after(i, u // SLOTS + 1))
                        ins = nc.tensor.transpose(to[:, N:N + P], et_s[:, g, :], ident[:, :])
                    ins.then_inc(s_ET.sem, 1)

                def values(i, u):
                    b, h, g = u // HEADS, u % HEADS, u // SLOTS % 2
                    pe.wait_ge(s_ETs.sem, s_ETs.after(i, u + 1))
                    for t in range(NT):
                        a = t * P + h * HD
                        ins = nc.tensor.matmul(bank[6 + b][:, a:a + HD], ET_s[:, u % SLOTS, 0, t * P:(t + 1) * P],
                                               v_s[:, b * NT + t, h * HD:(h + 1) * HD],
                                               start=(h == 0 and t == 0), stop=False, skip_group_check=True)
                    if u % SLOTS == SLOTS - 1:
                        a = h // SLOTS * SLOTS * HD
                        ins = nc.tensor.matmul(bank[6 + b][:, P + a:P + a + SLOTS * HD], tail_s[:, g, :],
                                               vt_s[:, b, a:a + SLOTS * HD],
                                               start=False, stop=(h == HEADS - 1), skip_group_check=True)
                    ins.then_inc(s_PV.sem, 1)

                def turn_tiles(to, column, of, b, done):
                    for t in range(NT):
                        a = b * N + t * P
                        ins = nc.tensor.transpose(to[:, column + t * P:column + (t + 1) * P], of[:, a:a + P], ident[:, :])
                    ins.then_inc(done.sem, 1)

                def turn_out(i, b):
                    pe.wait_ge(s_o.sem, s_o.after(i, b + 1))
                    turn_tiles(bank[6 + b], N, o_s[:, :, :].rearrange("p t c -> p (t c)"), b, s_oT)

                def project(i, b):
                    pe.wait_ge(s_oTs.sem, s_oTs.after(i, b + 1))
                    for t in range(NT):
                        a = b * N + t * P
                        ins = nc.tensor.matmul(bank[6 + b][:, t * P:(t + 1) * P], oT_s[:, a:a + P], Wo3[:, :],
                                               start=True, stop=True)
                    ins.then_inc(s_y.sem, 1)

                def turn_norm(i, b):
                    pe.wait_ge(s_r.sem, s_r.after(i, b + 1))
                    turn_tiles(bank[6 + b], 0, r_s, b, s_rT)
                    pe.wait_ge(s_rTs.sem, s_rTs.after(i, b + 1))
                    pe.wait_ge(s_xn.sem, s_xn.after(i, b + 1))
                    turn_tiles(bank[6 + b], N, xn_s, b, s_xT)

                with pe.Fori(0, GROUPS) as i:
                    pe.wait_ge(xs_in.sem, xs_in.after(i))
                    pe.wait_ge(s_done.sem, s_done.before(i))
                    for t in range(TILES):
                        nc.tensor.matmul(bank[t][:, 0:3 * P], xs[:, t * P:(t + 1) * P], Wqkv3[:, :],
                                         start=True, stop=True).then_inc(s_proj.sem, 1)
                    pe.wait_ge(s_xt.sem, s_xt.after(i))
                    for b in range(PAIR):
                        ins = nc.tensor.matmul(bank[4][:, b * P:(b + 1) * P],
                                               xt_s[:, b, :], Wqkv3[:, 2 * P:3 * P],
                                               start=True, stop=True)
                    ins.then_inc(s_tail.sem, 1)
                    pe.wait_ge(s_qp.sem, s_qp.after(i))
                    for n in range(4):
                        for t in range(TILES):
                            ins = nc.tensor.transpose(bank[4 + n][:, t * P:(t + 1) * P], qp[:, t, n, :], ident[:, :])
                        ins.then_inc(s_qT.sem, 1)
                    pe.wait_ge(s_qTs.sem, s_qTs.after(i))
                    for s in range(UNITS + PV_LAG):
                        if s < UNITS:
                            scores(i, s)
                        if ET_LAG <= s < UNITS + ET_LAG:
                            turn_exp(i, s - ET_LAG)
                        if s >= PV_LAG:
                            values(i, s - PV_LAG)
                        if s == HEADS + PV_LAG + 1:
                            turn_out(i, 0)
                        if s == HEADS + PV_LAG + 3:
                            project(i, 0)
                    turn_norm(i, 0)
                    turn_out(i, 1)
                    project(i, 1)
                    turn_norm(i, 1)
                    pe.wait_ge(s_xTs.sem, s_xTs.after(i))
                    for t in range(TILES):
                        ins = nc.tensor.matmul(bank[4][:, t * EXPERTS:(t + 1) * EXPERTS], xc_s[:, t * P:(t + 1) * P],
                                               router[:, :], start=True, stop=True)
                    ins.then_inc(s_lg.sem, 1)
                    pe.wait_ge(s_cb.sem, s_cb.after(i))
                    for t in range(TILES):
                        ins = nc.tensor.transpose(bank[5][0:EXPERTS, t * P:(t + 1) * P], pr[:, 3, t, :], ident[:, :])
                    ins.then_inc(s_cT.sem, 1)
                    pe.wait_ge(s_cTs.sem, s_cTs.after(i))
                    for n in range(4):
                        nc.tensor.matmul(bank[n][:, :], expert_rows[:, n * P:(n + 1) * P], cT_s[:, :],
                                         start=True, stop=True).then_inc(s_cr.sem, 1)

            @block.scalar
            def _(act):
                act.sem_inc(s_done.sem, s_done.ahead)

                def store_out(i, b):
                    act.wait_ge(s_oT.sem, s_oT.after(i, b + 1))
                    nc.scalar.copy(oT_s[:, b * N:(b + 1) * N], bank[6 + b][:, N:2 * N]).then_inc(s_oTs.sem, 1)

                def store_norm(i, b):
                    act.wait_ge(s_rT.sem, s_rT.after(i, b + 1))
                    hold(act)
                    nc.scalar.copy(R_C[:, bass.ds(i * W + b * N, N)], bank[6 + b][:, 0:N]).then_inc(s_rTs.sem, 1)
                    act.wait_ge(s_xT.sem, s_xT.after(i, b + 1))
                    nc.scalar.copy(xc_s[:, b * N:(b + 1) * N], bank[6 + b][:, N:2 * N]).then_inc(s_xTs.sem, 1)

                with act.Fori(0, GROUPS) as i:
                    for t in range(TILES):
                        act.wait_ge(s_proj.sem, s_proj.after(i, t + 1))
                        nc.scalar.copy(qk3[:, t, :], bank[t][:, 0:2 * P]).then_inc(s_qks.sem, 1)
                    act.wait_ge(s_qks.sem, s_qks.after(i))
                    nc.scalar.activation(qa[:, :, :], qk3[:, :, :], ACT.Square).then_inc(s_sq.sem, 1)
                    for t in range(TILES):
                        nc.scalar.copy(v_s[:, t, :], bank[t][:, 2 * P:3 * P]).then_inc(s_vs.sem, 1)
                    for n in range(4):
                        act.wait_ge(s_qT.sem, s_qT.after(i, n + 1))
                        to = q_s if n < 2 else k_s
                        nc.scalar.copy(to[:, n % 2, :], bank[4 + n][:, :]).then_inc(s_qTs.sem, 1)
                    for u in range(UNITS):
                        b, h, g, j = u // HEADS, u % HEADS, u // SLOTS % 2, u % SLOTS
                        act.wait_ge(s_nm.sem, s_nm.after(i, u + 1))
                        if u >= 2 * SLOTS:
                            act.wait_ge(s_ET.sem, s_ET.after(i, (u - 2 * SLOTS) // SLOTS * SLOTS + SLOTS))
                        for t in range(NT):
                            a = WIN if t == 0 else 0
                            ins = nc.scalar.activation(E_s[:, g, j, t, a:KEYS], bank[j][:, t * KEYS + a:(t + 1) * KEYS],
                                                       ACT.Exp, bias=negmax[:, b, h, t:t + 1],
                                                       accum_out=rowsum[:, b, h, t:t + 1])
                        ins.then_inc(s_E.sem, 1)
                        if u == HEADS + PV_LAG + 3:
                            store_out(i, 0)
                    act.wait_ge(s_xc.sem, s_xc.before(i))
                    store_norm(i, 0)
                    store_out(i, 1)
                    store_norm(i, 1)
                    act.wait_ge(s_sh.sem, s_sh.after(i))
                    nc.scalar.activation(pr[:, 1, :, :], pr[:, 0, :, :], ACT.Exp).then_inc(s_pe.sem, 1)
                    act.wait_ge(s_cT.sem, s_cT.after(i))
                    nc.scalar.copy(cT_s[:, :], bank[5][0:EXPERTS, :]).then_inc(s_cTs.sem, 1)
                    for n in range(4):
                        act.wait_ge(s_cr.sem, s_cr.after(i, n + 1))
                        hold(act)
                        nc.scalar.copy(CB[:, bass.ds(i * 4 * W + n * W, W)], bank[n][:, :]).then_inc(s_done.sem, 1)

            @block.vector
            def _(dve):
                link = Chain(dve, s_link)
                STEPS = 4 + RSQRT + PAIR * (1 + NORM) + 11

                def normalise(i, b):
                    dve.wait_ge(s_PV.sem, s_PV.after(i, (b + 1) * HEADS))
                    link(nc.vector.reciprocal(rinv[:, b, :, :], rowsum[:, b, :, :]))
                    nc.vector.tensor_tensor(o_s[:, b * NT:(b + 1) * NT, :].rearrange("p t (h d) -> p t h d", d=HD),
                                            bank[6 + b][:, 0:N].rearrange("p (t h d) -> p t h d", t=NT, d=HD),
                                            rinv[:, b, :, :].rearrange("p h t -> p t h")[:, :, :, None].broadcast_to([P, NT, HEADS, HD]),
                                            ALU.mult).then_inc(s_o.sem, 1)

                def residual(i, b):
                    dve.wait_ge(s_y.sem, s_y.after(i, b + 1))
                    at = bass.ds(i * W + b * N, N)
                    nc.vector.tensor_tensor(r_s[:, b * N:(b + 1) * N], bank[6 + b][:, 0:N], R[:, at], ALU.add).then_inc(s_r.sem, 1)
                    dve.wait_ge(s_r.sem, s_r.after(i, b + 1))
                    token_norm(dve, link, 1e-5, range(b * NT, (b + 1) * NT), s_xn)

                nc.vector.memset(qp[:, :, :, :], 0.0).then_inc(s_pads, 1)
                dve.wait_ge(s_pads, 1)
                with dve.Fori(0, GROUPS) as i:
                    link.turn(i, STEPS)
                    dve.wait_ge(s_tail.sem, s_tail.after(i))
                    for b in range(PAIR):
                        ins = nc.vector.tensor_tensor(vt_s[:, b, :].rearrange("p (h d) -> p h d", d=HD),
                                                      bank[4][:, b * P:(b + 1) * P].rearrange("p (h d) -> p h d", d=HD),
                                                      tail_mask[:, :, None].broadcast_to([P, HEADS, HD]), ALU.mult)
                    link(ins)
                    dve.wait_ge(s_sq.sem, s_sq.after(i))
                    heads = TILES * 2 * HEADS
                    link(nc.vector.tensor_reduce(var[:, 0:heads], qa[:, :, :].rearrange("p t (g d) -> p (t g) d", d=HD), AX.X, ALU.add))
                    link(nc.vector.tensor_scalar(var[:, 0:heads], var[:, 0:heads], 1.0 / HD, 1e-6, ALU.mult, ALU.add))
                    rsqrt(link, heads)
                    flat = qk3[:, :, :].rearrange("p t (g d) -> p (t g) d", d=HD)
                    nc.vector.tensor_tensor(flat, flat, rstd[:, 0:heads, None].broadcast_to([P, heads, HD]), ALU.mult).then_inc(s_rms.sem, 1)
                    dve.wait_ge(s_rms.sem, s_rms.after(i))
                    for t in range(TILES):
                        ins = nc.vector.tensor_tensor(qa[:, t, :].rearrange("p (c h d) -> p c h d", c=2, d=HD),
                                                      qk3[:, t, :].rearrange("p (c h d) -> p c h d", c=2, d=HD),
                                                      cosw[:, t % NT, :, None, :].broadcast_to([P, 2, HEADS, HD]), ALU.mult)
                    link(ins)
                    dve.wait_ge(s_rot.sem, s_rot.after(i))
                    nc.vector.tensor_tensor(qp[:, :, :, :].rearrange("p t n (j r) -> p (t n j) r", r=32)[:, :, 0:HD],
                                            qa[:, :, :].rearrange("p t (g d) -> p (t g) d", d=HD),
                                            qb[:, :, :].rearrange("p t (g d) -> p (t g) d", d=HD), ALU.add).then_inc(s_qp.sem, 1)
                    for s in range(UNITS + PV_LAG):
                        if s < UNITS:
                            dve.wait_ge(s_S.sem, s_S.after(i, s + 1))
                            nc.vector.tensor_reduce(negmax[:, s // HEADS, s % HEADS, :],
                                                    bank[s % SLOTS][:, 0:2 * KEYS].rearrange("p (t k) -> p t k", t=NT),
                                                    AX.X, ALU.max, negate=True).then_inc(s_nm.sem, 1)
                        u = s - ET_LAG
                        if 0 <= u < UNITS:
                            dve.wait_ge(s_ET.sem, s_ET.after(i, u + 1))
                            if u >= SLOTS:
                                dve.wait_ge(s_PV.sem, s_PV.after(i, u - SLOTS + 1))
                            ins = nc.vector.tensor_copy(ET_s[:, u % SLOTS, 0, :], bank[4 + u % 2][:, 0:N])
                            if u % SLOTS == SLOTS - 1:
                                ins = nc.vector.tensor_copy(tail_s[:, u // SLOTS % 2, :], bank[4 + u % 2][:, N:N + P])
                            ins.then_inc(s_ETs.sem, 1)
                        if s == HEADS + PV_LAG:
                            normalise(i, 0)
                    residual(i, 0)
                    normalise(i, 1)
                    residual(i, 1)
                    dve.wait_ge(s_lg.sem, s_lg.after(i))
                    logits = bank[4][:, 0:TILES * EXPERTS].rearrange("p (t e) -> p t e", e=EXPERTS)
                    link(nc.vector.tensor_reduce(gate[:, 0, :], logits, AX.X, ALU.max))
                    nc.vector.tensor_tensor(pr[:, 0, :, :], logits, gate[:, 0, :, None].broadcast_to([P, TILES, EXPERTS]),
                                            ALU.subtract).then_inc(s_sh.sem, 1)
                    dve.wait_ge(s_pe.sem, s_pe.after(i))
                    link(nc.vector.tensor_reduce(gate[:, 1, :], pr[:, 1, :, :], AX.X, ALU.add))
                    link(nc.vector.reciprocal(gate[:, 2, :], gate[:, 1, :]))
                    link(nc.vector.tensor_tensor(pr[:, 2, :, :], pr[:, 1, :, :], gate[:, 2, :, None].broadcast_to([P, TILES, EXPERTS]), ALU.mult))
                    hold(dve)
                    for t in range(TILES):
                        ins = nc.vector.max(top[:, t, :], pr[:, 2, t, :])
                    link(ins)
                    hold(dve)
                    for t in range(TILES):
                        ins = nc.vector.max_index(topi[:, t, :], top[:, t, :], pr[:, 2, t, :])
                    link(ins)
                    link(nc.vector.tensor_copy(topf[:, :, :], topi[:, :, :]))
                    for n in range(2):
                        ins = nc.vector.tensor_tensor(pr[:, 3 * n, :, :], iota8[:, None, :].broadcast_to([P, TILES, EXPERTS]),
                                                      topf[:, :, n:n + 1].broadcast_to([P, TILES, EXPERTS]), ALU.is_equal)
                        link(ins)
                    link(nc.vector.tensor_tensor(pr[:, 0, :, :], pr[:, 0, :, :], pr[:, 3, :, :], ALU.add))
                    link(nc.vector.tensor_tensor(pr[:, 3, :, :], pr[:, 0, :, :], pr[:, 2, :, :], ALU.mult))
                    nc.vector.tensor_copy(gate[:, 5, :], gate[:, 2, :]).then_inc(s_cb.sem, 1)
                    link.ended(STEPS)

            @block.gpsimd
            def _(pool):
                pool.sem_inc(s_xc.sem, s_xc.ahead)
                H = HD // 2
                with pool.Fori(0, GROUPS) as i:
                    pool.wait_ge(xs_in.sem, xs_in.after(i))
                    hold(pool)
                    for b in range(PAIR):
                        a = b * N + P - WIN
                        ins = nc.gpsimd.tensor_copy(xt_s[:, b, :].rearrange("p (j r) -> p j r", r=WIN),
                                                    xs[:, None, a:a + WIN].broadcast_to([P, SLOTS, WIN]))
                    ins.then_inc(s_xt.sem, 1)
                    pool.wait_ge(s_rms.sem, s_rms.after(i))
                    for t in range(TILES):
                        x = qk3[:, t, :].rearrange("p (c h d) -> p c h d", c=2, d=HD)
                        y = qb[:, t, :].rearrange("p (c h d) -> p c h d", c=2, d=HD)
                        s = sinw[:, t % NT, :, None, :].broadcast_to([P, 2, HEADS, HD])
                        nc.gpsimd.tensor_tensor(y[:, :, :, 0:H], x[:, :, :, H:HD], s[:, :, :, 0:H], ALU.mult)
                        ins = nc.gpsimd.tensor_tensor(y[:, :, :, H:HD], x[:, :, :, 0:H], s[:, :, :, H:HD], ALU.mult)
                    ins.then_inc(s_rot.sem, 1)
                    for n in range(UNITS // SLOTS):
                        pool.wait_ge(s_E.sem, s_E.after(i, (n + 1) * SLOTS))
                        if n >= 2:
                            pool.wait_ge(s_ET.sem, s_ET.after(i, (n - 1) * SLOTS))
                        hold(pool)
                        nc.gpsimd.tensor_copy(et_s[:, n % 2, :].rearrange("p (j r) -> p j r", r=WIN),
                                              E_s[:, n % 2, :, 1, 0:WIN]).then_inc(s_et.sem, 1)
                    pool.wait_ge(s_xTs.sem, s_xTs.after(i))
                    hold(pool)
                    nc.gpsimd.tensor_copy(XN_C[:, bass.ds(i * W, W)], xc_s[:, :]).then_inc(s_xc.sem, 1)
        attn3.close()

        a_s = sb("a_s", [P, 2, W])
        c_s = sb("c_s", [P, 2, W])
        BLOCKS = 5
        s_G, s_Up, s_si, s_m, s_c, s_Dn = (signal(n, BLOCKS) for n in ("ex_gate", "ex_up", "ex_silu", "ex_product", "ex_weighted", "ex_down"))
        s_out, s_sum = signal("out_stored", 16, True), signal("ex_sum", 1, True)
        with nc.Block() as block:
            @block.tensor
            def _(pe):
                with pe.Fori(0, GROUPS) as i:
                    pe.wait_ge(s_sum.sem, s_sum.before(i))
                    for s in range(BLOCKS + 1):
                        if s < BLOCKS:
                            m = P if s < 4 else EH
                            if s >= 2:
                                pe.wait_ge(s_m.sem, s_m.after(i, s - 1))
                            if s == 4:
                                hold(pe)
                            for to, w, done in ((bank[s % 2], Wgate[:, 2 * s:2 * s + 2, :] if s < 4 else Sgate[:, :], s_G),
                                                (bank[2 + s % 2], Wup[:, 2 * s:2 * s + 2, :] if s < 4 else Sup[:, :], s_Up)):
                                nc.tensor.matmul(to[0:m, :], w, XN_C[:, bass.ds(i * W, W)], start=True, stop=True).then_inc(done.sem, 1)
                        n = s - 1
                        if n >= 0:
                            pe.wait_ge(s_c.sem, s_c.after(i, n + 1))
                            m = P if n < 4 else EH
                            nc.tensor.matmul(bank[6][:, :], Wdown[:, n, :] if n < 4 else Sdown[:, :], c_s[0:m, n % 2, :],
                                             start=(n == 0), stop=(n == BLOCKS - 1)).then_inc(s_Dn.sem, 1)

            @block.scalar
            def _(act):
                with act.Fori(0, GROUPS) as i:
                    for n in range(BLOCKS):
                        m = P if n < 4 else EH
                        act.wait_ge(s_G.sem, s_G.after(i, n + 1))
                        if n >= 2:
                            act.wait_ge(s_m.sem, s_m.after(i, n - 1))
                        nc.scalar.activation(a_s[0:m, n % 2, :], bank[n % 2][0:m, :], ACT.Silu).then_inc(s_si.sem, 1)

            @block.vector
            def _(dve):
                dve.sem_inc(s_sum.sem, s_sum.ahead)
                with dve.Fori(0, GROUPS) as i:
                    for n in range(BLOCKS):
                        m = P if n < 4 else EH
                        dve.wait_ge(s_Up.sem, s_Up.after(i, n + 1))
                        dve.wait_ge(s_si.sem, s_si.after(i, n + 1))
                        if n >= 2:
                            dve.wait_ge(s_Dn.sem, s_Dn.after(i, n - 1))
                        nc.vector.tensor_tensor(c_s[0:m, n % 2, :], a_s[0:m, n % 2, :], bank[2 + n % 2][0:m, :],
                                                ALU.mult).then_inc(s_m.sem, 1)
                        dve.wait_ge(s_m.sem, s_m.after(i, n + 1))
                        if n < 4:
                            nc.vector.tensor_tensor(c_s[:, n % 2, :], c_s[:, n % 2, :], CB[:, bass.ds(i * 4 * W + n * W, W)],
                                                    ALU.mult).then_inc(s_c.sem, 1)
                        else:
                            dve.sem_inc(s_c.sem, 1)
                    dve.wait_ge(s_Dn.sem, s_Dn.after(i))
                    dve.wait_ge(s_out.sem, s_out.before(i))
                    nc.vector.tensor_tensor(y_s[:, :], bank[6][:, :], R_C[:, bass.ds(i * W, W)], ALU.add).then_inc(s_sum.sem, 1)

            @block.sync
            def _(sp):
                sp.sem_inc(s_out.sem, s_out.ahead)
                with sp.Fori(0, GROUPS) as i:
                    sp.wait_ge(s_sum.sem, s_sum.after(i))
                    sp.dma_start(OUT[:, bass.ds(i * PAIR, PAIR), :], y_s[:, :].rearrange("p (b n) -> p b n", n=N)).then_inc(s_out.sem, 16)
                sp.wait_ge(s_out.sem, 16 * (GROUPS + 1))


_INS = ["x", "L0_conv_Wb", "L0_conv_Wc", "L0_conv_Wd", "L0_conv_gamma", "L1_conv_W_qkv", "L1_conv_b_qkv",
        "L1_conv_W_proj", "L1_conv_b_proj", "L2_ffn_Wg", "L2_ffn_W1", "L2_ffn_b1", "L2_ffn_W2", "L2_ffn_b2",
        "L3_attn_rope_cos", "L3_attn_rope_sin", "L3_attn_W_q", "L3_attn_W_k", "L3_attn_W_v", "L3_attn_W_o",
        "L3_attn_q_norm_w", "L3_attn_k_norm_w", "L3_ffn_router", "L3_ffn_shared_gate", "L3_ffn_shared_up",
        "L3_ffn_shared_down", "L3_ffn_W_gate", "L3_ffn_W_up", "L3_ffn_W_down"]


def kernel(**inputs):
    import numpy as _np
    import concourse.bacc as _bacc
    from concourse import mybir as _mybir
    from concourse.bass_utils import run_bass_kernel_spmd as _run

    nc = _bacc.Bacc("TRN2", target_bir_lowering=False, num_devices=1)
    arrays, args = {}, {}
    for name in _INS:
        a = _np.ascontiguousarray(inputs[name])
        arrays[f"in_{name}_dram"] = a
        args[name] = nc.dram_tensor(f"in_{name}_dram", a.shape, _mybir.dt.from_np(a.dtype), kind="ExternalInput").ap()
    out = nc.dram_tensor("out_0_dram", (8, 128, 16, 16), _mybir.dt.float32, kind="ExternalOutput").ap()
    bass_conv_attn_hybrid_kernel(nc, args, out)
    r = _run(nc, [arrays], core_ids=[0])
    return r.results[0]["out_0_dram"]
```

```python
from contextlib import ExitStack

import concourse.bass as bass
from concourse import mybir
from concourse.alu_op_type import AluOpType as ALU

F32 = mybir.dt.float32
BF16 = mybir.dt.bfloat16
I32 = mybir.dt.int32
U32 = mybir.dt.uint32
ACT = mybir.ActivationFunctionType
AX = mybir.AxisListType

P = 128
IMAGES = 8
N = 256
TOKENS = IMAGES * N
GROUPS = 4
W = TOKENS // GROUPS
TILES = W // P
PAIR = W // N
NT = N // P
HEADS, HD = 8, 16
SLOTS = 4
EXPERTS = 8
FF = 512
FT = EXPERTS * FF // P
EH = 64
WIN = 32
KEYS = WIN + P
NO_KEY = -1.0e30


class Signal:

    def __init__(self, sem, per, ahead):
        self.sem, self.per, self.ahead = sem, per, per if ahead else 0

    def after(self, turn, count=None):
        return turn * self.per + self.ahead + (self.per if count is None else count)

    def before(self, turn):
        return turn * self.per + self.ahead


class Chain:

    def __init__(self, eng, sem, idle=None):
        self.eng, self.sem, self.idle, self.count, self.base = eng, sem, idle, 0, 0

    def turn(self, i, steps):
        self.base, self.count = i * steps, 0

    def __call__(self, ins):
        ins.then_inc(self.sem, 1)
        self.count += 1
        self.eng.wait_ge(self.sem, self.base + self.count)
        if self.idle is not None:
            self.eng.sem_inc(self.idle, 1)

    def ended(self, steps):
        assert self.count == steps, f"a turn has {self.count} linked steps, not {steps}"


def bass_conv_attn_hybrid_kernel(nc, A, out):
    with ExitStack() as ctx:
        def sb(name, shape, dt=F32):
            return ctx.enter_context(nc.sbuf_tensor(name, shape, dt))

        def sem(name):
            return ctx.enter_context(nc.semaphore(name))

        def signal(name, per, ahead=False):
            return Signal(sem(name), per, ahead)

        bank = [ctx.enter_context(nc.psum_tensor(f"bank{k}", [P, 512], F32)) for k in range(8)]

        R = sb("R", [P, TOKENS])
        XN_C = sb("XN_C", [P, TOKENS])
        XN_T = sb("XN_T", [P, TOKENS])
        R_C = sb("R_C", [P, TOKENS])

        ident = sb("ident", [P, P])
        ones = sb("ones", [P, P])
        identb = sb("identb", [P, P], BF16)
        bandb = sb("bandb", [P, 2, KEYS], BF16)
        band = sb("band", [P, 2, KEYS])
        groups4 = sb("groups4", [P, P])
        wraw = sb("wraw", [P, 7, P])
        WbT = sb("WbT", [P, 16])
        WcT = sb("WcT", [P, 16])
        WdT = sb("WdT", [P, P])
        Wqk1 = sb("Wqk1", [P, 2, P])
        WvT = sb("WvT", [P, P])
        Wp_raw = sb("Wp_raw", [P, 2, P])
        Wp1 = sb("Wp1", [P, 2, P])
        bqk = sb("bqk", [P, 2])
        bias_rows = sb("bias_rows", [P, P])
        bv_all = sb("bv_all", [P, P])
        bp_all = sb("bp_all", [P, P])
        gamma_all = sb("gamma_all", [P, 1])
        Wg = sb("Wg", [P, EXPERTS])
        W1 = sb("W1", [P, EXPERTS, FF])
        W2 = sb("W2", [P, FT, P])
        b1 = sb("b1", [P, FT])
        b2two = sb("b2two", [P, 1])
        Wqkv3 = sb("Wqkv3", [P, 3 * P])
        Wo3 = sb("Wo3", [P, 2, P])
        norm_w = sb("norm_w", [P, 2, HD])
        rope = sb("rope", [P, 2, NT, HD])
        cosw = sb("cosw", [P, NT, 2, HD])
        sinw = sb("sinw", [P, NT, 2, HD])
        router = sb("router", [P, EXPERTS])
        Wgate = sb("Wgate", [P, EXPERTS, EH])
        Wup = sb("Wup", [P, EXPERTS, EH])
        Wdown = sb("Wdown", [P, 4, P])
        Sgate = sb("Sgate", [P, EH])
        Sup = sb("Sup", [P, EH])
        Sdown = sb("Sdown", [EH, P])
        rows_f = sb("rows_f", [3 * EXPERTS, EXPERTS, EH])
        iota_i = sb("iota_i", [P, EXPERTS], I32)
        iota8 = sb("iota8", [P, EXPERTS])
        expert_rows = sb("expert_rows", [3 * EXPERTS, EXPERTS * EH], BF16)

        xs = sb("xs", [P, W])
        q_s = sb("q_s", [16, W])
        k_s = sb("k_s", [16, W])
        v_s = sb("v_s", [P, TILES, P])
        xT_s = sb("xT_s", [P, W])
        E_s = sb("E_s", [P, SLOTS, NT, N])
        ET_s = sb("ET_s", [P, SLOTS, 2, N])
        negmax = sb("negmax", [P, PAIR, HEADS, NT])
        rowsum = sb("rowsum", [P, PAIR, HEADS, NT])
        rinv = sb("rinv", [P, PAIR, HEADS, NT])
        o_raw = sb("o_raw", [P, 2, N])
        rx = sb("rx", [P, NT, 2, P])
        shift = sb("shift", [P, TILES])
        oT = sb("oT", [P, 2, N])
        r_s = sb("r_s", [P, W])
        xn_s = sb("xn_s", [P, W])
        xc_s = sb("xc_s", [P, W])
        stats = sb("stats", [P, TILES, 6])
        mv = sb("mv", [P, TILES, 2])
        mm_s = sb("mm_s", [P, PAIR, 2])
        gm = sb("gm", [P, PAIR, 2])
        var = sb("var", [P, 64])
        rstd = sb("rstd", [P, 64])
        ntmp = sb("ntmp", [P, 64])
        top = sb("top", [P, TILES, 8])
        gate = sb("gate", [P, 6, TILES])
        y_s = sb("y_s", [P, W])
        idle = sem("idle")

        X = A["x"].rearrange("b c h w -> c b (h w)")
        OUT = out.rearrange("b c h w -> c b (h w)")

        def hold(eng):
            eng.sem_inc(idle, 1)

        def rsqrt(on, link, a, n, fused=True):
            y, v, t = rstd[:, a:a + n], var[:, a:a + n], ntmp[:, a:a + n]
            link(on.tensor_scalar(y.bitcast(I32), v.bitcast(I32), -0.5, float(0x5F3759DF), ALU.mult, ALU.add))
            for _ in range(3):
                link(on.tensor_tensor(t, y, y, ALU.mult))
                if fused:
                    link(on.scalar_tensor_tensor(t, t, -0.5, v, ALU.mult, ALU.mult))
                    link(on.scalar_tensor_tensor(y, t, 1.5, y, ALU.add, ALU.mult))
                else:
                    link(on.tensor_tensor(t, t, v, ALU.mult))
                    link(on.tensor_scalar(t, t, -0.5, 1.5, ALU.mult, ALU.add))
                    link(on.tensor_tensor(y, t, y, ALU.mult))

        RSQRT, RSQRT_POOL = 10, 13

        def token_norm(dve, link, eps, tiles, done):
            a, n = tiles[0], len(tiles)
            for t in tiles:
                ins = nc.vector.bn_stats(stats[:, t, :], r_s[:, t * P:(t + 1) * P])
            link(ins)
            hold(dve)
            for t in tiles:
                ins = nc.vector.bn_aggr(mv[:, t, :], stats[:, t, :])
            link(ins)
            link(nc.vector.tensor_scalar(var[:, 0:n], mv[:, a:a + n, 1], eps, None, ALU.add))
            rsqrt(nc.vector, link, 0, n)
            for t in tiles:
                ins = nc.vector.tensor_scalar(xn_s[:, t * P:(t + 1) * P], r_s[:, t * P:(t + 1) * P],
                                              mv[:, t, 0:1], rstd[:, t - a:t - a + 1], ALU.subtract, ALU.mult)
            ins.then_inc(done.sem, 1)

        NORM = 3 + RSQRT

        w_raw, w_c, w_l2, w_l3, w_pads = (sem(n) for n in (
            "w_raw_loaded", "w_conv_loaded", "w_layer2_loaded", "w_layer3_loaded", "pads_zero"))
        s_ident, s_wT, s_prep = sem("ident_ready"), sem("weights_turned"), sem("prep_steps")
        s_prep_p, s_zero, s_wp = sem("pool_prep_steps"), sem("raw_rows_zero"), sem("proj_columns_placed")
        with nc.Block() as block:
            @block.sync
            def _(sp):
                sp.wait_ge(s_zero, 2)
                sp.dma_start(wraw[0:16, 0, :], A["L0_conv_Wb"]).then_inc(w_raw, 16)
                sp.dma_start(wraw[32:48, 0, :], A["L0_conv_Wc"]).then_inc(w_raw, 16)
                sp.dma_start(wraw[:, 1, :], A["L0_conv_Wd"]).then_inc(w_raw, 16)
                sp.dma_start(wraw[:, 2:5, :], A["L1_conv_W_qkv"].rearrange("(k o) c -> o k c", k=3)).then_inc(w_raw, 16)
                sp.dma_start(wraw[:, 5, :], A["L1_conv_W_proj"]).then_inc(w_raw, 16)
                sp.dma_start(wraw[0:FT, 6, :], A["L2_ffn_b1"].rearrange("e (q f) -> (e q) f", f=P)).then_inc(w_raw, 16)
                sp.dma_start(wraw[32:32 + EXPERTS, 6, :], A["L2_ffn_b2"]).then_inc(w_raw, 16)
                for kind in range(2):
                    sp.dma_start(wraw[64 + kind:65 + kind, 6, :], A["L1_conv_b_qkv"][None, kind * P:(kind + 1) * P]).then_inc(w_raw, 16)
                sp.dma_start(gamma_all[:, :], A["L0_conv_gamma"][None, :].broadcast_to([P, 1])).then_inc(w_c, 16)
                sp.dma_start(bv_all[:, :], A["L1_conv_b_qkv"][None, 2 * P:3 * P].broadcast_to([P, P])).then_inc(w_c, 16)
                sp.dma_start(bp_all[:, :], A["L1_conv_b_proj"][None, :].broadcast_to([P, P])).then_inc(w_c, 16)
                sp.wait_ge(w_pads, 1)
                sp.dma_start(rope[:, 0, :, :], A["L3_attn_rope_cos"][0:N, :].rearrange("(t p) d -> p t d", p=P)).then_inc(w_l3, 16)
                sp.dma_start(rope[:, 1, :, :], A["L3_attn_rope_sin"][0:N, :].rearrange("(t p) d -> p t d", p=P)).then_inc(w_l3, 16)
                sp.dma_start(norm_w[:, 0, :], A["L3_attn_q_norm_w"][None, :].broadcast_to([P, HD])).then_inc(w_l3, 16)
                sp.dma_start(norm_w[:, 1, :], A["L3_attn_k_norm_w"][None, :].broadcast_to([P, HD])).then_inc(w_l3, 16)
                sp.dma_start(Wg[:, :], A["L2_ffn_Wg"]).then_inc(w_l2, 16)
                sp.dma_start(W1[:, :, :], A["L2_ffn_W1"].rearrange("e d f -> d e f")).then_inc(w_l2, 16)
                sp.dma_start(W2[:, :, :], A["L2_ffn_W2"].rearrange("e (q f) c -> f (e q) c", f=P)).then_inc(w_l2, 16)
                for n, name in enumerate(("L3_attn_W_q", "L3_attn_W_k", "L3_attn_W_v")):
                    sp.dma_start(Wqkv3[:, n * P:(n + 1) * P], A[name]).then_inc(w_l2, 16)
                for h in range(HEADS):
                    sp.dma_start(Wo3[32 * (h % SLOTS):32 * (h % SLOTS) + HD, h // SLOTS, :],
                                 A["L3_attn_W_o"][h * HD:(h + 1) * HD, :]).then_inc(w_l2, 16)
                sp.dma_start(router[:, :], A["L3_ffn_router"]).then_inc(w_l2, 16)
                sp.dma_start(Wgate[:, :, :], A["L3_ffn_W_gate"].rearrange("e d f -> d e f")).then_inc(w_l2, 16)
                sp.dma_start(Wup[:, :, :], A["L3_ffn_W_up"].rearrange("e d f -> d e f")).then_inc(w_l2, 16)
                sp.dma_start(Wdown[:, :, :], A["L3_ffn_W_down"].rearrange("(q e) f c -> (e f) q c", e=2)).then_inc(w_l2, 16)
                sp.dma_start(Sgate[:, :], A["L3_ffn_shared_gate"]).then_inc(w_l2, 16)
                sp.dma_start(Sup[:, :], A["L3_ffn_shared_up"]).then_inc(w_l2, 16)
                sp.dma_start(Sdown[:, :], A["L3_ffn_shared_down"]).then_inc(w_l2, 16)

            @block.gpsimd
            def _(pool):
                link = Chain(pool, s_prep_p)
                nc.gpsimd.memset(wraw[:, 0, :], 0.0).then_inc(s_zero, 1)
                nc.gpsimd.memset(wraw[:, 6, :], 0.0).then_inc(s_zero, 1)
                link(nc.gpsimd.memset(ones[:, :], 1.0))
                nc.gpsimd.affine_select(out=ident[:, :], in_=ones[:, :], compare_op=ALU.is_equal, fill=0.0,
                                        base=0, pattern=[[-1, P]], channel_multiplier=1).then_inc(s_ident, 1)
                link(nc.gpsimd.memset(groups4[:, :], 0.25))
                v = groups4[:, :].rearrange("p (g d) -> p g d", d=4)
                link(nc.gpsimd.affine_select(out=v, in_=v, compare_op=ALU.is_ge, fill=0.0, base=0,
                                             pattern=[[-4, P // 4], [0, 4]], channel_multiplier=1))
                link(nc.gpsimd.affine_select(out=v, in_=v, compare_op=ALU.is_ge, fill=0.0, base=3,
                                             pattern=[[4, P // 4], [0, 4]], channel_multiplier=-1))
                link(nc.gpsimd.memset(band[:, :, :], 0.0))
                link(nc.gpsimd.affine_select(out=band[:, :, :], in_=band[:, :, :], compare_op=ALU.is_ge, fill=NO_KEY,
                                             base=WIN, pattern=[[0, 2], [-1, KEYS]], channel_multiplier=1))
                link(nc.gpsimd.affine_select(out=band[:, :, :], in_=band[:, :, :], compare_op=ALU.is_gt, fill=NO_KEY,
                                             base=0, pattern=[[0, 2], [1, KEYS]], channel_multiplier=-1))
                link(nc.gpsimd.memset(band[:, 0, 0:WIN], NO_KEY))
                link(nc.gpsimd.tensor_copy(bandb[:, :, :], band[:, :, :]))
                link(nc.gpsimd.tensor_copy(identb[:, :], ident[:, :]))
                link(nc.gpsimd.memset(rows_f[:, :, :], 0.0))
                for part in range(3):
                    link(nc.gpsimd.affine_select(out=rows_f[:, :, :], in_=rows_f[:, :, :], compare_op=ALU.not_equal, fill=1.0,
                                                 base=-part * EXPERTS, pattern=[[-1, EXPERTS], [0, EH]], channel_multiplier=1))
                link(nc.gpsimd.tensor_copy(expert_rows[:, :], rows_f[:, :, :].rearrange("p e f -> p (e f)")))
                link(nc.gpsimd.iota(iota_i[:, :], pattern=[[1, EXPERTS]], base=0, channel_multiplier=0))
                link(nc.gpsimd.tensor_copy(iota8[:, :], iota_i[:, :]))

            @block.tensor
            def _(pe):
                pe.wait_ge(s_ident, 1)
                pe.wait_ge(w_raw, 9 * 16)
                pe.wait_ge(s_zero, 2)
                for n in range(5):
                    nc.tensor.transpose(bank[n][:, 0:P], wraw[:, n, :], ident[:, :]).then_inc(s_wT, 1)
                nc.tensor.transpose(bank[6][:, 0:P], wraw[:, 6, :], ident[:, :]).then_inc(s_wT, 1)
                pe.wait_ge(s_wp, 1)
                nc.tensor.transpose(bank[6][:, P:2 * P], bias_rows[:, :], ident[:, :]).then_inc(s_wT, 1)
                for half in range(2):
                    nc.tensor.transpose(bank[5][:, half * P:(half + 1) * P], Wp_raw[:, half, :], ident[:, :]).then_inc(s_wT, 1)

            @block.vector
            def _(dve):
                link = Chain(dve, s_prep)
                nc.vector.memset(Wo3[:, :, :], 0.0).then_inc(w_pads, 1)
                link(nc.vector.memset(Wp_raw[:, :, :], 0.0))
                dve.wait_ge(w_raw, 9 * 16)
                link(nc.vector.tensor_copy(bias_rows[:, :].rearrange("p (d h) -> p h d", h=HEADS),
                                           wraw[:, 6, :].rearrange("p (h d) -> p h d", d=HD)))
                nc.vector.tensor_copy(Wp_raw[:, :, :].rearrange("p f (j r) -> p (f j) r", r=32)[:, :, 0:HD],
                                      wraw[:, 5, :].rearrange("p (g d) -> p g d", d=HD)).then_inc(s_wp, 1)
                dve.wait_ge(s_wT, 9)
                nc.vector.tensor_copy(WbT[:, :], bank[0][:, 0:16])
                nc.vector.tensor_copy(WcT[:, :], bank[0][:, 32:48])
                nc.vector.tensor_copy(WdT[:, :], bank[1][:, 0:P])
                for kind in range(2):
                    nc.vector.tensor_copy(Wqk1[:, kind, :].rearrange("p (d h) -> p h d", h=HEADS),
                                          bank[2 + kind][:, 0:P].rearrange("p (h d) -> p h d", d=HD))
                nc.vector.tensor_copy(WvT[:, :], bank[4][:, 0:P])
                nc.vector.tensor_copy(Wp1[:, :, :].rearrange("p f c -> p (f c)"), bank[5][:, 0:2 * P])
                nc.vector.tensor_copy(b1[:, :], bank[6][:, 0:FT])
                nc.vector.tensor_scalar(bqk[:, 0:1], bank[6][:, P + 64:P + 65], HD ** -0.5, None, ALU.mult)
                nc.vector.tensor_copy(bqk[:, 1:2], bank[6][:, P + 65:P + 66])
                link(nc.vector.tensor_reduce(b2two[:, :], bank[6][:, FT:FT + EXPERTS], AX.X, ALU.add))
                link(nc.vector.tensor_scalar(b2two[:, :], b2two[:, :], 2.0, None, ALU.mult))
                dve.wait_ge(w_l3, 4 * 16)
                link(nc.vector.tensor_scalar(norm_w[:, 0, :], norm_w[:, 0, :], HD ** -0.5, None, ALU.mult))
                H = HD // 2
                for t in range(NT):
                    for kind in range(2):
                        nc.vector.tensor_tensor(cosw[:, t, kind, :], rope[:, 0, t, :], norm_w[:, kind, :], ALU.mult)
                        nc.vector.scalar_tensor_tensor(sinw[:, t, kind, 0:H], rope[:, 1, t, 0:H], -1.0,
                                                       norm_w[:, kind, H:HD], ALU.mult, ALU.mult)
                        nc.vector.tensor_tensor(sinw[:, t, kind, H:HD], rope[:, 1, t, H:HD], norm_w[:, kind, 0:H], ALU.mult)

        x_in = signal("l0_x_in", 16)
        ps_x, ps_q, ps_d = signal("l0_xT", 1), signal("l0_qk", 2), signal("l0_d", 1, True)
        a_st = signal("l0_stored", 4)
        s_S, s_nm, s_E = signal("l0_scores", 2), signal("l0_negmax", 2), signal("l0_exp", 4)
        s_ET, s_ETs, s_O = signal("l0_ET", 2), signal("l0_ET_stored", 2), signal("l0_O", 2)
        s_r, s_rc, s_mm, s_gm, s_done = (signal("l0_r", 1), signal("l0_r_c", 1), signal("l0_moments", 1),
                                         signal("l0_group_moments", 1), signal("l0_done", 1, True))
        s_link = sem("l0_steps")
        with nc.Block() as block:
            @block.sync
            def _(sp):
                with sp.Fori(0, GROUPS) as i:
                    sp.wait_ge(ps_d.sem, ps_d.before(i))
                    sp.dma_start(xs[:, :].rearrange("p (b n) -> p b n", n=N), X[:, bass.ds(i * PAIR, PAIR), :]).then_inc(x_in.sem, 16)

            @block.tensor
            def _(pe):
                pe.sem_inc(ps_d.sem, ps_d.ahead)
                with pe.Fori(0, GROUPS) as i:
                    pe.wait_ge(x_in.sem, x_in.after(i))
                    pe.wait_ge(s_done.sem, s_done.before(i))
                    for t in range(TILES):
                        ins = nc.tensor.transpose(bank[0][:, t * P:(t + 1) * P], xs[:, t * P:(t + 1) * P], ident[:, :])
                    ins.then_inc(ps_x.sem, 1)
                    nc.tensor.matmul(bank[1][0:16, :], WbT[:, :], xs[:, :], start=True, stop=True).then_inc(ps_q.sem, 1)
                    nc.tensor.matmul(bank[2][0:16, :], WcT[:, :], xs[:, :], start=True, stop=True).then_inc(ps_q.sem, 1)
                    for t in range(TILES):
                        ins = nc.tensor.matmul(bank[3][:, t * P:(t + 1) * P], xs[:, t * P:(t + 1) * P], WdT[:, :],
                                               start=True, stop=True)
                    ins.then_inc(ps_d.sem, 1)
                    ins = None
                    pe.wait_ge(a_st.sem, a_st.after(i, 3))
                    for b in range(PAIR):
                        for t in range(NT):
                            a = b * N + t * P
                            ins = nc.tensor.matmul(bank[4 + b][:, t * N:(t + 1) * N], q_s[:, a:a + P],
                                                   k_s[:, b * N:(b + 1) * N], start=True, stop=True)
                        ins.then_inc(s_S.sem, 1)
                    for b in range(PAIR):
                        pe.wait_ge(s_E.sem, s_E.after(i, 2 * b + 2))
                        for t in range(NT):
                            for kt in range(NT):
                                ins = nc.tensor.transpose(bank[6 + b][:, kt * N + t * P:kt * N + (t + 1) * P],
                                                          E_s[:, b, t, kt * P:(kt + 1) * P], ident[:, :])
                        ins.then_inc(s_ET.sem, 1)
                    pe.wait_ge(a_st.sem, a_st.after(i, 4))
                    for b in range(PAIR):
                        pe.wait_ge(s_ETs.sem, s_ETs.after(i, b + 1))
                        for t in range(NT):
                            for kt in range(NT):
                                ins = nc.tensor.matmul(bank[b][:, t * P:(t + 1) * P],
                                                       ET_s[:, b, kt, t * P:(t + 1) * P], v_s[:, b * NT + kt, :],
                                                       start=(kt == 0), stop=(kt == NT - 1))
                        ins.then_inc(s_O.sem, 1)
                    pe.wait_ge(s_r.sem, s_r.after(i))
                    for t in range(TILES):
                        ins = nc.tensor.transpose(bank[2][:, t * P:(t + 1) * P], r_s[:, t * P:(t + 1) * P], ident[:, :])
                    ins.then_inc(s_rc.sem, 1)
                    pe.wait_ge(s_mm.sem, s_mm.after(i))
                    nc.tensor.matmul(bank[3][:, 0:2 * PAIR], groups4[:, :], mm_s[:, :, :].rearrange("p b m -> p (b m)"),
                                     start=True, stop=True).then_inc(s_gm.sem, 1)

            @block.scalar
            def _(act):
                with act.Fori(0, GROUPS) as i:
                    act.wait_ge(ps_x.sem, ps_x.after(i))
                    act.wait_ge(s_done.sem, s_done.before(i))
                    nc.scalar.copy(xT_s[:, :], bank[0][:, :]).then_inc(a_st.sem, 1)
                    act.wait_ge(ps_q.sem, ps_q.after(i, 1))
                    nc.scalar.copy(q_s[:, :], bank[1][0:16, :]).then_inc(a_st.sem, 1)
                    act.wait_ge(ps_q.sem, ps_q.after(i, 2))
                    nc.scalar.copy(k_s[:, :], bank[2][0:16, :]).then_inc(a_st.sem, 1)
                    act.wait_ge(ps_d.sem, ps_d.after(i))
                    nc.scalar.copy(v_s[:, :, :].rearrange("p t c -> p (t c)"), bank[3][:, :]).then_inc(a_st.sem, 1)
                    for b in range(PAIR):
                        act.wait_ge(s_nm.sem, s_nm.after(i, b + 1))
                        for t in range(NT):
                            nc.scalar.activation(E_s[:, b, t, 0:N], bank[4 + b][:, t * N:(t + 1) * N], ACT.Exp,
                                                 bias=negmax[:, b, 0, t:t + 1],
                                                 accum_out=rowsum[:, b, 0, t:t + 1]).then_inc(s_E.sem, 1)

            @block.vector
            def _(dve):
                link = Chain(dve, s_link)
                STEPS = 9 + RSQRT
                dve.sem_inc(s_done.sem, s_done.ahead)
                with dve.Fori(0, GROUPS) as i:
                    link.turn(i, STEPS)
                    for b in range(PAIR):
                        dve.wait_ge(s_S.sem, s_S.after(i, b + 1))
                        nc.vector.tensor_reduce(negmax[:, b, 0, :], bank[4 + b][:, :].rearrange("p (t k) -> p t k", t=NT),
                                                AX.X, ALU.max, negate=True).then_inc(s_nm.sem, 1)
                    for b in range(PAIR):
                        dve.wait_ge(s_ET.sem, s_ET.after(i, b + 1))
                        nc.vector.tensor_copy(ET_s[:, b, :, :].rearrange("p k n -> p (k n)"), bank[6 + b][:, :]).then_inc(s_ETs.sem, 1)
                    dve.wait_ge(s_E.sem, s_E.after(i))
                    link(nc.vector.reciprocal(rinv[:, :, 0, :], rowsum[:, :, 0, :]))
                    link(nc.vector.tensor_scalar(rinv[:, :, 0, :], rinv[:, :, 0, :], gamma_all[:, :], None, ALU.mult))
                    for b in range(PAIR):
                        dve.wait_ge(s_O.sem, s_O.after(i, b + 1))
                        for t in range(NT):
                            a = (b * NT + t) * P
                            ins = nc.vector.scalar_tensor_tensor(r_s[:, a:a + P], bank[b][:, t * P:(t + 1) * P],
                                                                 rinv[:, b, 0, t:t + 1], xT_s[:, a:a + P], ALU.mult, ALU.add)
                    ins.then_inc(s_r.sem, 1)
                    dve.wait_ge(s_r.sem, s_r.after(i))
                    link(nc.vector.tensor_tensor(R[:, bass.ds(i * W, W)].rearrange("p (t c) -> p t c", c=P),
                                                 r_s[:, :].rearrange("p (t c) -> p t c", c=P),
                                                 bp_all[:, None, :].broadcast_to([P, TILES, P]), ALU.add))
                    dve.wait_ge(s_rc.sem, s_rc.after(i))
                    for b in range(PAIR):
                        ins = nc.vector.bn_stats(stats[:, b, :], bank[2][:, b * N:(b + 1) * N])
                    link(ins)
                    hold(dve)
                    for b in range(PAIR):
                        ins = nc.vector.bn_aggr(mm_s[:, b, :], stats[:, b, :])
                    link(ins)
                    link(nc.vector.tensor_tensor(ntmp[:, 0:PAIR], mm_s[:, :, 0], mm_s[:, :, 0], ALU.mult))
                    nc.vector.tensor_tensor(mm_s[:, :, 1], mm_s[:, :, 1], ntmp[:, 0:PAIR], ALU.add).then_inc(s_mm.sem, 1)
                    dve.wait_ge(s_gm.sem, s_gm.after(i))
                    link(nc.vector.tensor_copy(gm[:, :, :].rearrange("p b m -> p (b m)"), bank[3][:, 0:2 * PAIR]))
                    link(nc.vector.tensor_tensor(ntmp[:, 0:PAIR], gm[:, :, 0], gm[:, :, 0], ALU.mult))
                    link(nc.vector.scalar_tensor_tensor(var[:, 0:PAIR], gm[:, :, 1], 1e-5, ntmp[:, 0:PAIR],
                                                        ALU.add, ALU.subtract))
                    rsqrt(nc.vector, link, 0, PAIR)
                    for b in range(PAIR):
                        ins = nc.vector.tensor_scalar(XN_C[:, bass.ds(i * W + b * N, N)], bank[2][:, b * N:(b + 1) * N],
                                                      gm[:, b, 0:1], rstd[:, b:b + 1], ALU.subtract, ALU.mult)
                    ins.then_inc(s_done.sem, 1)
                    link.ended(STEPS)

        PARTS = 3
        BLOCKS_Q = (0, 0, 0, 1, 1, 1, 2, 2)
        BLOCKS_K = (0, 1, 2, 0, 1, 2, 0, 1)
        STACK_DMAS = len(BLOCKS_Q) + 3
        qk_dram = nc.dram_tensor("qk_parts", (IMAGES, 2, PARTS, P, N), BF16, kind="Internal").ap()
        vall = ctx.enter_context(nc.sbuf_tensor("vall", [P, TOKENS], F32))
        v_pad = ctx.enter_context(nc.sbuf_tensor("v_pad", [P, PAIR, NT, HEADS, 32], F32))
        stack = ctx.enter_context(nc.sbuf_tensor("stack", [P, PAIR, 2, HEADS, N], BF16))

        prep1 = ctx.enter_context(ExitStack())
        xs2 = prep1.enter_context(nc.sbuf_tensor("xs2", [P, 2, W], F32))
        qk_f = prep1.enter_context(nc.sbuf_tensor("qk_f", [P, 2, 2, W], F32))
        parts = prep1.enter_context(nc.sbuf_tensor("parts", [P, 2, PARTS, 2, W], BF16))

        def write_parts(sp, parts, g, b, part, done):
            for kind in range(2):
                sp.dma_start(qk_dram[bass.ds(g * PAIR, PAIR), kind, part, :, :].rearrange("b p n -> p b n"),
                             parts[:, b, part, kind, :].rearrange("p (b n) -> p b n", n=N)).then_inc(done.sem, 16)

        def read_stack(sp, image, b, done):
            rows = [qk_dram[image, kind, :, :, :].rearrange("o a (d h) n -> (o a d) (h n)", h=HEADS) for kind in range(2)]
            for n, part in enumerate(BLOCKS_Q):
                sp.dma_start(stack[n * HD:(n + 1) * HD, b, 0, :, :].rearrange("p h n -> p (h n)"),
                             rows[0][part * HD:(part + 1) * HD, :]).then_inc(done.sem, 16)
            for n, count in ((0, 3), (3, 3), (6, 2)):
                sp.dma_start(stack[n * HD:(n + count) * HD, b, 1, :, :].rearrange("p h n -> p (h n)"),
                             rows[1][0:count * HD, :]).then_inc(done.sem, 16)

        xs_in = [signal(f"l1_xs_in{b}", 16) for b in range(2)]
        p_q, p_v, a_qk, v_st = signal("l1_qk", 2 * 2), signal("l1_v", 2, True), signal("l1_qk_stored", 2, True), signal("l1_v_stored", 2, True)
        s_c1, s_r1, s_c2, s_c3 = (signal("l1_part1", 2), signal("l1_rest1", 2), signal("l1_part2", 2),
                                  signal("l1_part3", 2, True))
        s_out = [signal(f"l1_parts_in_dram{b}", 6 * 16, True) for b in range(2)]
        s_vpad = sem("v_pads_set")
        qk_in = [signal(f"l1_stack_in{b}", STACK_DMAS * 16) for b in range(PAIR)]
        with nc.Block() as block:
            @block.sync
            def _(sp):
                for b in range(2):
                    sp.sem_inc(s_out[b].sem, s_out[b].ahead)
                for i in range(GROUPS // 2):
                    for b in range(2):
                        sp.wait_ge(p_v.sem, p_v.after(i, b - 1))
                        sp.dma_start(xs2[:, b, :], XN_C[:, bass.ds((i * 2 + b) * W, W)]).then_inc(xs_in[b].sem, 16)
                    if i == 1:
                        sp.wait_ge(s_out[0].sem, s_out[0].after(0))
                        read_stack(sp, bass.ds(0, 1), 0, qk_in[0])
                    for b in range(2):
                        sp.wait_ge(s_c1.sem, s_c1.after(i, b + 1))
                        write_parts(sp, parts, i * 2 + b, b, 0, s_out[b])
                        sp.wait_ge(s_c2.sem, s_c2.after(i, b + 1))
                        write_parts(sp, parts, i * 2 + b, b, 1, s_out[b])
                        sp.wait_ge(s_c3.sem, s_c3.after(i, b + 1))
                        write_parts(sp, parts, i * 2 + b, b, 2, s_out[b])
                for b in range(2):
                    sp.wait_ge(s_out[b].sem, s_out[b].after(GROUPS // 2 - 1))

            @block.tensor
            def _(pe):
                pe.sem_inc(p_v.sem, p_v.ahead)
                with pe.Fori(0, GROUPS // 2) as i:
                    for b in range(2):
                        pe.wait_ge(xs_in[b].sem, xs_in[b].after(i))
                        pe.wait_ge(a_qk.sem, a_qk.after(i, b - 1))
                        for kind in range(2):
                            nc.tensor.matmul(bank[3 * b + kind][:, :], Wqk1[:, kind, :], xs2[:, b, :],
                                             start=True, stop=True).then_inc(p_q.sem, 1)
                        pe.wait_ge(v_st.sem, v_st.after(i, b - 1))
                        for t in range(TILES):
                            ins = nc.tensor.matmul(bank[3 * b + 2][:, t * P:(t + 1) * P], xs2[:, b, t * P:(t + 1) * P],
                                                   WvT[:, :], start=True, stop=True)
                        ins.then_inc(p_v.sem, 1)

            @block.scalar
            def _(act):
                act.sem_inc(a_qk.sem, a_qk.ahead)
                with act.Fori(0, GROUPS // 2) as i:
                    for b in range(2):
                        act.wait_ge(s_c3.sem, s_c3.after(i, b - 1))
                        for kind in range(2):
                            act.wait_ge(p_q.sem, p_q.after(i, 2 * b + kind + 1))
                            ins = nc.scalar.activation(qk_f[:, b, kind, :], bank[3 * b + kind][:, :], ACT.Identity,
                                                       bias=bqk[:, kind:kind + 1], scale=HD ** -0.5 if kind == 0 else 1.0)
                        ins.then_inc(a_qk.sem, 1)
                        act.wait_ge(s_out[b].sem, s_out[b].before(i))
                        act.wait_ge(a_qk.sem, a_qk.after(i, b + 1))
                        nc.scalar.copy(parts[:, b, 0, :, :], qk_f[:, b, :, :]).then_inc(s_c1.sem, 1)
                    for b in range(2):
                        act.wait_ge(s_r1.sem, s_r1.after(i, b + 1))
                        nc.scalar.copy(parts[:, b, 1, :, :], qk_f[:, b, :, :]).then_inc(s_c2.sem, 1)

            @block.vector
            def _(dve):
                dve.sem_inc(s_c3.sem, s_c3.ahead)
                dve.sem_inc(v_st.sem, v_st.ahead)
                with dve.Fori(0, GROUPS // 2) as i:
                    for b in range(2):
                        dve.wait_ge(p_v.sem, p_v.after(i, b + 1))
                        nc.vector.tensor_tensor(vall[:, bass.ds((i * 2 + b) * W, W)].rearrange("p (t c) -> p t c", c=P),
                                                bank[3 * b + 2][:, :].rearrange("p (t c) -> p t c", c=P),
                                                bv_all[:, None, :].broadcast_to([P, TILES, P]), ALU.add).then_inc(v_st.sem, 1)
                        dve.wait_ge(s_c1.sem, s_c1.after(i, b + 1))
                        nc.vector.tensor_tensor(qk_f[:, b, :, :], qk_f[:, b, :, :], parts[:, b, 0, :, :], ALU.subtract).then_inc(s_r1.sem, 1)
                    for b in range(2):
                        dve.wait_ge(s_c2.sem, s_c2.after(i, b + 1))
                        nc.vector.tensor_tensor(parts[:, b, 2, :, :], qk_f[:, b, :, :], parts[:, b, 1, :, :], ALU.subtract).then_inc(s_c3.sem, 1)

            @block.gpsimd
            def _(pool):
                nc.gpsimd.memset(v_pad[:, :, :, :, :], 0.0).then_inc(s_vpad, 1)
                pool.wait_ge(s_vpad, 1)
        prep1.close()

        UNITS = PAIR * HEADS
        ET_LAG, PV_LAG = 2, 3

        def exists(i, n):
            return n >= 0 or not (isinstance(i, int) and i == 0)

        STORE, SPREAD, SCALE, PROJECT, ADD, NORMALISE, TURN, KEEP = 3, 6, 7, 0, 1, 4, 5, 6

        def all_turns(eng, steps):
            for s in range(UNITS):
                steps(0, s, True)
            with eng.Fori(1, GROUPS) as i:
                for s in range(UNITS):
                    steps(i, s, True)
            for s in range(HEADS + KEEP + 1):
                steps(GROUPS, s, False)

        def attention(name, windowed, Wp, qk_in):
            s_v = signal(name + "_v_padded", PAIR)
            s_S, s_nm, s_E = signal(name + "_scores", UNITS, True), signal(name + "_negmax", UNITS), signal(name + "_exp", UNITS)
            s_ET, s_ETs, s_PV = signal(name + "_ET", UNITS), signal(name + "_ET_stored", UNITS), signal(name + "_PV", UNITS, True)
            s_o, s_rx, s_rT, s_oT, s_y = (signal(name + "_o", PAIR), signal(name + "_rinv_spread", PAIR), signal(name + "_rinvT", PAIR),
                                          signal(name + "_oT", PAIR), signal(name + "_y", PAIR))
            s_ri, s_mv, s_rs = signal(name + "_rinv", PAIR), signal(name + "_moments", PAIR), signal(name + "_rstd", PAIR)
            s_xn, s_xT, s_kept, s_done = (signal(name + "_xn", PAIR), signal(name + "_xnT", PAIR), signal(name + "_xn_kept", PAIR, True),
                                          signal(name + "_done", PAIR))
            s_link, s_link_p = sem(name + "_steps"), sem(name + "_pool_steps")

            width = 2 * (KEYS if windowed else N)
            turned = 3 * P if windowed else 2 * N
            Ew = E_s[:, :, :, :].rearrange("p j t n -> p j (t n)")[:, :, 0:P + KEYS]
            with nc.Block() as block:
                @block.sync
                def _(sp):
                    read_stack(sp, bass.ds(1, 1), 1, qk_in[1])
                    with sp.Fori(1, GROUPS) as i:
                        for b in range(PAIR):
                            sp.wait_ge(s_S.sem, s_S.after(i, (b - 1) * HEADS))
                            read_stack(sp, bass.ds(i * PAIR + b, 1), b, qk_in[b])

                @block.tensor
                def _(pe):
                    pe.sem_inc(s_S.sem, s_S.ahead)
                    pe.sem_inc(s_PV.sem, s_PV.ahead)

                    def scores(i, u):
                        b, h, j = u // HEADS % PAIR, u % HEADS, u % SLOTS
                        if h == 0:
                            pe.wait_ge(qk_in[b].sem, qk_in[b].after(i))
                        if exists(i, u - SLOTS):
                            pe.wait_ge(s_E.sem, s_E.after(i, u - SLOTS + 1))
                        q, k = stack[:, b, 0, h, :], stack[:, b, 1, h, :]
                        if windowed:
                            nc.tensor.matmul(bank[j][:, 0:2 * KEYS], identb[:, :], bandb[:, :, :].rearrange("p t s -> p (t s)"),
                                             start=True, stop=False, skip_group_check=True)
                            nc.tensor.matmul(bank[j][:, WIN:KEYS], q[:, 0:P], k[:, 0:P],
                                             start=False, stop=False, skip_group_check=True)
                            nc.tensor.matmul(bank[j][:, KEYS:2 * KEYS], q[:, P:N], k[:, P - WIN:N],
                                             start=False, stop=True, skip_group_check=True).then_inc(s_S.sem, 1)
                        else:
                            for t in range(NT):
                                ins = nc.tensor.matmul(bank[j][:, t * N:(t + 1) * N], q[:, t * P:(t + 1) * P], k,
                                                       start=True, stop=True)
                            ins.then_inc(s_S.sem, 1)

                    def turn_exp(i, u):
                        pe.wait_ge(s_E.sem, s_E.after(i, u + 1))
                        if exists(i, u - 2):
                            pe.wait_ge(s_ETs.sem, s_ETs.after(i, u - 1))
                        if windowed:
                            for n, a in enumerate((0, P + WIN, WIN)):
                                ins = nc.tensor.transpose(bank[4 + u % 2][:, n * P:(n + 1) * P],
                                                          Ew[:, u % SLOTS, a:a + P], ident[:, :])
                        else:
                            for t in range(NT):
                                for kt in range(NT):
                                    ins = nc.tensor.transpose(bank[4 + u % 2][:, kt * N + t * P:kt * N + (t + 1) * P],
                                                              E_s[:, u % SLOTS, t, kt * P:(kt + 1) * P], ident[:, :])
                        ins.then_inc(s_ET.sem, 1)

                    def values(i, u):
                        image, b, h = u // HEADS, u // HEADS % PAIR, u % HEADS
                        pe.wait_ge(s_ETs.sem, s_ETs.after(i, u + 1))
                        if h == 0:
                            pe.wait_ge(s_v.sem, s_v.after(i, image + 1))
                            if exists(i, image - 1):
                                pe.wait_ge(s_o.sem, s_o.after(i, image))
                        rows, at = slice(32 * (h % SLOTS), 32 * (h % SLOTS) + 32), h // SLOTS * N
                        if windowed:
                            for t in range(NT):
                                nc.tensor.matmul(bank[6][rows, at + t * P:at + (t + 1) * P], v_pad[:, b, t, h, :],
                                                 ET_s[:, u % SLOTS, 0, t * P:(t + 1) * P], start=True, stop=(t == 0),
                                                 skip_group_check=True)
                            nc.tensor.matmul(bank[6][rows, at + P:at + N], v_pad[P - WIN:P, b, 0, h, :],
                                             ET_s[P - WIN:P, u % SLOTS, 1, 0:P], start=False, stop=True,
                                             skip_group_check=True).then_inc(s_PV.sem, 1)
                        else:
                            for kt in range(NT):
                                ins = nc.tensor.matmul(bank[6][rows, at:at + N], v_pad[:, b, kt, h, :],
                                                       ET_s[:, u % SLOTS, kt, :], start=(kt == 0), stop=(kt == NT - 1))
                            ins.then_inc(s_PV.sem, 1)

                    def steps(i, s, new):
                        r, image = s % HEADS, s // HEADS - 1
                        if new:
                            scores(i, s)
                        if exists(i, s - ET_LAG) and (new or s < ET_LAG):
                            turn_exp(i, s - ET_LAG)
                        if exists(i, s - PV_LAG) and (new or s < PV_LAG):
                            values(i, s - PV_LAG)
                        if r == SPREAD and exists(i, image) and (new or image < 0):
                            pe.wait_ge(s_rx.sem, s_rx.after(i, image + 1))
                            if exists(i, image - 1):
                                pe.wait_ge(s_done.sem, s_done.after(i, image))
                            for half in range(2):
                                for t in range(NT):
                                    ins = nc.tensor.transpose(bank[7][:, half * N + t * P:half * N + (t + 1) * P],
                                                              rx[:, t, half, :], ident[:, :])
                            ins.then_inc(s_rT.sem, 1)
                        if r == PROJECT and exists(i, image - 1):
                            pe.wait_ge(s_oT.sem, s_oT.after(i, image))
                            for t in range(NT):
                                for half in range(2):
                                    ins = nc.tensor.matmul(bank[7][:, t * P:(t + 1) * P], oT[:, half, t * P:(t + 1) * P],
                                                           Wp[:, half, :], start=(half == 0), stop=(half == 1))
                            ins.then_inc(s_y.sem, 1)
                        if r == TURN and exists(i, image - 1):
                            pe.wait_ge(s_xn.sem, s_xn.after(i, image))
                            for t in range(NT):
                                a = (image - 1) % PAIR * N + t * P
                                ins = nc.tensor.transpose(bank[7][:, N + t * P:N + (t + 1) * P], xn_s[:, a:a + P], ident[:, :])
                            ins.then_inc(s_xT.sem, 1)

                    all_turns(pe, steps)

                @block.scalar
                def _(act):
                    def steps(i, s, new):
                        r, image = s % HEADS, s // HEADS - 1
                        if r == NORMALISE and exists(i, image - 1):
                            b = (image - 1) % PAIR
                            act.wait_ge(s_rs.sem, s_rs.after(i, image))
                            for t in range(b * NT, (b + 1) * NT):
                                ins = nc.scalar.activation(xn_s[:, t * P:(t + 1) * P], r_s[:, t * P:(t + 1) * P], ACT.Identity,
                                                           bias=shift[:, t:t + 1], scale=rstd[:, t:t + 1])
                            ins.then_inc(s_xn.sem, 1)
                        if r == KEEP and exists(i, image - 1):
                            act.wait_ge(s_xT.sem, s_xT.after(i, image))
                            hold(act)
                            nc.scalar.copy(XN_C[:, bass.ds(i * W + (image - 1) * N, N)], bank[7][:, N:2 * N]).then_inc(s_done.sem, 1)
                        if r == STORE and exists(i, image) and (new or image < 0):
                            if exists(i, image - 1):
                                act.wait_ge(s_oT.sem, s_oT.after(i, image))
                            act.wait_ge(s_PV.sem, s_PV.after(i, (image + 1) * HEADS))
                            nc.scalar.copy(o_raw[:, :, :].rearrange("p f n -> p (f n)"), bank[6][:, :]).then_inc(s_o.sem, 1)
                        if new:
                            act.wait_ge(s_nm.sem, s_nm.after(i, s + 1))
                            if exists(i, s - SLOTS):
                                act.wait_ge(s_ET.sem, s_ET.after(i, s - SLOTS + 1))
                            for t in range(NT):
                                if windowed:
                                    to, of = (Ew[:, s % SLOTS, 0:P], bank[s % SLOTS][:, WIN:KEYS]) if t == 0 else (
                                        Ew[:, s % SLOTS, P:P + KEYS], bank[s % SLOTS][:, KEYS:2 * KEYS])
                                else:
                                    to, of = E_s[:, s % SLOTS, t, :], bank[s % SLOTS][:, t * N:(t + 1) * N]
                                ins = nc.scalar.activation(to, of,
                                                           ACT.Exp, bias=negmax[:, s // HEADS, s % HEADS, t:t + 1],
                                                           accum_out=rowsum[:, s // HEADS, s % HEADS, t:t + 1])
                            ins.then_inc(s_E.sem, 1)

                    all_turns(act, steps)

                @block.vector
                def _(dve):
                    link = Chain(dve, s_link)
                    STEPS = 3

                    def steps(i, s, new):
                        r, image = s % HEADS, s // HEADS - 1
                        if new:
                            dve.wait_ge(s_S.sem, s_S.after(i, s + 1))
                            nc.vector.tensor_reduce(negmax[:, s // HEADS, s % HEADS, :],
                                                    bank[s % SLOTS][:, 0:width].rearrange("p (t k) -> p t k", t=NT),
                                                    AX.X, ALU.max, negate=True).then_inc(s_nm.sem, 1)
                        u = s - ET_LAG
                        if exists(i, u) and (new or u < 0):
                            dve.wait_ge(s_ET.sem, s_ET.after(i, u + 1))
                            if exists(i, u - SLOTS):
                                dve.wait_ge(s_PV.sem, s_PV.after(i, u - SLOTS + 1))
                            nc.vector.tensor_copy(ET_s[:, u % SLOTS, :, :].rearrange("p k n -> p (k n)")[:, 0:turned],
                                                  bank[4 + u % 2][:, 0:turned]).then_inc(s_ETs.sem, 1)
                        if r == STORE and exists(i, image) and (new or image < 0):
                            if exists(i, image - 1):
                                dve.wait_ge(s_rx.sem, s_rx.after(i, image))
                            dve.wait_ge(s_E.sem, s_E.after(i, (image + 1) * HEADS))
                            nc.vector.reciprocal(rinv[:, image % PAIR, :, :], rowsum[:, image % PAIR, :, :]).then_inc(s_ri.sem, 1)
                        if r == SCALE and exists(i, image) and (new or image < 0):
                            dve.wait_ge(s_rT.sem, s_rT.after(i, image + 1))
                            dve.wait_ge(s_o.sem, s_o.after(i, image + 1))
                            nc.vector.tensor_tensor(oT[:, :, :].rearrange("p f n -> p (f n)"), o_raw[:, :, :].rearrange("p f n -> p (f n)"),
                                                    bank[7][:, :], ALU.mult).then_inc(s_oT.sem, 1)
                        if r == ADD and exists(i, image - 1):
                            image -= 1
                            b = image % PAIR
                            link.turn(i * PAIR + image, STEPS)
                            dve.wait_ge(s_kept.sem, s_kept.after(i, image - 1))
                            dve.wait_ge(s_y.sem, s_y.after(i, image + 1))
                            link(nc.vector.tensor_tensor(r_s[:, b * N:(b + 1) * N], bank[7][:, 0:N],
                                                         R[:, bass.ds(i * W + image * N, N)], ALU.add))
                            for t in range(b * NT, (b + 1) * NT):
                                ins = nc.vector.bn_stats(stats[:, t, :], r_s[:, t * P:(t + 1) * P])
                            link(ins)
                            hold(dve)
                            for t in range(b * NT, (b + 1) * NT):
                                ins = nc.vector.bn_aggr(mv[:, t, :], stats[:, t, :])
                            link(ins)
                            dve.sem_inc(s_mv.sem, 1)
                            link.ended(STEPS)

                    all_turns(dve, steps)

                @block.gpsimd
                def _(pool):
                    link = Chain(pool, s_link_p, idle)

                    def pad(i, b):
                        pool.wait_ge(s_PV.sem, s_PV.after(i, (b - 1) * HEADS))
                        hold(pool)
                        nc.gpsimd.tensor_copy(v_pad[:, b, :, :, 0:HD],
                                              vall[:, bass.ds(i * W + b * N, N)].rearrange("p (t h d) -> p t h d", t=NT, d=HD)).then_inc(s_v.sem, 1)

                    def spread(i, image):
                        if exists(i, image - 1):
                            pool.wait_ge(s_rT.sem, s_rT.after(i, image))
                        pool.wait_ge(s_ri.sem, s_ri.after(i, image + 1))
                        hold(pool)
                        nc.gpsimd.tensor_copy(rx[:, :, :, :].rearrange("p t f (j r) -> p t (f j) r", r=32),
                                              rinv[:, image % PAIR, :, :].rearrange("p h t -> p t h")[:, :, :, None].broadcast_to([P, NT, HEADS, 32])
                                              ).then_inc(s_rx.sem, 1)

                    def rsqrt_image(i, image):
                        a = image % PAIR * NT
                        link.turn(i * PAIR + image, RSQRT_POOL + 2)
                        pool.wait_ge(s_mv.sem, s_mv.after(i, image + 1))
                        hold(pool)
                        link(nc.gpsimd.tensor_scalar(var[:, a:a + NT], mv[:, a:a + NT, 1], 1e-5, None, ALU.add))
                        rsqrt(nc.gpsimd, link, a, NT, fused=False)
                        link(nc.gpsimd.tensor_tensor(shift[:, a:a + NT], mv[:, a:a + NT, 0], rstd[:, a:a + NT], ALU.mult))
                        nc.gpsimd.tensor_scalar(shift[:, a:a + NT], shift[:, a:a + NT], -1.0, None, ALU.mult).then_inc(s_rs.sem, 1)
                        link.ended(RSQRT_POOL + 2)

                    def keep(i, image):
                        b = image % PAIR
                        pool.wait_ge(s_xn.sem, s_xn.after(i, image + 1))
                        hold(pool)
                        if not windowed:
                            nc.gpsimd.tensor_copy(XN_T[:, bass.ds(i * W + image * N, N)], xn_s[:, b * N:(b + 1) * N])
                        nc.gpsimd.tensor_copy(R[:, bass.ds(i * W + image * N, N)], r_s[:, b * N:(b + 1) * N]).then_inc(s_kept.sem, 1)

                    pool.sem_inc(s_kept.sem, s_kept.ahead)

                    def turn(i):
                        pad(i, 0)
                        if exists(i, -2):
                            rsqrt_image(i, -2)
                        if exists(i, -1):
                            spread(i, -1)
                        if exists(i, -2):
                            keep(i, -2)
                        pad(i, 1)
                        if exists(i, -1):
                            rsqrt_image(i, -1)
                        spread(i, 0)
                        if exists(i, -1):
                            keep(i, -1)

                    turn(0)
                    with pool.Fori(1, GROUPS) as i:
                        turn(i)
                    rsqrt_image(GROUPS, -2)
                    spread(GROUPS, -1)
                    keep(GROUPS, -2)
                    rsqrt_image(GROUPS, -1)
                    keep(GROUPS, -1)

        attention("l1", False, Wp1, qk_in)

        layer2 = ctx.enter_context(ExitStack())

        def sb2(name, shape, dt=F32):
            return layer2.enter_context(nc.sbuf_tensor(name, shape, dt))

        PB = sb2("PB", [P, GROUPS * 2 * W])
        z_s = sb2("z_s", [P, 3, 2 * W])
        g_s = sb2("g_s", [P, 3, 2 * W])
        h_s = sb2("h_s", [P, 3, W])

        xs_in = signal("l2_xs_in", 16)
        s_S, s_nm, s_E = signal("l2_scores", 2, True), signal("l2_negmax", 2), signal("l2_exp", 2)
        s_ET, s_ETs, s_O = signal("l2_ET", 2), signal("l2_ET_stored", 2), signal("l2_O", 2)
        s_xn, s_xT, s_xTs, s_xc = signal("l2_xn", 1), signal("l2_xnT", 1), signal("l2_xnT_stored", 1), signal("l2_xn_c", 1, True)
        s_lg, s_gap, s_e, s_p = signal("l2_logits", 1), signal("l2_gap", 1), signal("l2_gate_exp", 1), signal("l2_gates", 1)
        s_pb, s_done = signal("l2_gate_rows", 2), signal("l2_done", 2, True)
        s_link = sem("l2_steps")
        with nc.Block() as block:
            @block.sync
            def _(sp):
                with sp.Fori(0, GROUPS) as i:
                    sp.wait_ge(s_S.sem, s_S.before(i))
                    sp.dma_start(xs[:, :], XN_C[:, bass.ds(i * W, W)]).then_inc(xs_in.sem, 16)

            @block.tensor
            def _(pe):
                pe.sem_inc(s_S.sem, s_S.ahead)
                with pe.Fori(0, GROUPS) as i:
                    pe.wait_ge(xs_in.sem, xs_in.after(i))
                    pe.wait_ge(s_done.sem, s_done.before(i))
                    for b in range(PAIR):
                        for t in range(NT):
                            a = b * N + t * P
                            ins = nc.tensor.matmul(bank[b][:, t * N:(t + 1) * N], xs[:, a:a + P], xs[:, b * N:(b + 1) * N],
                                                   start=True, stop=True)
                        ins.then_inc(s_S.sem, 1)
                    for b in range(PAIR):
                        pe.wait_ge(s_E.sem, s_E.after(i, b + 1))
                        for t in range(NT):
                            for kt in range(NT):
                                ins = nc.tensor.transpose(bank[2 + b][:, kt * N + t * P:kt * N + (t + 1) * P],
                                                          E_s[:, b, t, kt * P:(kt + 1) * P], ident[:, :])
                        ins.then_inc(s_ET.sem, 1)
                    for b in range(PAIR):
                        pe.wait_ge(s_ETs.sem, s_ETs.after(i, b + 1))
                        for t in range(NT):
                            for kt in range(NT):
                                ins = nc.tensor.matmul(bank[4 + b][:, t * P:(t + 1) * P], ET_s[:, b, kt, t * P:(t + 1) * P],
                                                       XN_T[:, bass.ds(i * W + (b * NT + kt) * P, P)],
                                                       start=(kt == 0), stop=(kt == NT - 1))
                        ins.then_inc(s_O.sem, 1)
                    pe.wait_ge(s_xn.sem, s_xn.after(i))
                    for t in range(TILES):
                        ins = nc.tensor.transpose(bank[6][:, t * P:(t + 1) * P], xn_s[:, t * P:(t + 1) * P], ident[:, :])
                    ins.then_inc(s_xT.sem, 1)
                    pe.wait_ge(s_xTs.sem, s_xTs.after(i))
                    for t in range(TILES):
                        ins = nc.tensor.matmul(bank[7][:, t * EXPERTS:(t + 1) * EXPERTS], xc_s[:, t * P:(t + 1) * P], Wg[:, :],
                                               start=True, stop=True)
                    ins.then_inc(s_lg.sem, 1)
                    pe.wait_ge(s_p.sem, s_p.after(i))
                    for w in range(2):
                        for t in range(TILES):
                            ins = nc.tensor.transpose(bank[w][:, t * P:(t + 1) * P],
                                                      gate[:, 3 + w, t:t + 1].broadcast_to([P, P]), ident[:, :])
                        ins.then_inc(s_pb.sem, 1)

            @block.scalar
            def _(act):
                act.sem_inc(s_done.sem, s_done.ahead)
                with act.Fori(0, GROUPS) as i:
                    for b in range(PAIR):
                        act.wait_ge(s_nm.sem, s_nm.after(i, b + 1))
                        for t in range(NT):
                            ins = nc.scalar.activation(E_s[:, b, t, :], bank[b][:, t * N:(t + 1) * N], ACT.Exp,
                                                       bias=negmax[:, b, 0, t:t + 1], accum_out=rowsum[:, b, 0, t:t + 1])
                        ins.then_inc(s_E.sem, 1)
                    act.wait_ge(s_xc.sem, s_xc.before(i))
                    act.wait_ge(s_xT.sem, s_xT.after(i))
                    nc.scalar.copy(xc_s[:, :], bank[6][:, :]).then_inc(s_xTs.sem, 1)
                    act.wait_ge(s_gap.sem, s_gap.after(i))
                    nc.scalar.activation(gate[:, 1, :], gate[:, 0, :], ACT.Exp).then_inc(s_e.sem, 1)
                    for w in range(2):
                        act.wait_ge(s_pb.sem, s_pb.after(i, w + 1))
                        hold(act)
                        nc.scalar.copy(PB[:, bass.ds(i * 2 * W + w * W, W)], bank[w][:, :]).then_inc(s_done.sem, 1)

            @block.vector
            def _(dve):
                link = Chain(dve, s_link)
                STEPS = 3 + NORM + 3
                with dve.Fori(0, GROUPS) as i:
                    link.turn(i, STEPS)
                    for b in range(PAIR):
                        dve.wait_ge(s_S.sem, s_S.after(i, b + 1))
                        nc.vector.tensor_reduce(negmax[:, b, 0, :], bank[b][:, :].rearrange("p (t k) -> p t k", t=NT),
                                                AX.X, ALU.max, negate=True).then_inc(s_nm.sem, 1)
                    for b in range(PAIR):
                        dve.wait_ge(s_ET.sem, s_ET.after(i, b + 1))
                        nc.vector.tensor_copy(ET_s[:, b, :, :].rearrange("p k n -> p (k n)"), bank[2 + b][:, :]).then_inc(s_ETs.sem, 1)
                    link(nc.vector.reciprocal(rinv[:, :, 0, :], rowsum[:, :, 0, :]))
                    dve.wait_ge(s_O.sem, s_O.after(i))
                    for b in range(PAIR):
                        for t in range(NT):
                            a = b * N + t * P
                            ins = nc.vector.scalar_tensor_tensor(r_s[:, a:a + P], bank[4 + b][:, t * P:(t + 1) * P],
                                                                 rinv[:, b, 0, t:t + 1], R[:, bass.ds(i * W + a, P)],
                                                                 ALU.mult, ALU.add)
                    link(ins)
                    hold(dve)
                    link(nc.vector.tensor_copy(R[:, bass.ds(i * W, W)], r_s[:, :]))
                    token_norm(dve, link, 1e-5, range(TILES), s_xn)
                    dve.wait_ge(s_lg.sem, s_lg.after(i))
                    hold(dve)
                    for t in range(TILES):
                        ins = nc.vector.max(top[:, t, :], bank[7][:, t * EXPERTS:(t + 1) * EXPERTS])
                    link(ins)
                    nc.vector.tensor_tensor(gate[:, 0, :], top[:, :, 1], top[:, :, 0], ALU.subtract).then_inc(s_gap.sem, 1)
                    dve.wait_ge(s_e.sem, s_e.after(i))
                    link(nc.vector.tensor_scalar(gate[:, 2, :], gate[:, 1, :], 1.0, None, ALU.add))
                    link(nc.vector.reciprocal(gate[:, 3, :], gate[:, 2, :]))
                    nc.vector.tensor_tensor(gate[:, 4, :], gate[:, 1, :], gate[:, 3, :], ALU.mult).then_inc(s_p.sem, 1)
                    link.ended(STEPS)

            @block.gpsimd
            def _(pool):
                pool.sem_inc(s_xc.sem, s_xc.ahead)
                with pool.Fori(0, GROUPS) as i:
                    pool.wait_ge(s_xTs.sem, s_xTs.after(i))
                    hold(pool)
                    nc.gpsimd.tensor_copy(XN_C[:, bass.ds(i * W, W)], xc_s[:, :]).then_inc(s_xc.sem, 1)

        s_U, s_z, s_g, s_h, s_D = (signal(n, FT) for n in ("ff_up", "ff_gated", "ff_gelu", "ff_hidden", "ff_down"))
        s_ys, s_yT, s_xn, s_xT, s_done = (signal("ff_y_stored", 1), signal("ff_yT", 1), signal("ff_xn", 1),
                                          signal("ff_xnT", 1), signal("ff_done", 1, True))
        s_link = sem("ff_steps")
        D_LAG, RING = 3, 3
        with nc.Block() as block:
            @block.tensor
            def _(pe):
                pe.wait_ge(w_l2, 20 * 16)
                with pe.Fori(0, GROUPS) as i:
                    pe.wait_ge(s_done.sem, s_done.before(i))
                    for s in range(FT + D_LAG):
                        if s < FT:
                            if s >= 4:
                                pe.wait_ge(s_z.sem, s_z.after(i, s - 3))
                            nc.tensor.matmul(bank[s % 4][:, :], W1[:, s // 4, s % 4 * P:(s % 4 + 1) * P],
                                             XN_C[:, bass.ds(i * W, W)], start=True, stop=True).then_inc(s_U.sem, 1)
                        f = s - D_LAG
                        if f >= 0:
                            pe.wait_ge(s_h.sem, s_h.after(i, f + 1))
                            nc.tensor.matmul(bank[7][:, :], W2[:, f, :], h_s[:, f % RING, :],
                                             start=(f == 0), stop=(f == FT - 1)).then_inc(s_D.sem, 1)
                    pe.wait_ge(s_ys.sem, s_ys.after(i))
                    for t in range(TILES):
                        ins = nc.tensor.transpose(bank[6][:, t * P:(t + 1) * P], y_s[:, t * P:(t + 1) * P], ident[:, :])
                    ins.then_inc(s_yT.sem, 1)
                    pe.wait_ge(s_xn.sem, s_xn.after(i))
                    for t in range(TILES):
                        ins = nc.tensor.transpose(bank[5][:, t * P:(t + 1) * P], xn_s[:, t * P:(t + 1) * P], ident[:, :])
                    ins.then_inc(s_xT.sem, 1)

            @block.vector
            def _(dve):
                link = Chain(dve, s_link)
                STEPS = 2 + NORM
                with dve.Fori(0, GROUPS) as i:
                    link.turn(i, STEPS)
                    for f in range(FT):
                        dve.wait_ge(s_U.sem, s_U.after(i, f + 1))
                        if f >= RING:
                            dve.wait_ge(s_g.sem, s_g.after(i, f - RING + 1))
                        nc.vector.tensor_tensor(z_s[:, f % RING, :].rearrange("p (w n) -> p w n", w=2),
                                                bank[f % 4][:, None, :].broadcast_to([P, 2, W]),
                                                PB[:, bass.ds(i * 2 * W, 2 * W)].rearrange("p (w n) -> p w n", w=2),
                                                ALU.mult).then_inc(s_z.sem, 1)
                    dve.wait_ge(s_yT.sem, s_yT.after(i))
                    link(nc.vector.tensor_tensor(r_s[:, :], bank[6][:, :], R[:, bass.ds(i * W, W)], ALU.add))
                    hold(dve)
                    link(nc.vector.tensor_copy(R[:, bass.ds(i * W, W)], r_s[:, :]))
                    token_norm(dve, link, 1e-5, range(TILES), s_xn)
                    link.ended(STEPS)

            @block.scalar
            def _(act):
                act.sem_inc(s_done.sem, s_done.ahead)
                with act.Fori(0, GROUPS) as i:
                    for f in range(FT):
                        act.wait_ge(s_z.sem, s_z.after(i, f + 1))
                        if f >= RING:
                            act.wait_ge(s_h.sem, s_h.after(i, f - RING + 1))
                        nc.scalar.activation(g_s[:, f % RING, :], z_s[:, f % RING, :], ACT.Gelu,
                                             bias=b1[:, f:f + 1]).then_inc(s_g.sem, 1)
                    act.wait_ge(s_D.sem, s_D.after(i))
                    nc.scalar.activation(y_s[:, :], bank[7][:, :], ACT.Identity, bias=b2two[:, :]).then_inc(s_ys.sem, 1)
                    act.wait_ge(s_xT.sem, s_xT.after(i))
                    hold(act)
                    nc.scalar.copy(XN_C[:, bass.ds(i * W, W)], bank[5][:, :]).then_inc(s_done.sem, 1)

            @block.gpsimd
            def _(pool):
                with pool.Fori(0, GROUPS) as i:
                    for f in range(FT):
                        pool.wait_ge(s_g.sem, s_g.after(i, f + 1))
                        if f >= RING:
                            pool.wait_ge(s_D.sem, s_D.after(i, f - RING + 1))
                        nc.gpsimd.tensor_tensor(h_s[:, f % RING, :], g_s[:, f % RING, 0:W], g_s[:, f % RING, W:2 * W],
                                                ALU.add).then_inc(s_h.sem, 1)
        layer2.close()

        prep3 = ctx.enter_context(ExitStack())

        def sb3(name, shape, dt=F32):
            return prep3.enter_context(nc.sbuf_tensor(name, shape, dt))

        xs3 = sb3("xs3", [P, 2, W])
        qk3 = XN_T[:, :].rearrange("p (b t c) -> p b t c", b=2, t=TILES)
        qb = R_C[:, :].rearrange("p (b t c) -> p b t c", b=2, t=TILES)
        qa = sb3("qa", [P, 2, TILES, 2 * P])
        qp = sb3("qp", [P, 2, TILES, 2, P])
        rest3 = sb3("rest3", [P, 2, 2, W])
        parts3 = sb3("parts3", [P, 2, PARTS, 2, W], BF16)

        xs_in = [signal(f"l3_xs_in{b}", 16) for b in range(2)]
        s_out = [signal(f"l3_parts_in_dram{b}", 6 * 16, True) for b in range(2)]
        qk_in3 = [signal(f"l3_stack_in{b}", STACK_DMAS * 16) for b in range(PAIR)]
        s_proj, s_qks, s_st = signal("l3_qkv", 2 * TILES, True), signal("l3_qk_stored", 2), signal("l3_qkv_stored", 2 * TILES, True)
        s_sq, s_rms, s_rot, s_qp, s_qT = (signal("l3_squares", 2), signal("l3_rms", 2), signal("l3_rotated", 2),
                                          signal("l3_qk_ready", 2, True), signal("l3_qkT", 2, True))
        s_c1, s_r1, s_c2, s_c3 = (signal("l3_part1", 2), signal("l3_rest1", 2, True), signal("l3_part2", 2),
                                  signal("l3_part3", 2, True))
        s_link = sem("l3_prep_steps")
        with nc.Block() as block:
            @block.sync
            def _(sp):
                for b in range(2):
                    sp.sem_inc(s_out[b].sem, s_out[b].ahead)
                for i in range(GROUPS // 2):
                    for b in range(2):
                        sp.wait_ge(s_proj.sem, s_proj.after(i, (b - 1) * TILES))
                        sp.dma_start(xs3[:, b, :], XN_C[:, bass.ds((i * 2 + b) * W, W)]).then_inc(xs_in[b].sem, 16)
                    if i == 1:
                        sp.wait_ge(s_out[0].sem, s_out[0].after(0))
                        read_stack(sp, bass.ds(0, 1), 0, qk_in3[0])
                    for b in range(2):
                        sp.wait_ge(s_c1.sem, s_c1.after(i, b + 1))
                        write_parts(sp, parts3, i * 2 + b, b, 0, s_out[b])
                        sp.wait_ge(s_c2.sem, s_c2.after(i, b + 1))
                        write_parts(sp, parts3, i * 2 + b, b, 1, s_out[b])
                        sp.wait_ge(s_c3.sem, s_c3.after(i, b + 1))
                        write_parts(sp, parts3, i * 2 + b, b, 2, s_out[b])
                for b in range(2):
                    sp.wait_ge(s_out[b].sem, s_out[b].after(GROUPS // 2 - 1))

            @block.tensor
            def _(pe):
                pe.sem_inc(s_proj.sem, s_proj.ahead)
                pe.sem_inc(s_qT.sem, s_qT.ahead)
                with pe.Fori(0, GROUPS // 2) as i:
                    for b in range(2):
                        pe.wait_ge(xs_in[b].sem, xs_in[b].after(i))
                        for t in range(TILES):
                            pe.wait_ge(s_st.sem, s_st.after(i, (b - 1) * TILES + t + 1))
                            nc.tensor.matmul(bank[t][:, 0:3 * P], xs3[:, b, t * P:(t + 1) * P], Wqkv3[:, :],
                                             start=True, stop=True).then_inc(s_proj.sem, 1)
                    for b in range(2):
                        pe.wait_ge(s_r1.sem, s_r1.after(i, b - 1))
                        pe.wait_ge(s_qp.sem, s_qp.after(i, b + 1))
                        for kind in range(2):
                            for t in range(TILES):
                                ins = nc.tensor.transpose(bank[4 + 2 * b + kind][:, t * P:(t + 1) * P], qp[:, b, t, kind, :], ident[:, :])
                        ins.then_inc(s_qT.sem, 1)

            @block.scalar
            def _(act):
                act.sem_inc(s_st.sem, s_st.ahead)
                with act.Fori(0, GROUPS // 2) as i:
                    for b in range(2):
                        act.wait_ge(s_qp.sem, s_qp.after(i, b - 1))
                        for t in range(TILES):
                            act.wait_ge(s_proj.sem, s_proj.after(i, b * TILES + t + 1))
                            hold(act)
                            ins = nc.scalar.copy(qk3[:, b, t, :], bank[t][:, 0:2 * P])
                            if t == TILES - 1:
                                ins.then_inc(s_qks.sem, 1)
                            nc.scalar.copy(vall[:, bass.ds((i * 2 + b) * W + t * P, P)], bank[t][:, 2 * P:3 * P]).then_inc(s_st.sem, 1)
                        act.wait_ge(s_qks.sem, s_qks.after(i, b + 1))
                        nc.scalar.activation(qa[:, b, :, :], qk3[:, b, :, :], ACT.Square).then_inc(s_sq.sem, 1)
                    for b in range(2):
                        act.wait_ge(s_out[b].sem, s_out[b].before(i))
                        act.wait_ge(s_qT.sem, s_qT.after(i, b + 1))
                        for kind in range(2):
                            ins = nc.scalar.copy(parts3[:, b, 0, kind, :], bank[4 + 2 * b + kind][:, :])
                        ins.then_inc(s_c1.sem, 1)
                    for b in range(2):
                        act.wait_ge(s_r1.sem, s_r1.after(i, b + 1))
                        nc.scalar.copy(parts3[:, b, 1, :, :], rest3[:, b, :, :]).then_inc(s_c2.sem, 1)

            @block.vector
            def _(dve):
                link = Chain(dve, s_link)
                STEPS = 3 + RSQRT
                for ahead in (s_qp, s_r1, s_c3):
                    dve.sem_inc(ahead.sem, ahead.ahead)
                with dve.Fori(0, GROUPS // 2) as i:
                    for b in range(2):
                        link.turn(i * 2 + b, STEPS)
                        dve.wait_ge(s_sq.sem, s_sq.after(i, b + 1))
                        heads = TILES * 2 * HEADS
                        link(nc.vector.tensor_reduce(var[:, 0:heads], qa[:, b, :, :].rearrange("p t (g d) -> p (t g) d", d=HD), AX.X, ALU.add))
                        link(nc.vector.tensor_scalar(var[:, 0:heads], var[:, 0:heads], 1.0 / HD, 1e-6, ALU.mult, ALU.add))
                        rsqrt(nc.vector, link, 0, heads)
                        flat = qk3[:, b, :, :].rearrange("p t (g d) -> p (t g) d", d=HD)
                        nc.vector.tensor_tensor(flat, flat, rstd[:, 0:heads, None].broadcast_to([P, heads, HD]), ALU.mult).then_inc(s_rms.sem, 1)
                        dve.wait_ge(s_rms.sem, s_rms.after(i, b + 1))
                        for t in range(TILES):
                            ins = nc.vector.tensor_tensor(qa[:, b, t, :].rearrange("p (c h d) -> p c h d", c=2, d=HD),
                                                          qk3[:, b, t, :].rearrange("p (c h d) -> p c h d", c=2, d=HD),
                                                          cosw[:, t % NT, :, None, :].broadcast_to([P, 2, HEADS, HD]), ALU.mult)
                        link(ins)
                        dve.wait_ge(s_rot.sem, s_rot.after(i, b + 1))
                        dve.wait_ge(s_qT.sem, s_qT.after(i, b - 1))
                        nc.vector.tensor_tensor(qp[:, b, :, :, :].rearrange("p t c (d h) -> p (t c) h d", h=HEADS),
                                                qa[:, b, :, :].rearrange("p t (c h d) -> p (t c) h d", c=2, d=HD),
                                                qb[:, b, :, :].rearrange("p t (c h d) -> p (t c) h d", c=2, d=HD), ALU.add).then_inc(s_qp.sem, 1)
                        link.ended(STEPS)
                    for b in range(2):
                        dve.wait_ge(s_c3.sem, s_c3.after(i, b - 1))
                        dve.wait_ge(s_c1.sem, s_c1.after(i, b + 1))
                        for kind in range(2):
                            ins = nc.vector.tensor_tensor(rest3[:, b, kind, :], bank[4 + 2 * b + kind][:, :], parts3[:, b, 0, kind, :], ALU.subtract)
                        ins.then_inc(s_r1.sem, 1)
                    for b in range(2):
                        dve.wait_ge(s_c2.sem, s_c2.after(i, b + 1))
                        nc.vector.tensor_tensor(parts3[:, b, 2, :, :], rest3[:, b, :, :], parts3[:, b, 1, :, :], ALU.subtract).then_inc(s_c3.sem, 1)

            @block.gpsimd
            def _(pool):
                H = HD // 2
                with pool.Fori(0, GROUPS // 2) as i:
                    for b in range(2):
                        pool.wait_ge(s_rms.sem, s_rms.after(i, b + 1))
                        for t in range(TILES):
                            x = qk3[:, b, t, :].rearrange("p (c h d) -> p c h d", c=2, d=HD)
                            y = qb[:, b, t, :].rearrange("p (c h d) -> p c h d", c=2, d=HD)
                            s = sinw[:, t % NT, :, None, :].broadcast_to([P, 2, HEADS, HD])
                            nc.gpsimd.tensor_tensor(y[:, :, :, 0:H], x[:, :, :, H:HD], s[:, :, :, 0:H], ALU.mult)
                            ins = nc.gpsimd.tensor_tensor(y[:, :, :, H:HD], x[:, :, :, 0:H], s[:, :, :, H:HD], ALU.mult)
                        ins.then_inc(s_rot.sem, 1)
        prep3.close()

        attention("l3", True, Wo3, qk_in3)

        ALL = TOKENS // P
        pr = sb("pr", [P, 4, ALL, EXPERTS])
        best = sb("best", [P, 3, ALL])
        top2 = sb("top2", [P, ALL, 8])
        top2i = sb("top2i", [P, ALL, 8], U32)
        top2f = sb("top2f", [P, ALL, 8])
        w_parts = sb("w_parts", [P, ALL, PARTS, EXPERTS], BF16)
        wT = sb("wT", [PARTS * EXPERTS, TOKENS], BF16)
        s_lg, s_sh, s_pe, s_wp, s_wT, s_rT, s_rc = (sem("l3_" + n) for n in (
            "logits", "shifted", "router_exp", "weight_parts", "weightsT", "residualT", "residual_c"))
        s_link = sem("router_steps")
        with nc.Block() as block:
            @block.tensor
            def _(pe):
                for t in range(ALL):
                    ins = nc.tensor.matmul(bank[4][:, t * EXPERTS:(t + 1) * EXPERTS], XN_C[:, t * P:(t + 1) * P],
                                           router[:, :], start=True, stop=True)
                ins.then_inc(s_lg, 1)
                for t in range(ALL):
                    nc.tensor.transpose(bank[t // TILES][:, t % TILES * P:(t % TILES + 1) * P], R[:, t * P:(t + 1) * P],
                                        ident[:, :]).then_inc(s_rT, 1)
                pe.wait_ge(s_rc, GROUPS)
                pe.wait_ge(s_wp, 1)
                for t in range(ALL):
                    nc.tensor.matmul(bank[t // TILES][0:PARTS * EXPERTS, t % TILES * P:(t % TILES + 1) * P],
                                     w_parts[:, t, :, :], identb[:, :], start=True, stop=True).then_inc(s_wT, 1)

            @block.scalar
            def _(act):
                act.wait_ge(s_sh, 1)
                nc.scalar.activation(pr[:, 1, :, :], pr[:, 0, :, :], ACT.Exp).then_inc(s_pe, 1)
                for g in range(GROUPS):
                    act.wait_ge(s_rT, (g + 1) * TILES)
                    nc.scalar.copy(R_C[:, g * W:(g + 1) * W], bank[g][:, :]).then_inc(s_rc, 1)
                for g in range(GROUPS):
                    act.wait_ge(s_wT, (g + 1) * TILES)
                    nc.scalar.copy(wT[:, g * W:(g + 1) * W], bank[g][0:PARTS * EXPERTS, :])

            @block.vector
            def _(dve):
                link = Chain(dve, s_link)
                wide = [P, ALL, EXPERTS]
                dve.wait_ge(s_lg, 1)
                logits = bank[4][:, 0:ALL * EXPERTS].rearrange("p (t e) -> p t e", e=EXPERTS)
                link(nc.vector.tensor_reduce(best[:, 0, :], logits, AX.X, ALU.max))
                nc.vector.tensor_tensor(pr[:, 0, :, :], logits, best[:, 0, :, None].broadcast_to(wide), ALU.subtract).then_inc(s_sh, 1)
                dve.wait_ge(s_pe, 1)
                link(nc.vector.tensor_reduce(best[:, 1, :], pr[:, 1, :, :], AX.X, ALU.add))
                link(nc.vector.reciprocal(best[:, 2, :], best[:, 1, :]))
                link(nc.vector.tensor_tensor(pr[:, 2, :, :], pr[:, 1, :, :], best[:, 2, :, None].broadcast_to(wide), ALU.mult))
                for t in range(ALL):
                    ins = nc.vector.max(top2[:, t, :], pr[:, 2, t, :])
                link(ins)
                for t in range(ALL):
                    ins = nc.vector.max_index(top2i[:, t, :], top2[:, t, :], pr[:, 2, t, :])
                link(ins)
                link(nc.vector.tensor_copy(top2f[:, :, :], top2i[:, :, :]))
                for n in range(2):
                    link(nc.vector.tensor_tensor(pr[:, 3 * n, :, :], iota8[:, None, :].broadcast_to(wide),
                                                 top2f[:, :, n:n + 1].broadcast_to(wide), ALU.is_equal))
                link(nc.vector.tensor_tensor(pr[:, 0, :, :], pr[:, 0, :, :], pr[:, 3, :, :], ALU.add))
                link(nc.vector.tensor_tensor(pr[:, 3, :, :], pr[:, 0, :, :], pr[:, 2, :, :], ALU.mult))
                for part in range(PARTS - 1):
                    link(nc.vector.tensor_copy(w_parts[:, :, part, :], pr[:, 3, :, :]))
                    link(nc.vector.tensor_tensor(pr[:, 3, :, :], pr[:, 3, :, :], w_parts[:, :, part, :], ALU.subtract))
                nc.vector.tensor_copy(w_parts[:, :, PARTS - 1, :], pr[:, 3, :, :]).then_inc(s_wp, 1)

        a_s = sb("a_s", [P, 2, W])
        c_s = sb("c_s", [P, 2, W])
        BLOCKS = 5
        s_G, s_Up, s_si, s_m, s_c, s_Dn = (signal(n, BLOCKS) for n in ("ex_gate", "ex_up", "ex_silu", "ex_product", "ex_weighted", "ex_down"))
        s_rw = signal("ex_weights", BLOCKS - 1)
        s_out, s_sum = signal("out_stored", 16, True), signal("ex_sum", 1, True)
        with nc.Block() as block:
            @block.tensor
            def _(pe):
                with pe.Fori(0, GROUPS) as i:
                    pe.wait_ge(s_sum.sem, s_sum.before(i))
                    for s in range(BLOCKS + 1):
                        if s < BLOCKS:
                            m = P if s < 4 else EH
                            if s >= 2:
                                pe.wait_ge(s_m.sem, s_m.after(i, s - 1))
                            if s == 4:
                                hold(pe)
                            for to, w, done in ((bank[s % 2], Wgate[:, 2 * s:2 * s + 2, :] if s < 4 else Sgate[:, :], s_G),
                                                (bank[2 + s % 2], Wup[:, 2 * s:2 * s + 2, :] if s < 4 else Sup[:, :], s_Up)):
                                nc.tensor.matmul(to[0:m, :], w, XN_C[:, bass.ds(i * W, W)], start=True, stop=True).then_inc(done.sem, 1)
                            if s < 4:
                                if s >= 2:
                                    pe.wait_ge(s_c.sem, s_c.after(i, s - 1))
                                    hold(pe)
                                nc.tensor.matmul(bank[4 + s % 2][:, :], expert_rows[:, s * P:(s + 1) * P],
                                                 wT[:, bass.ds(i * W, W)], start=True, stop=True).then_inc(s_rw.sem, 1)
                        n = s - 1
                        if n >= 0:
                            pe.wait_ge(s_c.sem, s_c.after(i, n + 1))
                            m = P if n < 4 else EH
                            nc.tensor.matmul(bank[6][:, :], Wdown[:, n, :] if n < 4 else Sdown[:, :], c_s[0:m, n % 2, :],
                                             start=(n == 0), stop=(n == BLOCKS - 1)).then_inc(s_Dn.sem, 1)

            @block.scalar
            def _(act):
                with act.Fori(0, GROUPS) as i:
                    for n in range(BLOCKS):
                        m = P if n < 4 else EH
                        act.wait_ge(s_G.sem, s_G.after(i, n + 1))
                        if n >= 2:
                            act.wait_ge(s_m.sem, s_m.after(i, n - 1))
                        nc.scalar.activation(a_s[0:m, n % 2, :], bank[n % 2][0:m, :], ACT.Silu).then_inc(s_si.sem, 1)

            @block.vector
            def _(dve):
                dve.sem_inc(s_sum.sem, s_sum.ahead)
                with dve.Fori(0, GROUPS) as i:
                    for n in range(BLOCKS):
                        m = P if n < 4 else EH
                        dve.wait_ge(s_Up.sem, s_Up.after(i, n + 1))
                        dve.wait_ge(s_si.sem, s_si.after(i, n + 1))
                        if n >= 2:
                            dve.wait_ge(s_Dn.sem, s_Dn.after(i, n - 1))
                        nc.vector.tensor_tensor(c_s[0:m, n % 2, :], a_s[0:m, n % 2, :], bank[2 + n % 2][0:m, :],
                                                ALU.mult).then_inc(s_m.sem, 1)
                        dve.wait_ge(s_m.sem, s_m.after(i, n + 1))
                        if n < 4:
                            dve.wait_ge(s_rw.sem, s_rw.after(i, n + 1))
                            nc.vector.tensor_tensor(c_s[:, n % 2, :], c_s[:, n % 2, :], bank[4 + n % 2][:, :],
                                                    ALU.mult).then_inc(s_c.sem, 1)
                        else:
                            dve.sem_inc(s_c.sem, 1)
                    dve.wait_ge(s_Dn.sem, s_Dn.after(i))
                    dve.wait_ge(s_out.sem, s_out.before(i))
                    nc.vector.tensor_tensor(y_s[:, :], bank[6][:, :], R_C[:, bass.ds(i * W, W)], ALU.add).then_inc(s_sum.sem, 1)

            @block.sync
            def _(sp):
                sp.sem_inc(s_out.sem, s_out.ahead)
                with sp.Fori(0, GROUPS) as i:
                    sp.wait_ge(s_sum.sem, s_sum.after(i))
                    sp.dma_start(OUT[:, bass.ds(i * PAIR, PAIR), :], y_s[:, :].rearrange("p (b n) -> p b n", n=N)).then_inc(s_out.sem, 16)
                sp.wait_ge(s_out.sem, 16 * (GROUPS + 1))


_INS = ["x", "L0_conv_Wb", "L0_conv_Wc", "L0_conv_Wd", "L0_conv_gamma", "L1_conv_W_qkv", "L1_conv_b_qkv",
        "L1_conv_W_proj", "L1_conv_b_proj", "L2_ffn_Wg", "L2_ffn_W1", "L2_ffn_b1", "L2_ffn_W2", "L2_ffn_b2",
        "L3_attn_rope_cos", "L3_attn_rope_sin", "L3_attn_W_q", "L3_attn_W_k", "L3_attn_W_v", "L3_attn_W_o",
        "L3_attn_q_norm_w", "L3_attn_k_norm_w", "L3_ffn_router", "L3_ffn_shared_gate", "L3_ffn_shared_up",
        "L3_ffn_shared_down", "L3_ffn_W_gate", "L3_ffn_W_up", "L3_ffn_W_down"]


def kernel(**inputs):
    import numpy as _np
    import concourse.bacc as _bacc
    from concourse import mybir as _mybir
    from concourse.bass_utils import run_bass_kernel_spmd as _run

    nc = _bacc.Bacc("TRN2", target_bir_lowering=False, num_devices=1)
    arrays, args = {}, {}
    for name in _INS:
        a = _np.ascontiguousarray(inputs[name])
        arrays[f"in_{name}_dram"] = a
        args[name] = nc.dram_tensor(f"in_{name}_dram", a.shape, _mybir.dt.from_np(a.dtype), kind="ExternalInput").ap()
    out = nc.dram_tensor("out_0_dram", (8, 128, 16, 16), _mybir.dt.float32, kind="ExternalOutput").ap()
    bass_conv_attn_hybrid_kernel(nc, args, out)
    r = _run(nc, [arrays], core_ids=[0])
    return r.results[0]["out_0_dram"]
```

```python
from contextlib import ExitStack

import concourse.bass as bass
from concourse import mybir
from concourse.alu_op_type import AluOpType as ALU

F32 = mybir.dt.float32
BF16 = mybir.dt.bfloat16
I32 = mybir.dt.int32
U32 = mybir.dt.uint32
ACT = mybir.ActivationFunctionType
AX = mybir.AxisListType

P = 128
IMAGES = 8
N = 256
TOKENS = IMAGES * N
GROUPS = 4
W = TOKENS // GROUPS
TILES = W // P
PAIR = W // N
NT = N // P
HEADS, HD = 8, 16
SLOTS = 4
EXPERTS = 8
FF = 512
FT = EXPERTS * FF // P
EH = 64
WIN = 32
KEYS = WIN + P
NO_KEY = -1.0e30


class Signal:

    def __init__(self, sem, per, ahead):
        self.sem, self.per, self.ahead = sem, per, per if ahead else 0

    def after(self, turn, count=None):
        return turn * self.per + self.ahead + (self.per if count is None else count)

    def before(self, turn):
        return turn * self.per + self.ahead


class Chain:

    def __init__(self, eng, sem, idle=None):
        self.eng, self.sem, self.idle, self.count, self.base = eng, sem, idle, 0, 0

    def turn(self, i, steps):
        self.base, self.count = i * steps, 0

    def __call__(self, ins):
        ins.then_inc(self.sem, 1)
        self.count += 1
        self.eng.wait_ge(self.sem, self.base + self.count)
        if self.idle is not None:
            self.eng.sem_inc(self.idle, 1)

    def ended(self, steps):
        assert self.count == steps, f"a turn has {self.count} linked steps, not {steps}"


def bass_conv_attn_hybrid_kernel(nc, A, out):
    with ExitStack() as ctx:
        def sb(name, shape, dt=F32):
            return ctx.enter_context(nc.sbuf_tensor(name, shape, dt))

        def sem(name):
            return ctx.enter_context(nc.semaphore(name))

        def signal(name, per, ahead=False):
            return Signal(nc.alloc_semaphore(name=name), per, ahead)

        def over(signals):
            nc.clear_and_free_semaphores([s.sem for s in signals])
            nc.all_engine_barrier()

        bank = [ctx.enter_context(nc.psum_tensor(f"bank{k}", [P, 512], F32)) for k in range(8)]

        R = sb("R", [P, TOKENS])
        XN_C = sb("XN_C", [P, TOKENS])
        XN_T = sb("XN_T", [P, TOKENS])
        R_C = sb("R_C", [P, TOKENS])

        ident = sb("ident", [P, P])
        ones = sb("ones", [P, P])
        identb = sb("identb", [P, P], BF16)
        bandb = sb("bandb", [P, 2, KEYS], BF16)
        band = sb("band", [P, 2, KEYS])
        groups4 = sb("groups4", [P, P])
        wraw = sb("wraw", [P, 8, P])
        Wbc = sb("Wbc", [P, P])
        WdT = sb("WdT", [P, P])
        Wqk1 = sb("Wqk1", [P, 2, P])
        WvT = sb("WvT", [P, P])
        Wp_raw = sb("Wp_raw", [P, 2, P])
        Wp1 = sb("Wp1", [P, 2, P])
        bqk = sb("bqk", [P, 2])
        bias_rows = sb("bias_rows", [P, P])
        bv_all = sb("bv_all", [P, P])
        bp_all = sb("bp_all", [P, P])
        gamma_all = sb("gamma_all", [P, 1])
        Wg = sb("Wg", [P, EXPERTS])
        W1 = sb("W1", [P, EXPERTS, FF])
        W2 = sb("W2", [P, FT, P])
        b1 = sb("b1", [P, FT])
        b2two = sb("b2two", [P, 1])
        Wqkv3 = sb("Wqkv3", [P, 3 * P])
        Wo3 = sb("Wo3", [P, 2, P])
        norm_w = sb("norm_w", [P, 2, HD])
        rope = sb("rope", [P, 2, NT, HD])
        cosw = sb("cosw", [P, NT, 2, HD])
        sinw = sb("sinw", [P, NT, 2, HD])
        router = sb("router", [P, EXPERTS])
        Wgate = sb("Wgate", [P, EXPERTS, EH])
        Wup = sb("Wup", [P, EXPERTS, EH])
        Wdown = sb("Wdown", [P, 4, P])
        Sgate = sb("Sgate", [P, EH])
        Sup = sb("Sup", [P, EH])
        Sdown = sb("Sdown", [EH, P])
        rows_f = sb("rows_f", [3 * EXPERTS, EXPERTS, EH])
        iota_i = sb("iota_i", [P, EXPERTS], I32)
        iota8 = sb("iota8", [P, EXPERTS])
        expert_rows = sb("expert_rows", [3 * EXPERTS, EXPERTS * EH], BF16)

        xs = sb("xs", [P, W])
        v_s = sb("v_s", [P, TILES, P])
        xT_s = sb("xT_s", [P, W])
        E_s = sb("E_s", [P, SLOTS, NT, N])
        ET_s = sb("ET_s", [P, SLOTS, 2, N])
        negmax = sb("negmax", [P, PAIR, HEADS, NT])
        rowsum = sb("rowsum", [P, PAIR, HEADS, NT])
        rinv = sb("rinv", [P, PAIR, HEADS, NT])
        o_raw = sb("o_raw", [P, 2, N])
        rx = sb("rx", [P, NT, 2, P])
        shift = sb("shift", [P, TILES])
        oT = sb("oT", [P, 2, N])
        q_s = o_raw[:, :, :].rearrange("p f n -> p (f n)")
        r_s = sb("r_s", [P, W])
        xn_s = sb("xn_s", [P, W])
        stats = sb("stats", [P, TILES, 6])
        mv = sb("mv", [P, TILES, 2])
        mm_s = sb("mm_s", [P, PAIR, 2])
        gm = sb("gm", [P, PAIR, 2])
        var = sb("var", [P, 2 * TILES * 2 * HEADS])
        rstd = sb("rstd", [P, 2 * TILES * 2 * HEADS])
        ntmp = sb("ntmp", [P, 2 * TILES * 2 * HEADS])
        top2 = sb("top2", [P, TOKENS // P, 8])
        gate = sb("gate", [P, 5, TOKENS // P])
        y_s = sb("y_s", [P, W])
        idle = sem("idle")

        X = A["x"].rearrange("b c h w -> c b (h w)")
        OUT = out.rearrange("b c h w -> c b (h w)")

        def hold(eng):
            eng.sem_inc(idle, 1)

        def rsqrt(on, link, a, n, fused=True):
            y, v, t = rstd[:, a:a + n], var[:, a:a + n], ntmp[:, a:a + n]
            if fused:
                for k in range(RSQRT):
                    newton_step(on, link, k, y, v, t)
                return
            newton_step(on, link, 0, y, v, t)
            for _ in range(3):
                link(on.tensor_tensor(t, y, y, ALU.mult))
                link(on.tensor_tensor(t, t, v, ALU.mult))
                link(on.tensor_scalar(t, t, -0.5, 1.5, ALU.mult, ALU.add))
                link(on.tensor_tensor(y, t, y, ALU.mult))

        RSQRT, RSQRT_POOL = 10, 13

        def newton_step(on, link, k, y, v, t):
            if k == 0:
                link(on.tensor_scalar(y.bitcast(I32), v.bitcast(I32), -0.5, float(0x5F3759DF), ALU.mult, ALU.add))
            elif k % 3 == 1:
                link(on.tensor_tensor(t, y, y, ALU.mult))
            elif k % 3 == 2:
                link(on.scalar_tensor_tensor(t, t, -0.5, v, ALU.mult, ALU.mult))
            else:
                link(on.scalar_tensor_tensor(y, t, 1.5, y, ALU.add, ALU.mult))

        def norm_step(dve, link, k, eps, tiles, done):
            a, n = tiles[0], len(tiles)
            if k == 0:
                for t in tiles:
                    ins = nc.vector.bn_stats(stats[:, t, :], r_s[:, t * P:(t + 1) * P])
                link(ins)
            elif k == 1:
                hold(dve)
                for t in tiles:
                    ins = nc.vector.bn_aggr(mv[:, t, :], stats[:, t, :])
                link(ins)
            elif k == 2:
                link(nc.vector.tensor_scalar(var[:, a:a + n], mv[:, a:a + n, 1], eps, None, ALU.add))
            elif k < NORM:
                newton_step(nc.vector, link, k - 3, rstd[:, a:a + n], var[:, a:a + n], ntmp[:, a:a + n])
            else:
                for t in tiles:
                    ins = nc.vector.tensor_scalar(xn_s[:, t * P:(t + 1) * P], r_s[:, t * P:(t + 1) * P],
                                                  mv[:, t, 0:1], rstd[:, t:t + 1], ALU.subtract, ALU.mult)
                ins.then_inc(done.sem, 1)

        NORM = 3 + RSQRT

        w_raw, w_c, w_l2, w_l3, w_pads = (sem(n) for n in (
            "w_raw_loaded", "w_conv_loaded", "w_layer2_loaded", "w_layer3_loaded", "pads_zero"))
        s_ident, s_wT, s_prep = sem("ident_ready"), sem("weights_turned"), sem("prep_steps")
        s_prep_p, s_zero, s_wp = sem("pool_prep_steps"), sem("raw_rows_zero"), sem("proj_columns_placed")
        x_in = [signal(f"l0_x_in{b}", 16) for b in range(PAIR)]
        with nc.Block() as block:
            @block.sync
            def _(sp):
                sp.wait_ge(s_zero, 1)
                sp.dma_start(wraw[0:16, 0, :], A["L0_conv_Wb"]).then_inc(w_raw, 16)
                sp.dma_start(wraw[0:16, 7, :], A["L0_conv_Wc"]).then_inc(w_raw, 16)
                sp.dma_start(wraw[:, 1, :], A["L0_conv_Wd"]).then_inc(w_raw, 16)
                sp.dma_start(wraw[:, 2:5, :], A["L1_conv_W_qkv"].rearrange("(k o) c -> o k c", k=3)).then_inc(w_raw, 16)
                sp.dma_start(wraw[:, 5, :], A["L1_conv_W_proj"]).then_inc(w_raw, 16)
                sp.dma_start(wraw[0:FT, 6, :], A["L2_ffn_b1"].rearrange("e (q f) -> (e q) f", f=P)).then_inc(w_raw, 16)
                sp.dma_start(wraw[32:32 + EXPERTS, 6, :], A["L2_ffn_b2"]).then_inc(w_raw, 16)
                for kind in range(2):
                    sp.dma_start(wraw[64 + kind:65 + kind, 6, :], A["L1_conv_b_qkv"][None, kind * P:(kind + 1) * P]).then_inc(w_raw, 16)
                sp.dma_start(gamma_all[:, :], A["L0_conv_gamma"][None, :].broadcast_to([P, 1])).then_inc(w_c, 16)
                sp.dma_start(bv_all[:, :], A["L1_conv_b_qkv"][None, 2 * P:3 * P].broadcast_to([P, P])).then_inc(w_c, 16)
                sp.dma_start(bp_all[:, :], A["L1_conv_b_proj"][None, :].broadcast_to([P, P])).then_inc(w_c, 16)
                for b in range(PAIR):
                    sp.dma_start(xs[:, b * N:(b + 1) * N], X[:, b, :]).then_inc(x_in[b].sem, 16)

            @block.gpsimd
            def _(pool):
                link = Chain(pool, s_prep_p)
                nc.gpsimd.memset(wraw[:, 6, :], 0.0).then_inc(s_zero, 1)
                link(nc.gpsimd.memset(ones[:, :], 1.0))
                nc.gpsimd.affine_select(out=ident[:, :], in_=ones[:, :], compare_op=ALU.is_equal, fill=0.0,
                                        base=0, pattern=[[-1, P]], channel_multiplier=1).then_inc(s_ident, 1)
                link(nc.gpsimd.memset(groups4[:, :], 0.25))
                v = groups4[:, :].rearrange("p (g d) -> p g d", d=4)
                link(nc.gpsimd.affine_select(out=v, in_=v, compare_op=ALU.is_ge, fill=0.0, base=0,
                                             pattern=[[-4, P // 4], [0, 4]], channel_multiplier=1))
                link(nc.gpsimd.affine_select(out=v, in_=v, compare_op=ALU.is_ge, fill=0.0, base=3,
                                             pattern=[[4, P // 4], [0, 4]], channel_multiplier=-1))
                link(nc.gpsimd.memset(band[:, :, :], 0.0))
                link(nc.gpsimd.affine_select(out=band[:, :, :], in_=band[:, :, :], compare_op=ALU.is_ge, fill=NO_KEY,
                                             base=WIN, pattern=[[0, 2], [-1, KEYS]], channel_multiplier=1))
                link(nc.gpsimd.affine_select(out=band[:, :, :], in_=band[:, :, :], compare_op=ALU.is_gt, fill=NO_KEY,
                                             base=0, pattern=[[0, 2], [1, KEYS]], channel_multiplier=-1))
                link(nc.gpsimd.memset(band[:, 0, 0:WIN], NO_KEY))
                link(nc.gpsimd.tensor_copy(bandb[:, :, :], band[:, :, :]))
                link(nc.gpsimd.tensor_copy(identb[:, :], ident[:, :]))
                link(nc.gpsimd.memset(rows_f[:, :, :], 0.0))
                for part in range(3):
                    link(nc.gpsimd.affine_select(out=rows_f[:, :, :], in_=rows_f[:, :, :], compare_op=ALU.not_equal, fill=1.0,
                                                 base=-part * EXPERTS, pattern=[[-1, EXPERTS], [0, EH]], channel_multiplier=1))
                link(nc.gpsimd.tensor_copy(expert_rows[:, :], rows_f[:, :, :].rearrange("p e f -> p (e f)")))
                link(nc.gpsimd.iota(iota_i[:, :], pattern=[[1, EXPERTS]], base=0, channel_multiplier=0))
                link(nc.gpsimd.tensor_copy(iota8[:, :], iota_i[:, :]))

            @block.tensor
            def _(pe):
                pe.wait_ge(s_ident, 1)
                pe.wait_ge(w_raw, 9 * 16)
                pe.wait_ge(s_zero, 1)
                nc.tensor.matmul(bank[0][:, 0:P], wraw[0:16, 0, :], wraw[0:16, 7, :], start=True, stop=True).then_inc(s_wT, 1)
                for n in range(1, 5):
                    nc.tensor.transpose(bank[n][:, 0:P], wraw[:, n, :], ident[:, :]).then_inc(s_wT, 1)
                nc.tensor.transpose(bank[6][:, 0:P], wraw[:, 6, :], ident[:, :]).then_inc(s_wT, 1)
                pe.wait_ge(s_wp, 1)
                nc.tensor.transpose(bank[6][:, P:2 * P], bias_rows[:, :], ident[:, :]).then_inc(s_wT, 1)
                for half in range(2):
                    nc.tensor.transpose(bank[5][:, half * P:(half + 1) * P], Wp_raw[:, half, :], ident[:, :]).then_inc(s_wT, 1)

            @block.vector
            def _(dve):
                link = Chain(dve, s_prep)
                nc.vector.memset(Wo3[:, :, :], 0.0).then_inc(w_pads, 1)
                link(nc.vector.memset(Wp_raw[:, :, :], 0.0))
                dve.wait_ge(w_raw, 9 * 16)
                link(nc.vector.tensor_copy(bias_rows[:, :].rearrange("p (d h) -> p h d", h=HEADS),
                                           wraw[:, 6, :].rearrange("p (h d) -> p h d", d=HD)))
                nc.vector.tensor_copy(Wp_raw[:, :, :].rearrange("p f (j r) -> p (f j) r", r=32)[:, :, 0:HD],
                                      wraw[:, 5, :].rearrange("p (g d) -> p g d", d=HD)).then_inc(s_wp, 1)
                dve.wait_ge(s_wT, 9)
                nc.vector.tensor_copy(Wbc[:, :], bank[0][:, 0:P])
                nc.vector.tensor_copy(WdT[:, :], bank[1][:, 0:P])
                for kind in range(2):
                    nc.vector.tensor_copy(Wqk1[:, kind, :].rearrange("p (d h) -> p h d", h=HEADS),
                                          bank[2 + kind][:, 0:P].rearrange("p (h d) -> p h d", d=HD))
                nc.vector.tensor_copy(WvT[:, :], bank[4][:, 0:P])
                nc.vector.tensor_copy(Wp1[:, :, :].rearrange("p f c -> p (f c)"), bank[5][:, 0:2 * P])
                nc.vector.tensor_copy(b1[:, :], bank[6][:, 0:FT])
                nc.vector.tensor_scalar(bqk[:, 0:1], bank[6][:, P + 64:P + 65], HD ** -0.5, None, ALU.mult)
                nc.vector.tensor_copy(bqk[:, 1:2], bank[6][:, P + 65:P + 66])
                link(nc.vector.tensor_reduce(b2two[:, :], bank[6][:, FT:FT + EXPERTS], AX.X, ALU.add))
                link(nc.vector.tensor_scalar(b2two[:, :], b2two[:, :], 2.0, None, ALU.mult))

        def is_image(i, n):
            return not isinstance(i, int) or i * PAIR + n >= 0

        def image_turns(eng, steps):
            for i in range(2):
                for s in range(PAIR):
                    steps(i, s, True)
            with eng.Fori(2, GROUPS) as i:
                for s in range(PAIR):
                    steps(i, s, True)
            for s in range(3):
                steps(GROUPS, s, False)

        ps_q, ps_d = signal("l0_queries", PAIR), signal("l0_d", PAIR)
        a_q, a_d = signal("l0_queries_stored", PAIR), signal("l0_xT_and_d_stored", PAIR)
        s_S, s_nm, s_E = signal("l0_scores", PAIR, True), signal("l0_negmax", PAIR), signal("l0_exp", PAIR)
        s_ET, s_ETs, s_O = signal("l0_ET", PAIR), signal("l0_ET_stored", PAIR), signal("l0_O", PAIR)
        s_r, s_kept, s_rc, s_mm, s_gm, s_rs, s_done = (signal("l0_" + n, PAIR) for n in (
            "r", "r_kept", "r_c", "moments", "group_moments", "rstd", "done"))
        s_norm_w = sem("norm_w_scaled")
        s_link, s_ri, s_st = sem("l0_steps"), sem("l0_rinv"), sem("l0_stat_steps")
        with nc.Block() as block:
            @block.sync
            def _(sp):
                with sp.Fori(1, GROUPS) as i:
                    for b in range(PAIR):
                        sp.wait_ge(s_S.sem, s_S.after(i, b - 1))
                        sp.dma_start(xs[:, b * N:(b + 1) * N], X[:, bass.ds(i * PAIR + b, 1), :].rearrange("c o n -> c (o n)")).then_inc(x_in[b].sem, 16)
                sp.wait_ge(w_pads, 1)
                sp.dma_start(rope[:, 0, :, :], A["L3_attn_rope_cos"][0:N, :].rearrange("(t p) d -> p t d", p=P)).then_inc(w_l3, 16)
                sp.dma_start(rope[:, 1, :, :], A["L3_attn_rope_sin"][0:N, :].rearrange("(t p) d -> p t d", p=P)).then_inc(w_l3, 16)
                sp.dma_start(norm_w[:, 0, :], A["L3_attn_q_norm_w"][None, :].broadcast_to([P, HD])).then_inc(w_l3, 16)
                sp.dma_start(norm_w[:, 1, :], A["L3_attn_k_norm_w"][None, :].broadcast_to([P, HD])).then_inc(w_l3, 16)
                sp.dma_start(Wg[:, :], A["L2_ffn_Wg"]).then_inc(w_l2, 16)
                sp.dma_start(W1[:, :, :], A["L2_ffn_W1"].rearrange("e d f -> d e f")).then_inc(w_l2, 16)
                sp.dma_start(W2[:, :, :], A["L2_ffn_W2"].rearrange("e (q f) c -> f (e q) c", f=P)).then_inc(w_l2, 16)
                for n, name in enumerate(("L3_attn_W_q", "L3_attn_W_k", "L3_attn_W_v")):
                    sp.dma_start(Wqkv3[:, n * P:(n + 1) * P], A[name]).then_inc(w_l2, 16)
                for h in range(HEADS):
                    sp.dma_start(Wo3[32 * (h % SLOTS):32 * (h % SLOTS) + HD, h // SLOTS, :],
                                 A["L3_attn_W_o"][h * HD:(h + 1) * HD, :]).then_inc(w_l2, 16)
                sp.dma_start(router[:, :], A["L3_ffn_router"]).then_inc(w_l2, 16)
                sp.dma_start(Wgate[:, :, :], A["L3_ffn_W_gate"].rearrange("e d f -> d e f")).then_inc(w_l2, 16)
                sp.dma_start(Wup[:, :, :], A["L3_ffn_W_up"].rearrange("e d f -> d e f")).then_inc(w_l2, 16)
                sp.dma_start(Wdown[:, :, :], A["L3_ffn_W_down"].rearrange("(q e) f c -> (e f) q c", e=2)).then_inc(w_l2, 16)
                sp.dma_start(Sgate[:, :], A["L3_ffn_shared_gate"]).then_inc(w_l2, 16)
                sp.dma_start(Sup[:, :], A["L3_ffn_shared_up"]).then_inc(w_l2, 16)
                sp.dma_start(Sdown[:, :], A["L3_ffn_shared_down"]).then_inc(w_l2, 16)

            @block.tensor
            def _(pe):
                pe.sem_inc(s_S.sem, s_S.ahead)

                def steps(i, s, new):
                    n = s - 1
                    b = n % PAIR
                    if is_image(i, n) and (new or n < 0):
                        pe.wait_ge(s_E.sem, s_E.after(i, n + 1))
                        for t in range(NT):
                            for kt in range(NT):
                                ins = nc.tensor.transpose(bank[3][:, kt * N + t * P:kt * N + (t + 1) * P],
                                                          E_s[:, b, t, kt * P:(kt + 1) * P], ident[:, :])
                        ins.then_inc(s_ET.sem, 1)
                    if new:
                        pe.wait_ge(x_in[s].sem, x_in[s].after(i))
                        if is_image(i, s - 1):
                            pe.wait_ge(a_d.sem, a_d.after(i, s))
                        for t in range(NT):
                            a = s * N + t * P
                            nc.tensor.transpose(bank[0][:, t * P:(t + 1) * P], xs[:, a:a + P], ident[:, :])
                        nc.tensor.matmul(bank[1][:, 0:N], Wbc[:, :], xs[:, s * N:(s + 1) * N],
                                         start=True, stop=True).then_inc(ps_q.sem, 1)
                        for t in range(NT):
                            a = s * N + t * P
                            ins = nc.tensor.matmul(bank[0][:, N + t * P:N + (t + 1) * P], xs[:, a:a + P], WdT[:, :],
                                                   start=True, stop=True)
                        ins.then_inc(ps_d.sem, 1)
                    n = s - 3
                    if is_image(i, n) and (new or n < 0):
                        pe.wait_ge(s_mm.sem, s_mm.after(i, n + 1))
                        if is_image(i, n - 1):
                            pe.wait_ge(s_rs.sem, s_rs.after(i, n))
                        nc.tensor.matmul(bank[7][:, 0:2], groups4[:, :], mm_s[:, n % PAIR, :],
                                         start=True, stop=True).then_inc(s_gm.sem, 1)
                    if new:
                        pe.wait_ge(a_q.sem, a_q.after(i, s + 1))
                        for t in range(NT):
                            ins = nc.tensor.matmul(bank[2][:, t * N:(t + 1) * N], q_s[:, s * N + t * P:s * N + (t + 1) * P],
                                                   xs[:, s * N:(s + 1) * N], start=True, stop=True)
                        ins.then_inc(s_S.sem, 1)
                    n = s - 1
                    if is_image(i, n) and (new or n < 0):
                        pe.wait_ge(s_ETs.sem, s_ETs.after(i, n + 1))
                        pe.wait_ge(a_d.sem, a_d.after(i, n + 1))
                        if is_image(i, n - 1):
                            pe.wait_ge(s_r.sem, s_r.after(i, n))
                        for t in range(NT):
                            for kt in range(NT):
                                ins = nc.tensor.matmul(bank[4][:, t * P:(t + 1) * P], ET_s[:, b, kt, t * P:(t + 1) * P],
                                                       v_s[:, b * NT + kt, :], start=(kt == 0), stop=(kt == NT - 1))
                        ins.then_inc(s_O.sem, 1)
                    if is_image(i, s - 2) and (new or s < 2):
                        n = s - 2
                        pe.wait_ge(s_r.sem, s_r.after(i, n + 1))
                        if is_image(i, n - 2):
                            pe.wait_ge(s_done.sem, s_done.after(i, n - 1))
                        for t in range(NT):
                            a = n % PAIR * N + t * P
                            ins = nc.tensor.transpose(bank[5 + n % PAIR][:, t * P:(t + 1) * P], r_s[:, a:a + P], ident[:, :])
                        ins.then_inc(s_rc.sem, 1)

                image_turns(pe, steps)

            @block.scalar
            def _(act):
                def steps(i, s, new):
                    at = slice(s % PAIR * N, (s % PAIR + 1) * N)
                    if new:
                        if is_image(i, s - 2):
                            act.wait_ge(s_S.sem, s_S.after(i, s - 1))
                        act.wait_ge(ps_q.sem, ps_q.after(i, s + 1))
                        nc.scalar.copy(q_s[:, at], bank[1][:, 0:N]).then_inc(a_q.sem, 1)
                        if is_image(i, s - 2):
                            act.wait_ge(s_r.sem, s_r.after(i, s - 1))
                        act.wait_ge(ps_d.sem, ps_d.after(i, s + 1))
                        nc.scalar.copy(xT_s[:, at], bank[0][:, 0:N])
                        nc.scalar.copy(v_s[:, s * NT:(s + 1) * NT, :].rearrange("p t c -> p (t c)"), bank[0][:, N:2 * N]).then_inc(a_d.sem, 1)
                        act.wait_ge(s_nm.sem, s_nm.after(i, s + 1))
                        if is_image(i, s - 2):
                            act.wait_ge(s_ET.sem, s_ET.after(i, s - 1))
                        for t in range(NT):
                            ins = nc.scalar.activation(E_s[:, s, t, :], bank[2][:, t * N:(t + 1) * N], ACT.Exp,
                                                       bias=negmax[:, s, 0, t:t + 1], accum_out=rowsum[:, s, 0, t:t + 1])
                        ins.then_inc(s_E.sem, 1)
                    n = s - 3
                    b = n % PAIR
                    if is_image(i, n) and (new or n < 0):
                        act.wait_ge(s_rs.sem, s_rs.after(i, n + 1))
                        hold(act)
                        nc.scalar.activation(XN_C[:, bass.ds(i * W + n * N, N)], bank[5 + b][:, 0:N], ACT.Identity,
                                             bias=shift[:, b:b + 1], scale=rstd[:, b:b + 1]).then_inc(s_done.sem, 1)

                image_turns(act, steps)

            @block.vector
            def _(dve):
                link = Chain(dve, s_link)
                STEPS = RSQRT + 3

                def steps(i, s, new):
                    n = s - 2
                    b = n % PAIR
                    old = is_image(i, n) and (new or n < 0)
                    if old:
                        dve.wait_ge(s_O.sem, s_O.after(i, n + 1))
                        if is_image(i, n - 2):
                            dve.wait_ge(s_kept.sem, s_kept.after(i, n - 1))
                        for t in range(NT):
                            a = b * N + t * P
                            ins = nc.vector.scalar_tensor_tensor(r_s[:, a:a + P], bank[4][:, t * P:(t + 1) * P],
                                                                 rinv[:, b, 0, t:t + 1], xT_s[:, a:a + P], ALU.mult, ALU.add)
                        ins.then_inc(s_r.sem, 1)
                    if is_image(i, s - 1) and (new or s < 1):
                        e = (s - 1) % PAIR
                        dve.wait_ge(s_ET.sem, s_ET.after(i, s))
                        if is_image(i, s - 3):
                            dve.wait_ge(s_O.sem, s_O.after(i, s - 2))
                        nc.vector.reciprocal(rinv[:, e, 0, :], rowsum[:, e, 0, :]).then_inc(s_ri, 1)
                        dve.wait_ge(s_ri, i * PAIR + s)
                        nc.vector.tensor_scalar(rinv[:, e, 0, :], rinv[:, e, 0, :], gamma_all[:, :], None, ALU.mult)
                        nc.vector.tensor_copy(ET_s[:, e, :, :].rearrange("p k n -> p (k n)"), bank[3][:, :]).then_inc(s_ETs.sem, 1)
                    if new:
                        dve.wait_ge(s_S.sem, s_S.after(i, s + 1))
                        nc.vector.tensor_reduce(negmax[:, s, 0, :], bank[2][:, :].rearrange("p (t k) -> p t k", t=NT),
                                                AX.X, ALU.max, negate=True).then_inc(s_nm.sem, 1)
                    last = is_image(i, s - 3) and (new or s < 3)
                    c = (s - 3) % PAIR
                    if last:
                        link.turn(i * PAIR + s - 3, STEPS)
                        dve.wait_ge(s_gm.sem, s_gm.after(i, s - 2))
                        if is_image(i, s - 5):
                            dve.wait_ge(s_done.sem, s_done.after(i, s - 4))
                        link(nc.vector.tensor_copy(gm[:, c, :], bank[7][:, 0:2]))
                        link(nc.vector.tensor_tensor(ntmp[:, c:c + 1], gm[:, c, 0:1], gm[:, c, 0:1], ALU.mult))
                        link(nc.vector.scalar_tensor_tensor(var[:, c:c + 1], gm[:, c, 1:2], 1e-5, ntmp[:, c:c + 1],
                                                            ALU.add, ALU.subtract))
                        for k in range(RSQRT):
                            newton_step(nc.vector, link, k, rstd[:, c:c + 1], var[:, c:c + 1], ntmp[:, c:c + 1])
                        nc.vector.scalar_tensor_tensor(shift[:, c:c + 1], gm[:, c, 0:1], -1.0, rstd[:, c:c + 1],
                                                       ALU.mult, ALU.mult).then_inc(s_rs.sem, 1)
                    if old:
                        dve.wait_ge(s_rc.sem, s_rc.after(i, n + 1))
                        nc.vector.bn_stats(stats[:, b, :], bank[5 + b][:, 0:N]).then_inc(s_st, 1)
                        dve.wait_ge(s_st, (i * PAIR + n) * 3 + 1)
                        hold(dve)
                        nc.vector.bn_aggr(mm_s[:, b, :], stats[:, b, :]).then_inc(s_st, 1)
                        dve.wait_ge(s_st, (i * PAIR + n) * 3 + 2)
                        nc.vector.tensor_tensor(ntmp[:, 2:3], mm_s[:, b, 0:1], mm_s[:, b, 0:1], ALU.mult).then_inc(s_st, 1)
                        dve.wait_ge(s_st, (i * PAIR + n) * 3 + 3)
                        nc.vector.tensor_tensor(mm_s[:, b, 1:2], mm_s[:, b, 1:2], ntmp[:, 2:3], ALU.add).then_inc(s_mm.sem, 1)

                image_turns(dve, steps)
                dve.wait_ge(w_l3, 4 * 16)
                nc.vector.tensor_scalar(norm_w[:, 0, :], norm_w[:, 0, :], HD ** -0.5, None, ALU.mult).then_inc(s_norm_w, 1)
                dve.wait_ge(s_norm_w, 1)
                H = HD // 2
                for t in range(NT):
                    for kind in range(2):
                        nc.vector.tensor_tensor(cosw[:, t, kind, :], rope[:, 0, t, :], norm_w[:, kind, :], ALU.mult)
                        nc.vector.scalar_tensor_tensor(sinw[:, t, kind, 0:H], rope[:, 1, t, 0:H], -1.0,
                                                       norm_w[:, kind, H:HD], ALU.mult, ALU.mult)
                        nc.vector.tensor_tensor(sinw[:, t, kind, H:HD], rope[:, 1, t, H:HD], norm_w[:, kind, 0:H], ALU.mult)

            @block.gpsimd
            def _(pool):
                with pool.Fori(0, GROUPS) as i:
                    for b in range(PAIR):
                        pool.wait_ge(s_r.sem, s_r.after(i, b + 1))
                        hold(pool)
                        nc.gpsimd.tensor_tensor(R[:, bass.ds(i * W + b * N, N)].rearrange("p (t c) -> p t c", c=P),
                                                r_s[:, b * N:(b + 1) * N].rearrange("p (t c) -> p t c", c=P),
                                                bp_all[:, None, :].broadcast_to([P, NT, P]), ALU.add).then_inc(s_kept.sem, 1)
        over([ps_q, ps_d, a_q, a_d, s_S, s_nm, s_E, s_ET, s_ETs, s_O, s_r, s_kept, s_rc, s_mm, s_gm, s_rs, s_done])

        PARTS = 3
        BLOCKS_Q = (0, 0, 0, 1, 1, 1, 2, 2)
        BLOCKS_K = (0, 1, 2, 0, 1, 2, 0, 1)
        STACK_DMAS = len(BLOCKS_Q) + 3
        qk_dram = nc.dram_tensor("qk_parts", (IMAGES, 2, PARTS, P, N), BF16, kind="Internal").ap()
        vall = ctx.enter_context(nc.sbuf_tensor("vall", [P, TOKENS], F32))
        v_pad = ctx.enter_context(nc.sbuf_tensor("v_pad", [P, PAIR, NT, HEADS, 32], F32))
        stack = ctx.enter_context(nc.sbuf_tensor("stack", [P, PAIR, 2, HEADS, N], BF16))

        prep1 = ctx.enter_context(ExitStack())
        xs2 = prep1.enter_context(nc.sbuf_tensor("xs2", [P, 2, W], F32))
        qk_f = prep1.enter_context(nc.sbuf_tensor("qk_f", [P, 2, 2, W], F32))
        parts = prep1.enter_context(nc.sbuf_tensor("parts", [P, 2, PARTS, 2, W], BF16))

        def write_parts(sp, parts, g, b, part, done):
            for kind in range(2):
                sp.dma_start(qk_dram[bass.ds(g * PAIR, PAIR), kind, part, :, :].rearrange("b p n -> p b n"),
                             parts[:, b, part, kind, :].rearrange("p (b n) -> p b n", n=N)).then_inc(done.sem, 16)

        def read_stack(sp, image, b, done):
            rows = [qk_dram[image, kind, :, :, :].rearrange("o a (d h) n -> (o a d) (h n)", h=HEADS) for kind in range(2)]
            for n, part in enumerate(BLOCKS_Q):
                sp.dma_start(stack[n * HD:(n + 1) * HD, b, 0, :, :].rearrange("p h n -> p (h n)"),
                             rows[0][part * HD:(part + 1) * HD, :]).then_inc(done.sem, 16)
            for n, count in ((0, 3), (3, 3), (6, 2)):
                sp.dma_start(stack[n * HD:(n + count) * HD, b, 1, :, :].rearrange("p h n -> p (h n)"),
                             rows[1][0:count * HD, :]).then_inc(done.sem, 16)

        xs_in = [signal(f"l1_xs_in{b}", 16) for b in range(2)]
        p_q, p_v, a_qk, v_st = signal("l1_qk", 2 * 2), signal("l1_v", 2, True), signal("l1_qk_stored", 2, True), signal("l1_v_stored", 2, True)
        s_c1, s_r1, s_c2, s_c3 = (signal("l1_part1", 2), signal("l1_rest1", 2), signal("l1_part2", 2),
                                  signal("l1_part3", 2, True))
        s_out = [signal(f"l1_parts_in_dram{b}", 6 * 16, True) for b in range(2)]
        s_vpad = sem("v_pads_set")
        qk_in = [signal(f"l1_stack_in{b}", STACK_DMAS * 16) for b in range(PAIR)]
        with nc.Block() as block:
            @block.sync
            def _(sp):
                for b in range(2):
                    sp.sem_inc(s_out[b].sem, s_out[b].ahead)
                for i in range(GROUPS // 2):
                    for b in range(2):
                        sp.wait_ge(p_v.sem, p_v.after(i, b - 1))
                        sp.dma_start(xs2[:, b, :], XN_C[:, bass.ds((i * 2 + b) * W, W)]).then_inc(xs_in[b].sem, 16)
                    if i == 1:
                        sp.wait_ge(s_out[0].sem, s_out[0].after(0))
                        read_stack(sp, bass.ds(0, 1), 0, qk_in[0])
                    for b in range(2):
                        sp.wait_ge(s_c1.sem, s_c1.after(i, b + 1))
                        write_parts(sp, parts, i * 2 + b, b, 0, s_out[b])
                        sp.wait_ge(s_c2.sem, s_c2.after(i, b + 1))
                        write_parts(sp, parts, i * 2 + b, b, 1, s_out[b])
                        sp.wait_ge(s_c3.sem, s_c3.after(i, b + 1))
                        write_parts(sp, parts, i * 2 + b, b, 2, s_out[b])
                for b in range(2):
                    sp.wait_ge(s_out[b].sem, s_out[b].after(GROUPS // 2 - 1))

            @block.tensor
            def _(pe):
                pe.sem_inc(p_v.sem, p_v.ahead)
                with pe.Fori(0, GROUPS // 2) as i:
                    for b in range(2):
                        pe.wait_ge(xs_in[b].sem, xs_in[b].after(i))
                        pe.wait_ge(a_qk.sem, a_qk.after(i, b - 1))
                        for kind in range(2):
                            nc.tensor.matmul(bank[3 * b + kind][:, :], Wqk1[:, kind, :], xs2[:, b, :],
                                             start=True, stop=True).then_inc(p_q.sem, 1)
                        pe.wait_ge(v_st.sem, v_st.after(i, b - 1))
                        for t in range(TILES):
                            ins = nc.tensor.matmul(bank[3 * b + 2][:, t * P:(t + 1) * P], xs2[:, b, t * P:(t + 1) * P],
                                                   WvT[:, :], start=True, stop=True)
                        ins.then_inc(p_v.sem, 1)

            @block.scalar
            def _(act):
                act.sem_inc(a_qk.sem, a_qk.ahead)
                with act.Fori(0, GROUPS // 2) as i:
                    for b in range(2):
                        act.wait_ge(s_c3.sem, s_c3.after(i, b - 1))
                        for kind in range(2):
                            act.wait_ge(p_q.sem, p_q.after(i, 2 * b + kind + 1))
                            ins = nc.scalar.activation(qk_f[:, b, kind, :], bank[3 * b + kind][:, :], ACT.Identity,
                                                       bias=bqk[:, kind:kind + 1], scale=HD ** -0.5 if kind == 0 else 1.0)
                        ins.then_inc(a_qk.sem, 1)
                        act.wait_ge(s_out[b].sem, s_out[b].before(i))
                        act.wait_ge(a_qk.sem, a_qk.after(i, b + 1))
                        nc.scalar.copy(parts[:, b, 0, :, :], qk_f[:, b, :, :]).then_inc(s_c1.sem, 1)
                    for b in range(2):
                        act.wait_ge(s_r1.sem, s_r1.after(i, b + 1))
                        nc.scalar.copy(parts[:, b, 1, :, :], qk_f[:, b, :, :]).then_inc(s_c2.sem, 1)

            @block.vector
            def _(dve):
                dve.sem_inc(s_c3.sem, s_c3.ahead)
                dve.sem_inc(v_st.sem, v_st.ahead)
                with dve.Fori(0, GROUPS // 2) as i:
                    for b in range(2):
                        dve.wait_ge(p_v.sem, p_v.after(i, b + 1))
                        nc.vector.tensor_tensor(vall[:, bass.ds((i * 2 + b) * W, W)].rearrange("p (t c) -> p t c", c=P),
                                                bank[3 * b + 2][:, :].rearrange("p (t c) -> p t c", c=P),
                                                bv_all[:, None, :].broadcast_to([P, TILES, P]), ALU.add).then_inc(v_st.sem, 1)
                        dve.wait_ge(s_c1.sem, s_c1.after(i, b + 1))
                        nc.vector.tensor_tensor(qk_f[:, b, :, :], qk_f[:, b, :, :], parts[:, b, 0, :, :], ALU.subtract).then_inc(s_r1.sem, 1)
                    for b in range(2):
                        dve.wait_ge(s_c2.sem, s_c2.after(i, b + 1))
                        nc.vector.tensor_tensor(parts[:, b, 2, :, :], qk_f[:, b, :, :], parts[:, b, 1, :, :], ALU.subtract).then_inc(s_c3.sem, 1)

            @block.gpsimd
            def _(pool):
                nc.gpsimd.memset(v_pad[:, :, :, :, :], 0.0).then_inc(s_vpad, 1)
                pool.wait_ge(s_vpad, 1)
        prep1.close()

        UNITS = PAIR * HEADS
        ET_LAG, PV_LAG = 2, 4
        ON_ACT = 8

        def exists(i, n):
            return n >= 0 or not (isinstance(i, int) and i == 0)

        INVERT, WIDEN, STORE, SPREAD, SCALE, PROJECT, ADD, NORMALISE, TURN = 2, 3, 4, 5, 5, 6, 7, 5, 6

        def all_turns(eng, steps):
            for s in range(UNITS):
                steps(0, s, True)
            with eng.Fori(1, GROUPS) as i:
                for s in range(UNITS):
                    steps(i, s, True)
            for s in range(HEADS + TURN + 1):
                steps(GROUPS, s, False)

        def attention(name, windowed, Wp, qk_in):
            s_v = signal(name + "_v_padded", PAIR)
            s_S, s_nm, s_E = signal(name + "_scores", UNITS, True), signal(name + "_negmax", UNITS), signal(name + "_exp", UNITS)
            s_ET, s_PV = signal(name + "_ET", UNITS), signal(name + "_PV", UNITS, True)
            s_ETs, s_ETa = signal(name + "_ET_stored", UNITS - UNITS // ON_ACT), signal(name + "_ET_stored_act", UNITS // ON_ACT)
            s_o, s_rx, s_rT, s_oT, s_y = (signal(name + "_o", PAIR), signal(name + "_rinv_spread", PAIR), signal(name + "_rinvT", PAIR),
                                          signal(name + "_oT", PAIR), signal(name + "_y", PAIR))
            s_ri, s_mv, s_rs = signal(name + "_rinv", PAIR), signal(name + "_moments", PAIR), signal(name + "_rstd", PAIR)
            s_xn, s_xT, s_kept, s_done = (signal(name + "_xn", PAIR), signal(name + "_xnT", PAIR), signal(name + "_xn_kept", PAIR, True),
                                          signal(name + "_done", PAIR))
            s_link, s_link_p = sem(name + "_steps"), sem(name + "_pool_steps")

            def stored(u):
                return (s_ETa, u // ON_ACT + 1) if u % ON_ACT == ON_ACT - 1 else (s_ETs, u + 1 - (u + 1) // ON_ACT)

            width = 2 * (KEYS if windowed else N)
            turned = 3 * P if windowed else 2 * N
            Ew = E_s[:, :, :, :].rearrange("p j t n -> p j (t n)")[:, :, 0:P + KEYS]
            with nc.Block() as block:
                @block.sync
                def _(sp):
                    read_stack(sp, bass.ds(1, 1), 1, qk_in[1])
                    with sp.Fori(1, GROUPS) as i:
                        for b in range(PAIR):
                            sp.wait_ge(s_S.sem, s_S.after(i, (b - 1) * HEADS))
                            read_stack(sp, bass.ds(i * PAIR + b, 1), b, qk_in[b])

                @block.tensor
                def _(pe):
                    pe.sem_inc(s_S.sem, s_S.ahead)
                    pe.sem_inc(s_PV.sem, s_PV.ahead)

                    def scores(i, u):
                        b, h, j = u // HEADS % PAIR, u % HEADS, u % SLOTS
                        if h == 0:
                            pe.wait_ge(qk_in[b].sem, qk_in[b].after(i))
                        if exists(i, u - SLOTS):
                            pe.wait_ge(s_E.sem, s_E.after(i, u - SLOTS + 1))
                        q, k = stack[:, b, 0, h, :], stack[:, b, 1, h, :]
                        if windowed:
                            nc.tensor.matmul(bank[j][:, 0:2 * KEYS], identb[:, :], bandb[:, :, :].rearrange("p t s -> p (t s)"),
                                             start=True, stop=False, skip_group_check=True)
                            nc.tensor.matmul(bank[j][:, WIN:KEYS], q[:, 0:P], k[:, 0:P],
                                             start=False, stop=False, skip_group_check=True)
                            nc.tensor.matmul(bank[j][:, KEYS:2 * KEYS], q[:, P:N], k[:, P - WIN:N],
                                             start=False, stop=True, skip_group_check=True).then_inc(s_S.sem, 1)
                        else:
                            for t in range(NT):
                                ins = nc.tensor.matmul(bank[j][:, t * N:(t + 1) * N], q[:, t * P:(t + 1) * P], k,
                                                       start=True, stop=True)
                            ins.then_inc(s_S.sem, 1)

                    def turn_exp(i, u):
                        pe.wait_ge(s_E.sem, s_E.after(i, u + 1))
                        if (u + ET_LAG) % HEADS == TURN + 1 and exists(i, (u + ET_LAG) // HEADS - 2):
                            pe.wait_ge(s_done.sem, s_done.after(i, (u + ET_LAG) // HEADS - 1))
                        if exists(i, u - 2):
                            of, count = stored(u - 2)
                            pe.wait_ge(of.sem, of.after(i, count))
                        if windowed:
                            for n, a in enumerate((0, P + WIN, WIN)):
                                ins = nc.tensor.transpose(bank[4 + u % 2][:, n * P:(n + 1) * P],
                                                          Ew[:, u % SLOTS, a:a + P], ident[:, :])
                        else:
                            for t in range(NT):
                                for kt in range(NT):
                                    ins = nc.tensor.transpose(bank[4 + u % 2][:, kt * N + t * P:kt * N + (t + 1) * P],
                                                              E_s[:, u % SLOTS, t, kt * P:(kt + 1) * P], ident[:, :])
                        ins.then_inc(s_ET.sem, 1)

                    def values(i, u):
                        image, b, h = u // HEADS, u // HEADS % PAIR, u % HEADS
                        of, count = stored(u)
                        pe.wait_ge(of.sem, of.after(i, count))
                        if h == 0:
                            pe.wait_ge(s_v.sem, s_v.after(i, image + 1))
                            if exists(i, image - 1):
                                pe.wait_ge(s_o.sem, s_o.after(i, image))
                        rows, at = slice(32 * (h % SLOTS), 32 * (h % SLOTS) + 32), h // SLOTS * N
                        if windowed:
                            for t in range(NT):
                                nc.tensor.matmul(bank[6][rows, at + t * P:at + (t + 1) * P], v_pad[:, b, t, h, :],
                                                 ET_s[:, u % SLOTS, 0, t * P:(t + 1) * P], start=True, stop=(t == 0),
                                                 skip_group_check=True)
                            nc.tensor.matmul(bank[6][rows, at + P:at + N], v_pad[P - WIN:P, b, 0, h, :],
                                             ET_s[P - WIN:P, u % SLOTS, 1, 0:P], start=False, stop=True,
                                             skip_group_check=True).then_inc(s_PV.sem, 1)
                        else:
                            for kt in range(NT):
                                ins = nc.tensor.matmul(bank[6][rows, at:at + N], v_pad[:, b, kt, h, :],
                                                       ET_s[:, u % SLOTS, kt, :], start=(kt == 0), stop=(kt == NT - 1))
                            ins.then_inc(s_PV.sem, 1)

                    def steps(i, s, new):
                        r, image = s % HEADS, s // HEADS - 1
                        if new and s == 0:
                            scores(i, s)
                        if new and s < UNITS - 1:
                            scores(i, s + 1)
                        if exists(i, s - ET_LAG) and (new or s < ET_LAG):
                            turn_exp(i, s - ET_LAG)
                        if r == TURN and exists(i, image - 1):
                            pe.wait_ge(s_xn.sem, s_xn.after(i, image))
                            u = s - ET_LAG + 1
                            of, count = stored(u - 2)
                            if new or u - 2 < 0:
                                pe.wait_ge(of.sem, of.after(i, count))
                            for t in range(NT):
                                a = (image - 1) % PAIR * N + t * P
                                ins = nc.tensor.transpose(bank[4 + u % 2][:, t * P:(t + 1) * P], xn_s[:, a:a + P], ident[:, :])
                            ins.then_inc(s_xT.sem, 1)
                        if exists(i, s - PV_LAG) and (new or s < PV_LAG):
                            values(i, s - PV_LAG)
                        if r == SPREAD and exists(i, image) and (new or image < 0):
                            pe.wait_ge(s_rx.sem, s_rx.after(i, image + 1))
                            if exists(i, image - 1):
                                pe.wait_ge(s_mv.sem, s_mv.after(i, image))
                            for half in range(2):
                                for t in range(NT):
                                    ins = nc.tensor.transpose(bank[7][:, half * N + t * P:half * N + (t + 1) * P],
                                                              rx[:, t, half, :], ident[:, :])
                            ins.then_inc(s_rT.sem, 1)
                        if r == PROJECT and exists(i, image) and (new or image < 0):
                            pe.wait_ge(s_oT.sem, s_oT.after(i, image + 1))
                            for t in range(NT):
                                for half in range(2):
                                    ins = nc.tensor.matmul(bank[7][:, t * P:(t + 1) * P], oT[:, half, t * P:(t + 1) * P],
                                                           Wp[:, half, :], start=(half == 0), stop=(half == 1))
                            ins.then_inc(s_y.sem, 1)

                    all_turns(pe, steps)

                @block.scalar
                def _(act):
                    def steps(i, s, new):
                        r, image = s % HEADS, s // HEADS - 1
                        if r == NORMALISE and exists(i, image - 1):
                            b = (image - 1) % PAIR
                            act.wait_ge(s_rs.sem, s_rs.after(i, image))
                            for t in range(b * NT, (b + 1) * NT):
                                ins = nc.scalar.activation(xn_s[:, t * P:(t + 1) * P], r_s[:, t * P:(t + 1) * P], ACT.Identity,
                                                           bias=shift[:, t:t + 1], scale=rstd[:, t:t + 1])
                            ins.then_inc(s_xn.sem, 1)
                        if r == TURN and exists(i, image - 1):
                            act.wait_ge(s_xT.sem, s_xT.after(i, image))
                            hold(act)
                            nc.scalar.copy(XN_C[:, bass.ds(i * W + (image - 1) * N, N)],
                                           bank[4 + (s - ET_LAG + 1) % 2][:, 0:N]).then_inc(s_done.sem, 1)
                        if r == STORE and exists(i, image) and (new or image < 0):
                            if exists(i, image - 1):
                                act.wait_ge(s_oT.sem, s_oT.after(i, image))
                            act.wait_ge(s_PV.sem, s_PV.after(i, (image + 1) * HEADS))
                            nc.scalar.copy(o_raw[:, :, :].rearrange("p f n -> p (f n)"), bank[6][:, :]).then_inc(s_o.sem, 1)
                        if new:
                            act.wait_ge(s_nm.sem, s_nm.after(i, s + 1))
                            if exists(i, s - SLOTS):
                                act.wait_ge(s_ET.sem, s_ET.after(i, s - SLOTS + 1))
                            for t in range(NT):
                                if windowed:
                                    to, of = (Ew[:, s % SLOTS, 0:P], bank[s % SLOTS][:, WIN:KEYS]) if t == 0 else (
                                        Ew[:, s % SLOTS, P:P + KEYS], bank[s % SLOTS][:, KEYS:2 * KEYS])
                                else:
                                    to, of = E_s[:, s % SLOTS, t, :], bank[s % SLOTS][:, t * N:(t + 1) * N]
                                ins = nc.scalar.activation(to, of,
                                                           ACT.Exp, bias=negmax[:, s // HEADS, s % HEADS, t:t + 1],
                                                           accum_out=rowsum[:, s // HEADS, s % HEADS, t:t + 1])
                            ins.then_inc(s_E.sem, 1)
                        if r == WIDEN and exists(i, image) and (new or image < 0):
                            act.wait_ge(s_ri.sem, s_ri.after(i, image + 1))
                            if exists(i, image - 1):
                                act.wait_ge(s_rT.sem, s_rT.after(i, image))
                            of = rinv[:, image % PAIR, :, :].rearrange("p h t -> p t h")
                            for t in range(NT):
                                ins = nc.scalar.copy(rx[:, t, :, :].rearrange("p f (j r) -> p (f j) r", r=32),
                                                     of[:, t, :, None].broadcast_to([P, HEADS, 32]))
                            ins.then_inc(s_rx.sem, 1)
                        u = s - ET_LAG
                        if exists(i, u) and (new or u < 0) and u % ON_ACT == ON_ACT - 1:
                            act.wait_ge(s_ET.sem, s_ET.after(i, u + 1))
                            if exists(i, u - SLOTS):
                                act.wait_ge(s_PV.sem, s_PV.after(i, u - SLOTS + 1))
                            nc.scalar.copy(ET_s[:, u % SLOTS, :, :].rearrange("p k n -> p (k n)")[:, 0:turned],
                                           bank[4 + u % 2][:, 0:turned]).then_inc(s_ETa.sem, 1)

                    all_turns(act, steps)

                @block.vector
                def _(dve):
                    link = Chain(dve, s_link)
                    STEPS = 3

                    def steps(i, s, new):
                        r, image = s % HEADS, s // HEADS - 1
                        if new:
                            dve.wait_ge(s_S.sem, s_S.after(i, s + 1))
                            nc.vector.tensor_reduce(negmax[:, s // HEADS, s % HEADS, :],
                                                    bank[s % SLOTS][:, 0:width].rearrange("p (t k) -> p t k", t=NT),
                                                    AX.X, ALU.max, negate=True).then_inc(s_nm.sem, 1)
                        u = s - ET_LAG
                        if exists(i, u) and (new or u < 0) and u % ON_ACT != ON_ACT - 1:
                            dve.wait_ge(s_ET.sem, s_ET.after(i, u + 1))
                            if exists(i, u - SLOTS):
                                dve.wait_ge(s_PV.sem, s_PV.after(i, u - SLOTS + 1))
                            nc.vector.tensor_copy(ET_s[:, u % SLOTS, :, :].rearrange("p k n -> p (k n)")[:, 0:turned],
                                                  bank[4 + u % 2][:, 0:turned]).then_inc(s_ETs.sem, 1)
                        if r == INVERT and exists(i, image) and (new or image < 0):
                            if exists(i, image - 1):
                                dve.wait_ge(s_rx.sem, s_rx.after(i, image))
                            dve.wait_ge(s_E.sem, s_E.after(i, (image + 1) * HEADS))
                            nc.vector.reciprocal(rinv[:, image % PAIR, :, :], rowsum[:, image % PAIR, :, :]).then_inc(s_ri.sem, 1)
                        if r == SCALE and exists(i, image) and (new or image < 0):
                            dve.wait_ge(s_rT.sem, s_rT.after(i, image + 1))
                            dve.wait_ge(s_o.sem, s_o.after(i, image + 1))
                            nc.vector.tensor_tensor(oT[:, :, :].rearrange("p f n -> p (f n)"), o_raw[:, :, :].rearrange("p f n -> p (f n)"),
                                                    bank[7][:, :], ALU.mult).then_inc(s_oT.sem, 1)
                        if r == ADD and exists(i, image) and (new or image < 0):
                            b = image % PAIR
                            link.turn(i * PAIR + image, STEPS)
                            dve.wait_ge(s_kept.sem, s_kept.after(i, image - 1))
                            dve.wait_ge(s_y.sem, s_y.after(i, image + 1))
                            link(nc.vector.tensor_tensor(r_s[:, b * N:(b + 1) * N], bank[7][:, 0:N],
                                                         R[:, bass.ds(i * W + image * N, N)], ALU.add))
                            for t in range(b * NT, (b + 1) * NT):
                                ins = nc.vector.bn_stats(stats[:, t, :], r_s[:, t * P:(t + 1) * P])
                            link(ins)
                            hold(dve)
                            for t in range(b * NT, (b + 1) * NT):
                                ins = nc.vector.bn_aggr(mv[:, t, :], stats[:, t, :])
                            link(ins)
                            dve.sem_inc(s_mv.sem, 1)
                            link.ended(STEPS)

                    all_turns(dve, steps)

                @block.gpsimd
                def _(pool):
                    link = Chain(pool, s_link_p, idle)

                    def pad(i, b):
                        pool.wait_ge(s_PV.sem, s_PV.after(i, (b - 1) * HEADS))
                        hold(pool)
                        nc.gpsimd.tensor_copy(v_pad[:, b, :, :, 0:HD],
                                              vall[:, bass.ds(i * W + b * N, N)].rearrange("p (t h d) -> p t h d", t=NT, d=HD)).then_inc(s_v.sem, 1)

                    def rsqrt_image(i, image):
                        a = image % PAIR * NT
                        link.turn(i * PAIR + image, RSQRT_POOL + 2)
                        pool.wait_ge(s_mv.sem, s_mv.after(i, image + 1))
                        hold(pool)
                        link(nc.gpsimd.tensor_scalar(var[:, a:a + NT], mv[:, a:a + NT, 1], 1e-5, None, ALU.add))
                        rsqrt(nc.gpsimd, link, a, NT, fused=False)
                        link(nc.gpsimd.tensor_tensor(shift[:, a:a + NT], mv[:, a:a + NT, 0], rstd[:, a:a + NT], ALU.mult))
                        nc.gpsimd.tensor_scalar(shift[:, a:a + NT], shift[:, a:a + NT], -1.0, None, ALU.mult).then_inc(s_rs.sem, 1)
                        link.ended(RSQRT_POOL + 2)

                    def keep(i, image):
                        b = image % PAIR
                        pool.wait_ge(s_xn.sem, s_xn.after(i, image + 1))
                        hold(pool)
                        if not windowed:
                            nc.gpsimd.tensor_copy(XN_T[:, bass.ds(i * W + image * N, N)], xn_s[:, b * N:(b + 1) * N])
                        nc.gpsimd.tensor_copy(R[:, bass.ds(i * W + image * N, N)], r_s[:, b * N:(b + 1) * N]).then_inc(s_kept.sem, 1)

                    pool.sem_inc(s_kept.sem, s_kept.ahead)

                    def turn(i):
                        pad(i, 0)
                        if exists(i, -2):
                            rsqrt_image(i, -2)
                        pad(i, 1)
                        if exists(i, -2):
                            keep(i, -2)
                        if exists(i, -1):
                            rsqrt_image(i, -1)
                            keep(i, -1)

                    turn(0)
                    with pool.Fori(1, GROUPS) as i:
                        turn(i)
                    for image in (-2, -1):
                        rsqrt_image(GROUPS, image)
                        keep(GROUPS, image)

        attention("l1", False, Wp1, qk_in)

        layer2 = ctx.enter_context(ExitStack())

        def sb2(name, shape, dt=F32):
            return layer2.enter_context(nc.sbuf_tensor(name, shape, dt))

        PB = sb2("PB", [P, GROUPS * 2 * W])
        z_s = sb2("z_s", [P, 4, 2 * W])
        g_s = sb2("g_s", [P, 2, 2 * W])
        h_s = sb2("h_s", [P, 4, W])

        xs_in = [signal(f"l2_xs_in{b}", 16) for b in range(PAIR)]
        s_S, s_nm, s_E = signal("l2_scores", PAIR, True), signal("l2_negmax", PAIR), signal("l2_exp", PAIR)
        s_ET, s_ETs, s_O = signal("l2_ET", PAIR), signal("l2_ET_stored", PAIR), signal("l2_O", PAIR)
        s_r, s_rs, s_xn, s_xT, s_kept, s_done = (signal("l2_" + n, PAIR) for n in ("r", "rstd", "xn", "xnT", "r_kept", "done"))
        s_link = sem("l2_steps")
        with nc.Block() as block:
            @block.sync
            def _(sp):
                with sp.Fori(0, GROUPS) as i:
                    for b in range(PAIR):
                        sp.wait_ge(s_S.sem, s_S.after(i, b - 1))
                        sp.dma_start(xs[:, b * N:(b + 1) * N], XN_C[:, bass.ds(i * W + b * N, N)]).then_inc(xs_in[b].sem, 16)

            @block.tensor
            def _(pe):
                def steps(i, s, new):
                    n = s - 1
                    b = n % PAIR
                    if is_image(i, n) and (new or n < 0):
                        pe.wait_ge(s_E.sem, s_E.after(i, n + 1))
                        if is_image(i, n - 2):
                            pe.wait_ge(s_ETs.sem, s_ETs.after(i, n - 1))
                        for t in range(NT):
                            for kt in range(NT):
                                ins = nc.tensor.transpose(bank[2 + b][:, kt * N + t * P:kt * N + (t + 1) * P],
                                                          E_s[:, b, t, kt * P:(kt + 1) * P], ident[:, :])
                        ins.then_inc(s_ET.sem, 1)
                    if new:
                        pe.wait_ge(xs_in[s].sem, xs_in[s].after(i))
                        if is_image(i, s - 2):
                            pe.wait_ge(s_E.sem, s_E.after(i, s - 1))
                        for t in range(NT):
                            a = s * N + t * P
                            ins = nc.tensor.matmul(bank[s][:, t * N:(t + 1) * N], xs[:, a:a + P], xs[:, s * N:(s + 1) * N],
                                                   start=True, stop=True)
                        ins.then_inc(s_S.sem, 1)
                    if is_image(i, s - 3) and (new or s < 3):
                        n = s - 3
                        pe.wait_ge(s_xn.sem, s_xn.after(i, n + 1))
                        if is_image(i, n - 2):
                            pe.wait_ge(s_done.sem, s_done.after(i, n - 1))
                        for t in range(NT):
                            a = n % PAIR * N + t * P
                            ins = nc.tensor.transpose(bank[6 + n % PAIR][:, t * P:(t + 1) * P], xn_s[:, a:a + P], ident[:, :])
                        ins.then_inc(s_xT.sem, 1)
                    n = s - 1
                    if is_image(i, n) and (new or n < 0):
                        if is_image(i, n - 2):
                            pe.wait_ge(s_r.sem, s_r.after(i, n - 1))
                        pe.wait_ge(s_ETs.sem, s_ETs.after(i, n + 1))
                        for t in range(NT):
                            for kt in range(NT):
                                ins = nc.tensor.matmul(bank[4 + b][:, t * P:(t + 1) * P], ET_s[:, b, kt, t * P:(t + 1) * P],
                                                       XN_T[:, bass.ds(i * W + n * N + kt * P, P)],
                                                       start=(kt == 0), stop=(kt == NT - 1))
                        ins.then_inc(s_O.sem, 1)

                pe.sem_inc(s_S.sem, s_S.ahead)
                image_turns(pe, steps)

            @block.scalar
            def _(act):
                def steps(i, s, new):
                    if new:
                        act.wait_ge(s_nm.sem, s_nm.after(i, s + 1))
                        if is_image(i, s - 2):
                            act.wait_ge(s_ET.sem, s_ET.after(i, s - 1))
                        for t in range(NT):
                            ins = nc.scalar.activation(E_s[:, s, t, :], bank[s][:, t * N:(t + 1) * N], ACT.Exp,
                                                       bias=negmax[:, s, 0, t:t + 1], accum_out=rowsum[:, s, 0, t:t + 1])
                        ins.then_inc(s_E.sem, 1)
                    n = s - 3
                    if is_image(i, n) and (new or n < 0):
                        act.wait_ge(s_xT.sem, s_xT.after(i, n + 1))
                        hold(act)
                        nc.scalar.copy(XN_C[:, bass.ds(i * W + n * N, N)], bank[6 + n % PAIR][:, 0:N]).then_inc(s_done.sem, 1)
                    n = s - 2
                    if is_image(i, n) and (new or n < 0):
                        if is_image(i, n - 2):
                            act.wait_ge(s_xT.sem, s_xT.after(i, n - 1))
                        act.wait_ge(s_rs.sem, s_rs.after(i, n + 1))
                        for t in range(n % PAIR * NT, (n % PAIR + 1) * NT):
                            ins = nc.scalar.activation(xn_s[:, t * P:(t + 1) * P], r_s[:, t * P:(t + 1) * P], ACT.Identity,
                                                       bias=shift[:, t:t + 1], scale=rstd[:, t:t + 1])
                        ins.then_inc(s_xn.sem, 1)

                image_turns(act, steps)

            @block.vector
            def _(dve):
                link = Chain(dve, s_link)

                def steps(i, s, new):
                    n = s - 2
                    old = is_image(i, n) and (new or n < 0)
                    tiles = range(n % PAIR * NT, (n % PAIR + 1) * NT)
                    if old:
                        link.turn(i * PAIR + n, NORM)
                        dve.wait_ge(s_O.sem, s_O.after(i, n + 1))
                        if is_image(i, n - 2):
                            dve.wait_ge(s_kept.sem, s_kept.after(i, n - 1))
                            dve.wait_ge(s_xn.sem, s_xn.after(i, n - 1))
                        for t in range(NT):
                            a = n * N + t * P
                            b = n % PAIR
                            ins = nc.vector.scalar_tensor_tensor(r_s[:, b * N + t * P:b * N + (t + 1) * P],
                                                                 bank[4 + b][:, t * P:(t + 1) * P],
                                                                 rinv[:, b, 0, t:t + 1], R[:, bass.ds(i * W + a, P)],
                                                                 ALU.mult, ALU.add)
                        ins.then_inc(s_r.sem, 1)
                        dve.wait_ge(s_r.sem, s_r.after(i, n + 1))
                        norm_step(dve, link, 0, 1e-5, tiles, s_xn)
                    if is_image(i, s - 1) and (new or s < 1):
                        b = (s - 1) % PAIR
                        dve.wait_ge(s_ET.sem, s_ET.after(i, s))
                        if is_image(i, s - 3):
                            dve.wait_ge(s_O.sem, s_O.after(i, s - 2))
                        nc.vector.reciprocal(rinv[:, b, 0, :], rowsum[:, b, 0, :])
                        nc.vector.tensor_copy(ET_s[:, b, :, :].rearrange("p k n -> p (k n)"), bank[2 + b][:, :]).then_inc(s_ETs.sem, 1)
                    if new:
                        dve.wait_ge(s_S.sem, s_S.after(i, s + 1))
                        nc.vector.tensor_reduce(negmax[:, s, 0, :], bank[s][:, :].rearrange("p (t k) -> p t k", t=NT),
                                                AX.X, ALU.max, negate=True).then_inc(s_nm.sem, 1)
                    if old:
                        for k in range(1, 6):
                            norm_step(dve, link, k, 1e-5, tiles, s_xn)
                    if old:
                        for k in range(6, NORM):
                            norm_step(dve, link, k, 1e-5, tiles, s_xn)
                        a = tiles[0]
                        nc.vector.scalar_tensor_tensor(shift[:, a:a + NT], mv[:, a:a + NT, 0], -1.0, rstd[:, a:a + NT],
                                                       ALU.mult, ALU.mult).then_inc(s_rs.sem, 1)
                        link.ended(NORM)

                image_turns(dve, steps)

            @block.gpsimd
            def _(pool):
                with pool.Fori(0, GROUPS) as i:
                    for b in range(PAIR):
                        pool.wait_ge(s_r.sem, s_r.after(i, b + 1))
                        hold(pool)
                        nc.gpsimd.tensor_copy(R[:, bass.ds(i * W + b * N, N)], r_s[:, b * N:(b + 1) * N]).then_inc(s_kept.sem, 1)

        ALL = TOKENS // P
        s_lg, s_gap, s_e, s_p, s_pb, s_pbs = (sem("l2_" + n) for n in (
            "logits", "gap", "gap_exp", "gates", "gate_rows", "gate_rows_kept"))
        s_link = sem("l2_gate_steps")
        with nc.Block() as block:
            @block.tensor
            def _(pe):
                pe.wait_ge(w_l2, 20 * 16)
                for t in range(ALL):
                    ins = nc.tensor.matmul(bank[7][:, t * EXPERTS:(t + 1) * EXPERTS], XN_C[:, t * P:(t + 1) * P], Wg[:, :],
                                           start=True, stop=True)
                ins.then_inc(s_lg, 1)
                pe.wait_ge(s_p, 1)
                for g in range(GROUPS):
                    for w in range(2):
                        k = 2 * g + w
                        if k >= 4:
                            pe.wait_ge(s_pbs, k - 3)
                        for t in range(TILES):
                            ins = nc.tensor.transpose(bank[k % 4][:, t * P:(t + 1) * P],
                                                      gate[:, 3 + w, g * TILES + t:g * TILES + t + 1].broadcast_to([P, P]), ident[:, :])
                        ins.then_inc(s_pb, 1)

            @block.scalar
            def _(act):
                act.wait_ge(s_gap, 1)
                nc.scalar.activation(gate[:, 1, :], gate[:, 0, :], ACT.Exp).then_inc(s_e, 1)
                for k in range(2 * GROUPS):
                    act.wait_ge(s_pb, k + 1)
                    nc.scalar.copy(PB[:, k * W:(k + 1) * W], bank[k % 4][:, :]).then_inc(s_pbs, 1)

            @block.vector
            def _(dve):
                link = Chain(dve, s_link)
                dve.wait_ge(s_lg, 1)
                for t in range(ALL):
                    ins = nc.vector.max(top2[:, t, :], bank[7][:, t * EXPERTS:(t + 1) * EXPERTS])
                link(ins)
                nc.vector.tensor_tensor(gate[:, 0, :], top2[:, :, 1], top2[:, :, 0], ALU.subtract).then_inc(s_gap, 1)
                dve.wait_ge(s_e, 1)
                link(nc.vector.tensor_scalar(gate[:, 2, :], gate[:, 1, :], 1.0, None, ALU.add))
                link(nc.vector.reciprocal(gate[:, 3, :], gate[:, 2, :]))
                nc.vector.tensor_tensor(gate[:, 4, :], gate[:, 1, :], gate[:, 3, :], ALU.mult).then_inc(s_p, 1)

        s_U, s_z, s_g, s_h, s_D = (signal(n, FT) for n in ("ff_up", "ff_gated", "ff_gelu", "ff_hidden", "ff_down"))
        s_ys, s_yT, s_xn, s_xT = (signal("ff_y_stored", 1), signal("ff_yT", 1), signal("ff_xn", 1), signal("ff_xnT", 1))
        s_link = sem("ff_steps")
        D_LAG, RING, RING_G = 4, 4, 2
        Y_STORE, Y_TURN, ADD_Y, NORM_Y = D_LAG, 6, 8, 9
        XN_TURN, XN_KEEP = NORM_Y + NORM + 2, NORM_Y + NORM + 4

        def ff_turns(eng, steps):
            for s in range(FT):
                steps(0, s, True)
            with eng.Fori(1, GROUPS) as i:
                for s in range(FT):
                    steps(i, s, True)
            for s in range(XN_KEEP + 1):
                steps(GROUPS, s, False)

        with nc.Block() as block:
            @block.tensor
            def _(pe):
                def steps(i, s, new):
                    if new:
                        if exists(i, s - 4):
                            pe.wait_ge(s_z.sem, s_z.after(i, s - 3))
                        nc.tensor.matmul(bank[s % 4][:, :], W1[:, s // 4, s % 4 * P:(s % 4 + 1) * P],
                                         XN_C[:, bass.ds(i * W, W)], start=True, stop=True).then_inc(s_U.sem, 1)
                    f = s - D_LAG
                    if exists(i, f) and (new or f < 0):
                        if f == 0 and exists(i, f - 1):
                            pe.wait_ge(s_ys.sem, s_ys.after(i, 0))
                        pe.wait_ge(s_h.sem, s_h.after(i, f + 1))
                        nc.tensor.matmul(bank[7][:, :], W2[:, f % FT, :], h_s[:, f % RING, :],
                                         start=(f % FT == 0), stop=(f % FT == FT - 1)).then_inc(s_D.sem, 1)
                    if s == Y_TURN and exists(i, -1):
                        pe.wait_ge(s_ys.sem, s_ys.after(i, 0))
                        for t in range(TILES):
                            ins = nc.tensor.transpose(bank[6][:, t * P:(t + 1) * P], y_s[:, t * P:(t + 1) * P], ident[:, :])
                        ins.then_inc(s_yT.sem, 1)
                    if s == XN_TURN and exists(i, -1):
                        pe.wait_ge(s_xn.sem, s_xn.after(i, 0))
                        for t in range(TILES):
                            ins = nc.tensor.transpose(bank[5][:, t * P:(t + 1) * P], xn_s[:, t * P:(t + 1) * P], ident[:, :])
                        ins.then_inc(s_xT.sem, 1)

                pe.wait_ge(w_l2, 20 * 16)
                ff_turns(pe, steps)

            @block.vector
            def _(dve):
                link = Chain(dve, s_link)
                STEPS = 2 + NORM

                def steps(i, s, new):
                    if new:
                        dve.wait_ge(s_U.sem, s_U.after(i, s + 1))
                        if exists(i, s - RING):
                            dve.wait_ge(s_g.sem, s_g.after(i, s - RING + 1))
                        nc.vector.tensor_tensor(z_s[:, s % RING, :].rearrange("p (w n) -> p w n", w=2),
                                                bank[s % 4][:, None, :].broadcast_to([P, 2, W]),
                                                PB[:, bass.ds(i * 2 * W, 2 * W)].rearrange("p (w n) -> p w n", w=2),
                                                ALU.mult).then_inc(s_z.sem, 1)
                    if s == ADD_Y and exists(i, -1):
                        link.turn(i - 1, STEPS)
                        dve.wait_ge(s_yT.sem, s_yT.after(i, 0))
                        link(nc.vector.tensor_tensor(r_s[:, :], bank[6][:, :], R[:, bass.ds(i * W - W, W)], ALU.add))
                        hold(dve)
                        link(nc.vector.tensor_copy(R[:, bass.ds(i * W - W, W)], r_s[:, :]))
                    if NORM_Y <= s <= NORM_Y + NORM and exists(i, -1):
                        norm_step(dve, link, s - NORM_Y, 1e-5, range(TILES), s_xn)

                ff_turns(dve, steps)

            @block.scalar
            def _(act):
                def steps(i, s, new):
                    if s == Y_STORE and exists(i, -1):
                        act.wait_ge(s_D.sem, s_D.after(i, 0))
                        nc.scalar.activation(y_s[:, :], bank[7][:, :], ACT.Identity, bias=b2two[:, :]).then_inc(s_ys.sem, 1)
                    if new:
                        act.wait_ge(s_z.sem, s_z.after(i, s + 1))
                        if exists(i, s - RING_G):
                            act.wait_ge(s_h.sem, s_h.after(i, s - RING_G + 1))
                        nc.scalar.activation(g_s[:, s % RING_G, :], z_s[:, s % RING, :], ACT.Gelu,
                                             bias=b1[:, s:s + 1]).then_inc(s_g.sem, 1)
                    if s == XN_KEEP and exists(i, -1):
                        act.wait_ge(s_xT.sem, s_xT.after(i, 0))
                        hold(act)
                        nc.scalar.copy(XN_C[:, bass.ds(i * W - W, W)], bank[5][:, :])

                ff_turns(act, steps)

            @block.gpsimd
            def _(pool):
                def steps(i, s, new):
                    if new:
                        pool.wait_ge(s_g.sem, s_g.after(i, s + 1))
                        if exists(i, s - RING):
                            pool.wait_ge(s_D.sem, s_D.after(i, s - RING + 1))
                        nc.gpsimd.tensor_tensor(h_s[:, s % RING, :], g_s[:, s % RING_G, 0:W], g_s[:, s % RING_G, W:2 * W],
                                                ALU.add).then_inc(s_h.sem, 1)

                ff_turns(pool, steps)
        layer2.close()

        prep3 = ctx.enter_context(ExitStack())

        def sb3(name, shape, dt=F32):
            return prep3.enter_context(nc.sbuf_tensor(name, shape, dt))

        xs3 = sb3("xs3", [P, 2, W])
        qk3 = XN_T[:, :].rearrange("p (b t c) -> p b t c", b=2, t=TILES)
        qb = R_C[:, :].rearrange("p (b t c) -> p b t c", b=2, t=TILES)
        qa = sb3("qa", [P, 2, TILES, 2 * P])
        qp = sb3("qp", [P, 2, TILES, 2, P])
        rest3 = sb3("rest3", [P, 2, 2, W])
        parts3 = sb3("parts3", [P, 2, PARTS, 2, W], BF16)

        xs_in = [signal(f"l3_xs_in{b}", 16) for b in range(2)]
        s_out = [signal(f"l3_parts_in_dram{b}", 6 * 16, True) for b in range(2)]
        qk_in3 = [signal(f"l3_stack_in{b}", STACK_DMAS * 16) for b in range(PAIR)]
        s_proj, s_qks, s_st = signal("l3_qkv", 2 * TILES, True), signal("l3_qk_stored", 2), signal("l3_qkv_stored", 2 * TILES, True)
        s_sq, s_rms, s_rot, s_qp, s_qT = (signal("l3_squares", 2), signal("l3_rms", 2), signal("l3_rotated", 2),
                                          signal("l3_qk_ready", 2, True), signal("l3_qkT", 2, True))
        s_c1, s_r1, s_c2, s_c3 = (signal("l3_part1", 2), signal("l3_rest1", 2, True), signal("l3_part2", 2),
                                  signal("l3_part3", 2, True))
        s_link = sem("l3_prep_steps")
        with nc.Block() as block:
            @block.sync
            def _(sp):
                for b in range(2):
                    sp.sem_inc(s_out[b].sem, s_out[b].ahead)
                for i in range(GROUPS // 2):
                    for b in range(2):
                        sp.wait_ge(s_proj.sem, s_proj.after(i, (b - 1) * TILES))
                        sp.dma_start(xs3[:, b, :], XN_C[:, bass.ds((i * 2 + b) * W, W)]).then_inc(xs_in[b].sem, 16)
                    if i == 1:
                        sp.wait_ge(s_out[0].sem, s_out[0].after(0))
                        read_stack(sp, bass.ds(0, 1), 0, qk_in3[0])
                    for b in range(2):
                        sp.wait_ge(s_c1.sem, s_c1.after(i, b + 1))
                        write_parts(sp, parts3, i * 2 + b, b, 0, s_out[b])
                        sp.wait_ge(s_c2.sem, s_c2.after(i, b + 1))
                        write_parts(sp, parts3, i * 2 + b, b, 1, s_out[b])
                        sp.wait_ge(s_c3.sem, s_c3.after(i, b + 1))
                        write_parts(sp, parts3, i * 2 + b, b, 2, s_out[b])
                for b in range(2):
                    sp.wait_ge(s_out[b].sem, s_out[b].after(GROUPS // 2 - 1))

            @block.tensor
            def _(pe):
                pe.sem_inc(s_proj.sem, s_proj.ahead)
                pe.sem_inc(s_qT.sem, s_qT.ahead)
                with pe.Fori(0, GROUPS // 2) as i:
                    for b in range(2):
                        pe.wait_ge(xs_in[b].sem, xs_in[b].after(i))
                        for t in range(TILES):
                            pe.wait_ge(s_st.sem, s_st.after(i, (b - 1) * TILES + t + 1))
                            nc.tensor.matmul(bank[t][:, 0:3 * P], xs3[:, b, t * P:(t + 1) * P], Wqkv3[:, :],
                                             start=True, stop=True).then_inc(s_proj.sem, 1)
                    for b in range(2):
                        pe.wait_ge(s_r1.sem, s_r1.after(i, b - 1))
                        pe.wait_ge(s_qp.sem, s_qp.after(i, b + 1))
                        for kind in range(2):
                            for t in range(TILES):
                                ins = nc.tensor.transpose(bank[4 + 2 * b + kind][:, t * P:(t + 1) * P], qp[:, b, t, kind, :], ident[:, :])
                        ins.then_inc(s_qT.sem, 1)

            @block.scalar
            def _(act):
                act.sem_inc(s_st.sem, s_st.ahead)
                with act.Fori(0, GROUPS // 2) as i:
                    for b in range(2):
                        act.wait_ge(s_qp.sem, s_qp.after(i, b - 1))
                        for t in range(TILES):
                            act.wait_ge(s_proj.sem, s_proj.after(i, b * TILES + t + 1))
                            hold(act)
                            ins = nc.scalar.copy(qk3[:, b, t, :], bank[t][:, 0:2 * P])
                            if t == TILES - 1:
                                ins.then_inc(s_qks.sem, 1)
                            nc.scalar.copy(vall[:, bass.ds((i * 2 + b) * W + t * P, P)], bank[t][:, 2 * P:3 * P]).then_inc(s_st.sem, 1)
                        act.wait_ge(s_qks.sem, s_qks.after(i, b + 1))
                        nc.scalar.activation(qa[:, b, :, :], qk3[:, b, :, :], ACT.Square).then_inc(s_sq.sem, 1)
                    for b in range(2):
                        act.wait_ge(s_out[b].sem, s_out[b].before(i))
                        act.wait_ge(s_qT.sem, s_qT.after(i, b + 1))
                        for kind in range(2):
                            ins = nc.scalar.copy(parts3[:, b, 0, kind, :], bank[4 + 2 * b + kind][:, :])
                        ins.then_inc(s_c1.sem, 1)
                    for b in range(2):
                        act.wait_ge(s_r1.sem, s_r1.after(i, b + 1))
                        nc.scalar.copy(parts3[:, b, 1, :, :], rest3[:, b, :, :]).then_inc(s_c2.sem, 1)

            @block.vector
            def _(dve):
                link = Chain(dve, s_link)
                STEPS = 5 + RSQRT
                heads = TILES * 2 * HEADS
                for ahead in (s_qp, s_r1, s_c3):
                    dve.sem_inc(ahead.sem, ahead.ahead)
                with dve.Fori(0, GROUPS // 2) as i:
                    link.turn(i, STEPS)
                    for b in range(2):
                        dve.wait_ge(s_sq.sem, s_sq.after(i, b + 1))
                        link(nc.vector.tensor_reduce(var[:, b * heads:(b + 1) * heads],
                                                     qa[:, b, :, :].rearrange("p t (g d) -> p (t g) d", d=HD), AX.X, ALU.add))
                    link(nc.vector.tensor_scalar(var[:, :], var[:, :], 1.0 / HD, 1e-6, ALU.mult, ALU.add))
                    rsqrt(nc.vector, link, 0, 2 * heads)
                    for b in range(2):
                        flat = qk3[:, b, :, :].rearrange("p t (g d) -> p (t g) d", d=HD)
                        nc.vector.tensor_tensor(flat, flat, rstd[:, b * heads:(b + 1) * heads, None].broadcast_to([P, heads, HD]),
                                                ALU.mult).then_inc(s_rms.sem, 1)
                        dve.wait_ge(s_rms.sem, s_rms.after(i, b + 1))
                        for t in range(TILES):
                            ins = nc.vector.tensor_tensor(qa[:, b, t, :].rearrange("p (c h d) -> p c h d", c=2, d=HD),
                                                          qk3[:, b, t, :].rearrange("p (c h d) -> p c h d", c=2, d=HD),
                                                          cosw[:, t % NT, :, None, :].broadcast_to([P, 2, HEADS, HD]), ALU.mult)
                        link(ins)
                    for b in range(2):
                        dve.wait_ge(s_rot.sem, s_rot.after(i, b + 1))
                        dve.wait_ge(s_qT.sem, s_qT.after(i, b - 1))
                        nc.vector.tensor_tensor(qp[:, b, :, :, :].rearrange("p t c (d h) -> p (t c) h d", h=HEADS),
                                                qa[:, b, :, :].rearrange("p t (c h d) -> p (t c) h d", c=2, d=HD),
                                                qb[:, b, :, :].rearrange("p t (c h d) -> p (t c) h d", c=2, d=HD), ALU.add).then_inc(s_qp.sem, 1)
                    link.ended(STEPS)
                    for b in range(2):
                        dve.wait_ge(s_c3.sem, s_c3.after(i, b - 1))
                        dve.wait_ge(s_c1.sem, s_c1.after(i, b + 1))
                        for kind in range(2):
                            ins = nc.vector.tensor_tensor(rest3[:, b, kind, :], bank[4 + 2 * b + kind][:, :], parts3[:, b, 0, kind, :], ALU.subtract)
                        ins.then_inc(s_r1.sem, 1)
                    for b in range(2):
                        dve.wait_ge(s_c2.sem, s_c2.after(i, b + 1))
                        nc.vector.tensor_tensor(parts3[:, b, 2, :, :], rest3[:, b, :, :], parts3[:, b, 1, :, :], ALU.subtract).then_inc(s_c3.sem, 1)

            @block.gpsimd
            def _(pool):
                H = HD // 2
                with pool.Fori(0, GROUPS // 2) as i:
                    for b in range(2):
                        pool.wait_ge(s_rms.sem, s_rms.after(i, b + 1))
                        for t in range(TILES):
                            x = qk3[:, b, t, :].rearrange("p (c h d) -> p c h d", c=2, d=HD)
                            y = qb[:, b, t, :].rearrange("p (c h d) -> p c h d", c=2, d=HD)
                            s = sinw[:, t % NT, :, None, :].broadcast_to([P, 2, HEADS, HD])
                            nc.gpsimd.tensor_tensor(y[:, :, :, 0:H], x[:, :, :, H:HD], s[:, :, :, 0:H], ALU.mult)
                            ins = nc.gpsimd.tensor_tensor(y[:, :, :, H:HD], x[:, :, :, 0:H], s[:, :, :, H:HD], ALU.mult)
                        ins.then_inc(s_rot.sem, 1)
        prep3.close()

        attention("l3", True, Wo3, qk_in3)

        pr = sb("pr", [P, 4, ALL, EXPERTS])
        best = sb("best", [P, 3, ALL])
        top2i = sb("top2i", [P, ALL, 8], U32)
        top2f = sb("top2f", [P, ALL, 8])
        w_parts = sb("w_parts", [P, ALL, PARTS, EXPERTS], BF16)
        wT = sb("wT", [PARTS * EXPERTS, TOKENS], BF16)
        s_lg, s_sh, s_pe, s_wp, s_wT, s_rT, s_rc = (sem("l3_" + n) for n in (
            "logits", "shifted", "router_exp", "weight_parts", "weightsT", "residualT", "residual_c"))
        s_link = sem("router_steps")
        with nc.Block() as block:
            @block.tensor
            def _(pe):
                for t in range(ALL):
                    ins = nc.tensor.matmul(bank[4][:, t * EXPERTS:(t + 1) * EXPERTS], XN_C[:, t * P:(t + 1) * P],
                                           router[:, :], start=True, stop=True)
                ins.then_inc(s_lg, 1)
                for t in range(ALL):
                    nc.tensor.transpose(bank[t // TILES][:, t % TILES * P:(t % TILES + 1) * P], R[:, t * P:(t + 1) * P],
                                        ident[:, :]).then_inc(s_rT, 1)
                pe.wait_ge(s_rc, GROUPS)
                pe.wait_ge(s_wp, 1)
                for t in range(ALL):
                    nc.tensor.matmul(bank[t // TILES][0:PARTS * EXPERTS, t % TILES * P:(t % TILES + 1) * P],
                                     w_parts[:, t, :, :], identb[:, :], start=True, stop=True).then_inc(s_wT, 1)

            @block.scalar
            def _(act):
                act.wait_ge(s_sh, 1)
                nc.scalar.activation(pr[:, 1, :, :], pr[:, 0, :, :], ACT.Exp).then_inc(s_pe, 1)
                for g in range(GROUPS):
                    act.wait_ge(s_rT, (g + 1) * TILES)
                    nc.scalar.copy(R_C[:, g * W:(g + 1) * W], bank[g][:, :]).then_inc(s_rc, 1)
                for g in range(GROUPS):
                    act.wait_ge(s_wT, (g + 1) * TILES)
                    nc.scalar.copy(wT[:, g * W:(g + 1) * W], bank[g][0:PARTS * EXPERTS, :])

            @block.vector
            def _(dve):
                link = Chain(dve, s_link)
                wide = [P, ALL, EXPERTS]
                dve.wait_ge(s_lg, 1)
                logits = bank[4][:, 0:ALL * EXPERTS].rearrange("p (t e) -> p t e", e=EXPERTS)
                link(nc.vector.tensor_reduce(best[:, 0, :], logits, AX.X, ALU.max))
                nc.vector.tensor_tensor(pr[:, 0, :, :], logits, best[:, 0, :, None].broadcast_to(wide), ALU.subtract).then_inc(s_sh, 1)
                dve.wait_ge(s_pe, 1)
                link(nc.vector.tensor_reduce(best[:, 1, :], pr[:, 1, :, :], AX.X, ALU.add))
                link(nc.vector.reciprocal(best[:, 2, :], best[:, 1, :]))
                link(nc.vector.tensor_tensor(pr[:, 2, :, :], pr[:, 1, :, :], best[:, 2, :, None].broadcast_to(wide), ALU.mult))
                for t in range(ALL):
                    ins = nc.vector.max(top2[:, t, :], pr[:, 2, t, :])
                link(ins)
                for t in range(ALL):
                    ins = nc.vector.max_index(top2i[:, t, :], top2[:, t, :], pr[:, 2, t, :])
                link(ins)
                link(nc.vector.tensor_copy(top2f[:, :, :], top2i[:, :, :]))
                for n in range(2):
                    link(nc.vector.tensor_tensor(pr[:, 3 * n, :, :], iota8[:, None, :].broadcast_to(wide),
                                                 top2f[:, :, n:n + 1].broadcast_to(wide), ALU.is_equal))
                link(nc.vector.tensor_tensor(pr[:, 0, :, :], pr[:, 0, :, :], pr[:, 3, :, :], ALU.add))
                link(nc.vector.tensor_tensor(pr[:, 3, :, :], pr[:, 0, :, :], pr[:, 2, :, :], ALU.mult))
                for part in range(PARTS - 1):
                    link(nc.vector.tensor_copy(w_parts[:, :, part, :], pr[:, 3, :, :]))
                    link(nc.vector.tensor_tensor(pr[:, 3, :, :], pr[:, 3, :, :], w_parts[:, :, part, :], ALU.subtract))
                nc.vector.tensor_copy(w_parts[:, :, PARTS - 1, :], pr[:, 3, :, :]).then_inc(s_wp, 1)

        a_s = sb("a_s", [P, 2, W])
        c_s = sb("c_s", [P, 2, W])
        BLOCKS = 5
        s_G, s_Up, s_si = (signal(n, BLOCKS) for n in ("ex_gate", "ex_up", "ex_silu"))
        s_m, s_c, s_Dn = (signal(n, BLOCKS, True) for n in ("ex_product", "ex_weighted", "ex_down"))

        def two_before(n):
            return n - 1 if n >= 2 else -n

        s_rw = signal("ex_weights", BLOCKS - 1)
        s_out, s_sum = signal("out_stored", 16, True), signal("ex_sum", 1, True)
        with nc.Block() as block:
            @block.tensor
            def _(pe):
                pe.sem_inc(s_Dn.sem, s_Dn.ahead)
                with pe.Fori(0, GROUPS) as i:
                    for s in range(BLOCKS + 1):
                        if s < BLOCKS:
                            m = P if s < 4 else EH
                            pe.wait_ge(s_m.sem, s_m.after(i, two_before(s)))
                            if s == 4:
                                hold(pe)
                            for to, w, done in ((bank[s % 2], Wgate[:, 2 * s:2 * s + 2, :] if s < 4 else Sgate[:, :], s_G),
                                                (bank[2 + s % 2], Wup[:, 2 * s:2 * s + 2, :] if s < 4 else Sup[:, :], s_Up)):
                                nc.tensor.matmul(to[0:m, :], w, XN_C[:, bass.ds(i * W, W)], start=True, stop=True).then_inc(done.sem, 1)
                            if s < 4:
                                pe.wait_ge(s_c.sem, s_c.after(i, s - 1 if s >= 2 else s - 2))
                                hold(pe)
                                nc.tensor.matmul(bank[4 + s % 2][:, :], expert_rows[:, s * P:(s + 1) * P],
                                                 wT[:, bass.ds(i * W, W)], start=True, stop=True).then_inc(s_rw.sem, 1)
                        n = s - 1
                        if n >= 0:
                            if n == 0:
                                pe.wait_ge(s_sum.sem, s_sum.before(i))
                            pe.wait_ge(s_c.sem, s_c.after(i, n + 1))
                            m = P if n < 4 else EH
                            nc.tensor.matmul(bank[6][:, :], Wdown[:, n, :] if n < 4 else Sdown[:, :], c_s[0:m, n % 2, :],
                                             start=(n == 0), stop=(n == BLOCKS - 1)).then_inc(s_Dn.sem, 1)

            @block.scalar
            def _(act):
                with act.Fori(0, GROUPS) as i:
                    for n in range(BLOCKS):
                        m = P if n < 4 else EH
                        act.wait_ge(s_G.sem, s_G.after(i, n + 1))
                        act.wait_ge(s_m.sem, s_m.after(i, two_before(n)))
                        nc.scalar.activation(a_s[0:m, n % 2, :], bank[n % 2][0:m, :], ACT.Silu).then_inc(s_si.sem, 1)

            @block.vector
            def _(dve):
                for ahead in (s_sum, s_m, s_c):
                    dve.sem_inc(ahead.sem, ahead.ahead)
                with dve.Fori(0, GROUPS) as i:
                    for n in range(BLOCKS):
                        m = P if n < 4 else EH
                        dve.wait_ge(s_Up.sem, s_Up.after(i, n + 1))
                        dve.wait_ge(s_si.sem, s_si.after(i, n + 1))
                        dve.wait_ge(s_Dn.sem, s_Dn.after(i, two_before(n)))
                        nc.vector.tensor_tensor(c_s[0:m, n % 2, :], a_s[0:m, n % 2, :], bank[2 + n % 2][0:m, :],
                                                ALU.mult).then_inc(s_m.sem, 1)
                        dve.wait_ge(s_m.sem, s_m.after(i, n + 1))
                        if n < 4:
                            dve.wait_ge(s_rw.sem, s_rw.after(i, n + 1))
                            nc.vector.tensor_tensor(c_s[:, n % 2, :], c_s[:, n % 2, :], bank[4 + n % 2][:, :],
                                                    ALU.mult).then_inc(s_c.sem, 1)
                        else:
                            dve.sem_inc(s_c.sem, 1)
                    dve.wait_ge(s_Dn.sem, s_Dn.after(i))
                    dve.wait_ge(s_out.sem, s_out.before(i))
                    nc.vector.tensor_tensor(y_s[:, :], bank[6][:, :], R_C[:, bass.ds(i * W, W)], ALU.add).then_inc(s_sum.sem, 1)

            @block.sync
            def _(sp):
                sp.sem_inc(s_out.sem, s_out.ahead)
                with sp.Fori(0, GROUPS) as i:
                    sp.wait_ge(s_sum.sem, s_sum.after(i))
                    sp.dma_start(OUT[:, bass.ds(i * PAIR, PAIR), :], y_s[:, :].rearrange("p (b n) -> p b n", n=N)).then_inc(s_out.sem, 16)
                sp.wait_ge(s_out.sem, 16 * (GROUPS + 1))


_INS = ["x", "L0_conv_Wb", "L0_conv_Wc", "L0_conv_Wd", "L0_conv_gamma", "L1_conv_W_qkv", "L1_conv_b_qkv",
        "L1_conv_W_proj", "L1_conv_b_proj", "L2_ffn_Wg", "L2_ffn_W1", "L2_ffn_b1", "L2_ffn_W2", "L2_ffn_b2",
        "L3_attn_rope_cos", "L3_attn_rope_sin", "L3_attn_W_q", "L3_attn_W_k", "L3_attn_W_v", "L3_attn_W_o",
        "L3_attn_q_norm_w", "L3_attn_k_norm_w", "L3_ffn_router", "L3_ffn_shared_gate", "L3_ffn_shared_up",
        "L3_ffn_shared_down", "L3_ffn_W_gate", "L3_ffn_W_up", "L3_ffn_W_down"]


def kernel(**inputs):
    import numpy as _np
    import concourse.bacc as _bacc
    from concourse import mybir as _mybir
    from concourse.bass_utils import run_bass_kernel_spmd as _run

    nc = _bacc.Bacc("TRN2", target_bir_lowering=False, num_devices=1)
    arrays, args = {}, {}
    for name in _INS:
        a = _np.ascontiguousarray(inputs[name])
        arrays[f"in_{name}_dram"] = a
        args[name] = nc.dram_tensor(f"in_{name}_dram", a.shape, _mybir.dt.from_np(a.dtype), kind="ExternalInput").ap()
    out = nc.dram_tensor("out_0_dram", (8, 128, 16, 16), _mybir.dt.float32, kind="ExternalOutput").ap()
    bass_conv_attn_hybrid_kernel(nc, args, out)
    r = _run(nc, [arrays], core_ids=[0])
    return r.results[0]["out_0_dram"]
```
